# Optimizing a Trainium2 kernel written in Bass

```python
import numpy as np
import jax
import jax.numpy as jnp

def _softmax(x, axis=-1):
    return jax.nn.softmax(x, axis=axis)

def _gelu(x):
    return jax.nn.gelu(x, approximate=True)

def _silu(x):
    return jax.nn.silu(x)

def _sigmoid(x):
    return jax.nn.sigmoid(x)

def _layernorm(x, axis=-1, eps=1e-05):
    m = jnp.mean(x, axis=axis, keepdims=True)
    v = jnp.var(x, axis=axis, keepdims=True)
    return (x - m) / jnp.sqrt(v + eps)

def _scatter_add(tgt, idx, src, axis=0):
    return tgt.at[idx].add(src)

def _segment_sum(src, seg, n):
    return jax.ops.segment_sum(src, seg, n)
kernel_name = 'mk_decoder_postln_d2_seqx_r8_daa6f8'

def setup_inputs(seed: int=0):
    np.random.seed(seed)
    _w = jnp.asarray

    def _rec_inputs():
        import jax
        import jax.numpy as jnp
        _rk = jax.random.key(seed)
        x = -0.0002928 + 1 * jax.random.normal(jax.random.fold_in(_rk, 1), (64, 64, 128), jnp.float32)
        _lenS = 64 - jax.random.randint(jax.random.fold_in(_rk, 7), (64,), 0, max(1, 64 // 4) + 1, jnp.int32)
        _lenS2 = 64 - jax.random.randint(jax.random.fold_in(_rk, 8), (64,), 0, max(1, 64 // 4) + 1, jnp.int32)
        _ctx_1024P = jax.random.normal(jax.random.fold_in(_rk, 11), (64, 16, 128), jnp.float32)
        _ctx_1024c = jax.random.dirichlet(jax.random.fold_in(_rk, 511), 0.3 * jnp.ones((16,), jnp.float32), (64, 64))
        _ctx_1024t = jnp.einsum('bsk,bkd->bsd', _ctx_1024c, _ctx_1024P)
        _ctx_1024t = _ctx_1024t * jax.lax.rsqrt(jnp.mean(jnp.square(_ctx_1024t)) + 1e-12) * 0.953939
        ctx_1024 = 2.81802e-05 + 1.00001 * (_ctx_1024t + 0.3 * jax.random.normal(jax.random.fold_in(_rk, 611), (64, 64, 128), jnp.float32))
        _validS = jnp.arange(64)[None, :] < _lenS[:, None]
        _validS2 = jnp.arange(64)[None, :] < _lenS2[:, None]
        _causal = jnp.tril(jnp.ones((64, 64), dtype=bool))
        mask_BxS2_bk0 = jnp.logical_not(jnp.broadcast_to(_validS2[:, :], (64, 64)))
        return (x, ctx_1024, mask_BxS2_bk0)
    x, ctx_1024, mask_BxS2_bk0 = _rec_inputs()

    def _L0_attn_setup():
        import jax, jax.numpy as jnp
        import numpy as np
        import math
        D_MODEL = 128
        N_HEADS = 16
        D_K = D_MODEL // N_HEADS
        MAX_REL = 128

        def _rel_bias_matrix(rel_bias, seq_len):
            pos = jnp.arange(seq_len)
            rel = pos[:, None] - pos[None, :]
            idx = jnp.clip(rel, -MAX_REL, MAX_REL) + MAX_REL
            return rel_bias[:, idx]
        key = jax.random.key(seed)
        ks = jax.random.split(key, 10)
        B, S = (2, 256)
        std = 1.0 / math.sqrt(D_MODEL)
        inp = {'x': jax.random.normal(ks[0], (B, S, D_MODEL), dtype=jnp.float32), 'Wq': jax.random.normal(ks[1], (D_MODEL, D_MODEL), dtype=jnp.float32) * std, 'bq': jnp.zeros((D_MODEL,), dtype=jnp.float32), 'Wk': jax.random.normal(ks[2], (D_MODEL, D_MODEL), dtype=jnp.float32) * std, 'bk': jnp.zeros((D_MODEL,), dtype=jnp.float32), 'Wv': jax.random.normal(ks[3], (D_MODEL, D_MODEL), dtype=jnp.float32) * std, 'bv': jnp.zeros((D_MODEL,), dtype=jnp.float32), 'Wo': jax.random.normal(ks[4], (D_MODEL, D_MODEL), dtype=jnp.float32) * std, 'bo': jnp.zeros((D_MODEL,), dtype=jnp.float32), 'rel_bias': jax.random.normal(ks[5], (N_HEADS, 2 * MAX_REL + 1), dtype=jnp.float32) * 0.02}
        return inp
    _L0_attn_all = _L0_attn_setup()
    _L0_attn_in = {k: v for k, v in _L0_attn_all.items() if k in ('Wq', 'bq', 'Wk', 'bk', 'Wv', 'bv', 'Wo', 'bo', 'rel_bias')}
    del _L0_attn_all

    def _L0_xattn_setup():
        import jax, jax.numpy as jnp
        import numpy as np
        DIM = 128
        NUM_HEADS = 16
        HEAD_DIM = DIM // NUM_HEADS
        ROPE_BASE = 10000.0
        SCALE = 1.0 / np.sqrt(HEAD_DIM)

        def _rotate_half(x):
            x1, x2 = jnp.split(x, 2, axis=-1)
            return jnp.concatenate([-x2, x1], axis=-1)

        def _rope(x, seq_len):
            inv_freq = 1.0 / ROPE_BASE ** (jnp.arange(0, HEAD_DIM, 2, dtype=jnp.float32) / HEAD_DIM)
            t = jnp.arange(seq_len, dtype=jnp.float32)
            freqs = jnp.outer(t, inv_freq)
            emb = jnp.concatenate([freqs, freqs], -1)
            cos = jnp.cos(emb)[None, None]
            sin = jnp.sin(emb)[None, None]
            return x * cos + _rotate_half(x) * sin
        key = jax.random.key(seed)
        ks = jax.random.split(key, 6)
        B, T_q, T_k = (4, 128, 512)
        s = 1.0 / np.sqrt(DIM)
        return {'x_query': jax.random.normal(ks[0], (B, T_q, DIM), jnp.float32), 'x_kv': jax.random.normal(ks[1], (B, T_k, DIM), jnp.float32), 'Wq': jax.random.normal(ks[2], (DIM, DIM), jnp.float32) * s, 'Wk': jax.random.normal(ks[3], (DIM, DIM), jnp.float32) * s, 'Wv': jax.random.normal(ks[4], (DIM, DIM), jnp.float32) * s, 'Wo': jax.random.normal(ks[5], (DIM, DIM), jnp.float32) * s}
    _L0_xattn_all = _L0_xattn_setup()
    _L0_xattn_in = {k: v for k, v in _L0_xattn_all.items() if k in ('Wq', 'Wk', 'Wv', 'Wo')}
    del _L0_xattn_all

    def _L0_ffn_setup():
        import jax, jax.numpy as jnp
        import numpy as np
        D_MODEL = 128
        EXPERT_DIM = 64
        N_EXPERTS = 8
        TOP_K = 2

        def _sq_relu(h):
            return jnp.square(jax.nn.relu(h))
        key = jax.random.key(seed)
        ks = jax.random.split(key, 6)
        s = 0.02
        x = jax.random.normal(ks[0], (2, 256, D_MODEL), dtype=jnp.float32)
        Ws1 = jax.random.normal(ks[1], (D_MODEL, EXPERT_DIM), dtype=jnp.float32) * s
        Ws2 = jax.random.normal(ks[2], (EXPERT_DIM, D_MODEL), dtype=jnp.float32) * s
        W1 = jax.random.normal(ks[3], (N_EXPERTS, D_MODEL, EXPERT_DIM), dtype=jnp.float32) * s
        W2 = jax.random.normal(ks[4], (N_EXPERTS, EXPERT_DIM, D_MODEL), dtype=jnp.float32) * s
        Wr = jax.random.normal(ks[5], (D_MODEL, N_EXPERTS), dtype=jnp.float32) * s
        return {'x': x, 'Ws1': Ws1, 'Ws2': Ws2, 'W1': W1, 'W2': W2, 'Wr': Wr}
    _L0_ffn_all = _L0_ffn_setup()
    _L0_ffn_in = {k: v for k, v in _L0_ffn_all.items() if k in ('Ws1', 'Ws2', 'W1', 'W2', 'Wr')}
    del _L0_ffn_all

    def _L1_attn_setup():
        import jax, jax.numpy as jnp
        import numpy as np
        import math
        D_MODEL = 128
        N_HEAD = 16
        D_HEAD = D_MODEL // N_HEAD
        D_KMAP = 128
        B, L = (4, 512)

        def _fourier_kernel(x, proj_mat):
            p = jnp.einsum('blhd,dm->blhm', x, proj_mat) / math.sqrt(D_HEAD)
            return jnp.concatenate([jnp.cos(p), jnp.sin(p)], axis=-1) / math.sqrt(D_KMAP)
        key = jax.random.key(seed)
        ks = jax.random.split(key, 10)
        s = 1.0 / math.sqrt(D_MODEL)
        inp = {'x': jax.random.normal(ks[0], (B, L, D_MODEL), dtype=jnp.float32), 'proj_mat': jax.random.normal(ks[1], (D_HEAD, D_KMAP), dtype=jnp.float32), 'Wq': jax.random.uniform(ks[2], (D_MODEL, D_MODEL), minval=-s, maxval=s), 'bq': jax.random.uniform(ks[3], (D_MODEL,), minval=-s, maxval=s), 'Wk': jax.random.uniform(ks[4], (D_MODEL, D_MODEL), minval=-s, maxval=s), 'bk': jax.random.uniform(ks[5], (D_MODEL,), minval=-s, maxval=s), 'Wv': jax.random.uniform(ks[6], (D_MODEL, D_MODEL), minval=-s, maxval=s), 'bv': jax.random.uniform(ks[7], (D_MODEL,), minval=-s, maxval=s), 'Wo': jax.random.uniform(ks[8], (D_MODEL, D_MODEL), minval=-s, maxval=s), 'bo': jax.random.uniform(ks[9], (D_MODEL,), minval=-s, maxval=s)}
        return inp
    _L1_attn_all = _L1_attn_setup()
    _L1_attn_in = {k: v for k, v in _L1_attn_all.items() if k in ('proj_mat', 'Wq', 'bq', 'Wk', 'bk', 'Wv', 'bv', 'Wo', 'bo')}
    del _L1_attn_all

    def _L1_xattn_setup():
        import jax, jax.numpy as jnp
        import numpy as np
        EPS = 1e-05

        def layer_norm(x, g, b):
            mu = jnp.mean(x, axis=-1, keepdims=True)
            var = jnp.mean((x - mu) ** 2, axis=-1, keepdims=True)
            return (x - mu) * jax.lax.rsqrt(var + EPS) * g + b
        key = jax.random.key(seed)
        ks = jax.random.split(key, 8)
        b, n, l, D = (8, 512, 64, 128)
        heads, dim_head = (16, 64)
        inner = heads * dim_head
        x = jax.random.normal(ks[0], (b, n, D), dtype=jnp.float32)
        latents = jax.random.normal(ks[1], (b, l, D), dtype=jnp.float32)
        mask = jax.random.randint(ks[2], (b, n), 0, 2) > 0
        Wq = jax.random.normal(ks[3], (D, inner), dtype=jnp.float32) * D ** (-0.5)
        Wkv = jax.random.normal(ks[4], (D, 2 * inner), dtype=jnp.float32) * D ** (-0.5)
        Wout = jax.random.normal(ks[5], (inner, D), dtype=jnp.float32) * inner ** (-0.5)
        g1 = jnp.ones((D,), jnp.float32)
        b1 = jnp.zeros((D,), jnp.float32)
        g2 = jnp.ones((D,), jnp.float32)
        b2 = jnp.zeros((D,), jnp.float32)
        return {'x': x, 'latents': latents, 'mask': mask, 'g1': g1, 'b1': b1, 'g2': g2, 'b2': b2, 'Wq': Wq, 'Wkv': Wkv, 'Wout': Wout}
    _L1_xattn_all = _L1_xattn_setup()
    _L1_xattn_in = {k: v for k, v in _L1_xattn_all.items() if k in ('g1', 'b1', 'g2', 'b2', 'Wq', 'Wkv', 'Wout')}
    del _L1_xattn_all

    def _L1_ffn_setup():
        import jax, jax.numpy as jnp
        import numpy as np
        EPS_NORM = 1e-08
        EPS_Q = 1e-05

        def rmsnorm(x, w):
            v = jnp.mean(jnp.square(x.astype(jnp.float32)), axis=-1, keepdims=True)
            x_hat = x * jax.lax.rsqrt(v + EPS_NORM)
            return (x_hat * w).astype(x.dtype)

        def activation_quant(x):
            scale = 127.0 / jnp.clip(jnp.max(jnp.abs(x), axis=-1, keepdims=True), EPS_Q, None)
            return jnp.clip(jnp.round(x * scale), -128, 127) / scale

        def weight_quant(w):
            scale = 1.0 / jnp.clip(jnp.mean(jnp.abs(w)), EPS_Q, None)
            return jnp.clip(jnp.round(w * scale), -1, 1) / scale

        def bitlinear(x, norm_w, w):
            x_norm = rmsnorm(x, norm_w)
            x_q = x_norm + jax.lax.stop_gradient(activation_quant(x_norm) - x_norm)
            w_q = w + jax.lax.stop_gradient(weight_quant(w) - w)
            return jnp.einsum('bsd,hd->bsh', x_q, w_q)
        key = jax.random.key(seed)
        k1, k2, k3 = jax.random.split(key, 3)
        dim, hidden = (128, 512)
        return {'x': jax.random.normal(k1, (4, 256, dim), dtype=jnp.float32), 'norm1_w': jnp.ones((dim,), jnp.float32), 'w1': jax.random.normal(k2, (hidden, dim), jnp.float32) * 0.02, 'act_scale': jnp.ones((1,), jnp.float32), 'act_bias': jnp.zeros((1,), jnp.float32), 'norm2_w': jnp.ones((hidden,), jnp.float32), 'w2': jax.random.normal(k3, (dim, hidden), jnp.float32) * 0.02}
    _L1_ffn_all = _L1_ffn_setup()
    _L1_ffn_in = {k: v for k, v in _L1_ffn_all.items() if k in ('norm1_w', 'w1', 'act_scale', 'act_bias', 'norm2_w', 'w2')}
    del _L1_ffn_all
    return {'x': x, 'ctx_1024': ctx_1024, 'mask_BxS2_bk0': mask_BxS2_bk0, 'L0_attn_Wq': _L0_attn_in['Wq'], 'L0_attn_bq': _L0_attn_in['bq'], 'L0_attn_Wk': _L0_attn_in['Wk'], 'L0_attn_bk': _L0_attn_in['bk'], 'L0_attn_Wv': _L0_attn_in['Wv'], 'L0_attn_bv': _L0_attn_in['bv'], 'L0_attn_Wo': _L0_attn_in['Wo'], 'L0_attn_bo': _L0_attn_in['bo'], 'L0_attn_rel_bias': _L0_attn_in['rel_bias'], 'L0_xattn_Wq': _L0_xattn_in['Wq'], 'L0_xattn_Wk': _L0_xattn_in['Wk'], 'L0_xattn_Wv': _L0_xattn_in['Wv'], 'L0_xattn_Wo': _L0_xattn_in['Wo'], 'L0_ffn_Ws1': _L0_ffn_in['Ws1'], 'L0_ffn_Ws2': _L0_ffn_in['Ws2'], 'L0_ffn_W1': _L0_ffn_in['W1'], 'L0_ffn_W2': _L0_ffn_in['W2'], 'L0_ffn_Wr': _L0_ffn_in['Wr'], 'L1_attn_proj_mat': _L1_attn_in['proj_mat'], 'L1_attn_Wq': _L1_attn_in['Wq'], 'L1_attn_bq': _L1_attn_in['bq'], 'L1_attn_Wk': _L1_attn_in['Wk'], 'L1_attn_bk': _L1_attn_in['bk'], 'L1_attn_Wv': _L1_attn_in['Wv'], 'L1_attn_bv': _L1_attn_in['bv'], 'L1_attn_Wo': _L1_attn_in['Wo'], 'L1_attn_bo': _L1_attn_in['bo'], 'L1_xattn_g1': _L1_xattn_in['g1'], 'L1_xattn_b1': _L1_xattn_in['b1'], 'L1_xattn_g2': _L1_xattn_in['g2'], 'L1_xattn_b2': _L1_xattn_in['b2'], 'L1_xattn_Wq': _L1_xattn_in['Wq'], 'L1_xattn_Wkv': _L1_xattn_in['Wkv'], 'L1_xattn_Wout': _L1_xattn_in['Wout'], 'L1_ffn_norm1_w': _L1_ffn_in['norm1_w'], 'L1_ffn_w1': _L1_ffn_in['w1'], 'L1_ffn_act_scale': _L1_ffn_in['act_scale'], 'L1_ffn_act_bias': _L1_ffn_in['act_bias'], 'L1_ffn_norm2_w': _L1_ffn_in['norm2_w'], 'L1_ffn_w2': _L1_ffn_in['w2']}

def reference(x, ctx_1024, mask_BxS2_bk0, L0_attn_Wq, L0_attn_bq, L0_attn_Wk, L0_attn_bk, L0_attn_Wv, L0_attn_bv, L0_attn_Wo, L0_attn_bo, L0_attn_rel_bias, L0_xattn_Wq, L0_xattn_Wk, L0_xattn_Wv, L0_xattn_Wo, L0_ffn_Ws1, L0_ffn_Ws2, L0_ffn_W1, L0_ffn_W2, L0_ffn_Wr, L1_attn_proj_mat, L1_attn_Wq, L1_attn_bq, L1_attn_Wk, L1_attn_bk, L1_attn_Wv, L1_attn_bv, L1_attn_Wo, L1_attn_bo, L1_xattn_g1, L1_xattn_b1, L1_xattn_g2, L1_xattn_b2, L1_xattn_Wq, L1_xattn_Wkv, L1_xattn_Wout, L1_ffn_norm1_w, L1_ffn_w1, L1_ffn_act_scale, L1_ffn_act_bias, L1_ffn_norm2_w, L1_ffn_w2):
    import jax
    import jax.numpy as jnp

    def _L0_attn_ref(x, Wq, bq, Wk, bk, Wv, bv, Wo, bo, rel_bias):
        import jax, jax.numpy as jnp
        import numpy as np
        import math
        D_MODEL = 128
        N_HEADS = 16
        D_K = D_MODEL // N_HEADS
        MAX_REL = 128

        def _rel_bias_matrix(rel_bias, seq_len):
            pos = jnp.arange(seq_len)
            rel = pos[:, None] - pos[None, :]
            idx = jnp.clip(rel, -MAX_REL, MAX_REL) + MAX_REL
            return rel_bias[:, idx]
        B, S, _ = x.shape

        def proj(W, b):
            y = x @ W.T + b
            return y.reshape(B, S, N_HEADS, D_K).transpose(0, 2, 1, 3)
        Q, K, V = (proj(Wq, bq), proj(Wk, bk), proj(Wv, bv))
        scores = jnp.einsum('bhqd,bhkd->bhqk', Q, K) / math.sqrt(D_K)
        scores = scores + _rel_bias_matrix(rel_bias, S)[None]
        attn = jax.nn.softmax(scores, axis=-1)
        out = jnp.einsum('bhqk,bhkd->bhqd', attn, V)
        out = out.transpose(0, 2, 1, 3).reshape(B, S, D_MODEL)
        return out @ Wo.T + bo

    def _L0_xattn_ref(x_query, x_kv, Wq, Wk, Wv, Wo):
        import jax, jax.numpy as jnp
        import numpy as np
        DIM = 128
        NUM_HEADS = 16
        HEAD_DIM = DIM // NUM_HEADS
        ROPE_BASE = 10000.0
        SCALE = 1.0 / np.sqrt(HEAD_DIM)

        def _rotate_half(x):
            x1, x2 = jnp.split(x, 2, axis=-1)
            return jnp.concatenate([-x2, x1], axis=-1)

        def _rope(x, seq_len):
            inv_freq = 1.0 / ROPE_BASE ** (jnp.arange(0, HEAD_DIM, 2, dtype=jnp.float32) / HEAD_DIM)
            t = jnp.arange(seq_len, dtype=jnp.float32)
            freqs = jnp.outer(t, inv_freq)
            emb = jnp.concatenate([freqs, freqs], -1)
            cos = jnp.cos(emb)[None, None]
            sin = jnp.sin(emb)[None, None]
            return x * cos + _rotate_half(x) * sin
        B, T_q, _ = x_query.shape
        T_k = x_kv.shape[1]
        h, d = (NUM_HEADS, HEAD_DIM)
        q = (x_query @ Wq.T).reshape(B, T_q, h, d).transpose(0, 2, 1, 3)
        k = (x_kv @ Wk.T).reshape(B, T_k, h, d).transpose(0, 2, 1, 3)
        v = (x_kv @ Wv.T).reshape(B, T_k, h, d).transpose(0, 2, 1, 3)
        q = _rope(q, T_q)
        k = _rope(k, T_k)
        attn = jnp.einsum('bhqd,bhkd->bhqk', q, k) * SCALE
        attn = jax.nn.softmax(attn, axis=-1)
        out = jnp.einsum('bhqk,bhkd->bhqd', attn, v)
        out = out.transpose(0, 2, 1, 3).reshape(B, T_q, DIM)
        return out @ Wo.T

    def _L0_ffn_ref(x, Ws1, Ws2, W1, W2, Wr):
        import jax, jax.numpy as jnp
        import numpy as np
        D_MODEL = 128
        EXPERT_DIM = 64
        N_EXPERTS = 8
        TOP_K = 2

        def _sq_relu(h):
            return jnp.square(jax.nn.relu(h))
        shape = x.shape
        xf = x.reshape(-1, D_MODEL)
        out_shared = _sq_relu(xf @ Ws1) @ Ws2
        logits = xf @ Wr
        top_vals, top_idx = jax.lax.top_k(logits, TOP_K)
        rw = jax.nn.softmax(top_vals.astype(jnp.float32), axis=-1).astype(x.dtype)
        onehot = jax.nn.one_hot(top_idx, N_EXPERTS, dtype=x.dtype)
        prob = jnp.einsum('tk,tke->te', rw, onehot)
        prob = jnp.trunc(prob)
        h = _sq_relu(jnp.einsum('td,edf->tef', xf, W1))
        y = jnp.einsum('tef,efd->ted', h, W2)
        out_routed = jnp.einsum('ted,te->td', y, prob)
        return (out_shared + out_routed).reshape(shape)

    def _L1_attn_ref(x, proj_mat, Wq, bq, Wk, bk, Wv, bv, Wo, bo):
        import jax, jax.numpy as jnp
        import numpy as np
        import math
        D_MODEL = 128
        N_HEAD = 16
        D_HEAD = D_MODEL // N_HEAD
        D_KMAP = 128
        B, L = (4, 512)

        def _fourier_kernel(x, proj_mat):
            p = jnp.einsum('blhd,dm->blhm', x, proj_mat) / math.sqrt(D_HEAD)
            return jnp.concatenate([jnp.cos(p), jnp.sin(p)], axis=-1) / math.sqrt(D_KMAP)
        Bv, Lv, _ = x.shape
        q = (x @ Wq.T + bq).reshape(Bv, Lv, N_HEAD, D_HEAD)
        k = (x @ Wk.T + bk).reshape(Bv, Lv, N_HEAD, D_HEAD)
        v = (x @ Wv.T + bv).reshape(Bv, Lv, N_HEAD, D_HEAD)
        q_prime = _fourier_kernel(q, proj_mat)
        k_prime = _fourier_kernel(k, proj_mat)
        kv = jnp.einsum('blhm,blhd->bhmd', k_prime, v)
        out = jnp.einsum('blhm,bhmd->blhd', q_prime, kv)
        out = out.reshape(Bv, Lv, D_MODEL)
        return out @ Wo.T + bo

    def _L1_xattn_ref(x, latents, mask, g1, b1, g2, b2, Wq, Wkv, Wout):
        import jax, jax.numpy as jnp
        import numpy as np
        EPS = 1e-05

        def layer_norm(x, g, b):
            mu = jnp.mean(x, axis=-1, keepdims=True)
            var = jnp.mean((x - mu) ** 2, axis=-1, keepdims=True)
            return (x - mu) * jax.lax.rsqrt(var + EPS) * g + b
        heads, dim_head = (16, 64)
        b, n, D = x.shape
        l = latents.shape[1]
        xn = layer_norm(x, g1, b1)
        ln_lat = layer_norm(latents, g2, b2)
        q = ln_lat @ Wq
        kv = jnp.concatenate([xn, ln_lat], axis=1) @ Wkv
        k, v = jnp.split(kv, 2, axis=-1)

        def to_heads(t):
            return t.reshape(t.shape[0], t.shape[1], heads, dim_head).transpose(0, 2, 1, 3)
        q, k, v = (to_heads(q), to_heads(k), to_heads(v))
        scale = 1.0 / np.sqrt(np.sqrt(dim_head)).astype(np.float32)
        weight = jnp.einsum('bhld,bhnd->bhln', q * scale, k * scale)
        full_mask = jnp.concatenate([mask, jnp.ones((b, l), dtype=bool)], axis=1)
        neg = -jnp.finfo(weight.dtype).max
        weight = jnp.where(full_mask[:, None, None, :], weight, neg)
        weight = jax.nn.softmax(weight.astype(jnp.float32), axis=-1).astype(q.dtype)
        out = jnp.einsum('bhln,bhnd->bhld', weight, v)
        out = out.transpose(0, 2, 1, 3).reshape(b, l, heads * dim_head)
        return out @ Wout

    def _L1_ffn_ref(x, norm1_w, w1, act_scale, act_bias, norm2_w, w2):
        import jax, jax.numpy as jnp
        import numpy as np
        EPS_NORM = 1e-08
        EPS_Q = 1e-05

        def rmsnorm(x, w):
            v = jnp.mean(jnp.square(x.astype(jnp.float32)), axis=-1, keepdims=True)
            x_hat = x * jax.lax.rsqrt(v + EPS_NORM)
            return (x_hat * w).astype(x.dtype)

        def activation_quant(x):
            scale = 127.0 / jnp.clip(jnp.max(jnp.abs(x), axis=-1, keepdims=True), EPS_Q, None)
            return jnp.clip(jnp.round(x * scale), -128, 127) / scale

        def weight_quant(w):
            scale = 1.0 / jnp.clip(jnp.mean(jnp.abs(w)), EPS_Q, None)
            return jnp.clip(jnp.round(w * scale), -1, 1) / scale

        def bitlinear(x, norm_w, w):
            x_norm = rmsnorm(x, norm_w)
            x_q = x_norm + jax.lax.stop_gradient(activation_quant(x_norm) - x_norm)
            w_q = w + jax.lax.stop_gradient(weight_quant(w) - w)
            return jnp.einsum('bsd,hd->bsh', x_q, w_q)
        h = bitlinear(x, norm1_w, w1)
        h = act_scale * jnp.square(jax.nn.relu(h)) + act_bias
        y = bitlinear(h, norm2_w, w2)
        return y
    x = _layernorm(x + _L0_attn_ref(x, L0_attn_Wq, L0_attn_bq, L0_attn_Wk, L0_attn_bk, L0_attn_Wv, L0_attn_bv, L0_attn_Wo, L0_attn_bo, L0_attn_rel_bias), axis=-1)
    x = _layernorm(x + _L0_xattn_ref(x, ctx_1024, L0_xattn_Wq, L0_xattn_Wk, L0_xattn_Wv, L0_xattn_Wo), axis=-1)
    x = _layernorm(x + _L0_ffn_ref(x, L0_ffn_Ws1, L0_ffn_Ws2, L0_ffn_W1, L0_ffn_W2, L0_ffn_Wr), axis=-1)
    x = _layernorm(x + _L1_attn_ref(x, L1_attn_proj_mat, L1_attn_Wq, L1_attn_bq, L1_attn_Wk, L1_attn_bk, L1_attn_Wv, L1_attn_bv, L1_attn_Wo, L1_attn_bo), axis=-1)
    x = _layernorm(x + _L1_xattn_ref(ctx_1024, x, mask_BxS2_bk0, L1_xattn_g1, L1_xattn_b1, L1_xattn_g2, L1_xattn_b2, L1_xattn_Wq, L1_xattn_Wkv, L1_xattn_Wout), axis=-1)
    x = _layernorm(x + _L1_ffn_ref(x, L1_ffn_norm1_w, L1_ffn_w1, L1_ffn_act_scale, L1_ffn_act_bias, L1_ffn_norm2_w, L1_ffn_w2), axis=-1)
    return x

_drawn_inputs = setup_inputs


def setup_inputs(seed=0):
    import zlib

    import numpy as np

    out = dict(_drawn_inputs(seed))
    spreads = {'L0_attn_bq': (0.0, 0.321),
     'L0_attn_bk': (0.0, 2.0),
     'L0_attn_bv': (0.0, 0.1),
     'L0_attn_bo': (0.0, 0.1),
     'L1_xattn_g1': (1.0, 0.2),
     'L1_xattn_b1': (0.0, 0.312),
     'L1_xattn_g2': (1.0, 0.2),
     'L1_xattn_b2': (0.0, 0.1),
     'L1_ffn_norm1_w': (1.0, 0.2),
     'L1_ffn_norm2_w': (1.0, 0.2)}
    factors = {'L0_attn_rel_bias': 37.529,
     'L0_ffn_Ws1': 6.627,
     'L0_ffn_Ws2': 5.261,
     'L1_attn_bq': 4.881,
     'L1_attn_bk': 4.463,
     'L1_attn_bo': 5.784}
    for name, (base, spread) in spreads.items():
        noise = np.random.default_rng([zlib.crc32(name.encode()), seed]).standard_normal(out[name].shape)
        drawn = base * np.exp(spread * noise) if base else spread * noise
        out[name] = jnp.asarray(drawn.astype(out[name].dtype))
    for name, factor in factors.items():
        out[name] = (out[name] * factor).astype(out[name].dtype)
    return out
```

```python
from contextlib import ExitStack

import numpy as np

import concourse.bass as bass
from concourse import mybir

F32 = mybir.dt.float32
BF16 = mybir.dt.bfloat16
I32 = mybir.dt.int32
ALU = mybir.AluOpType
ACT = mybir.ActivationFunctionType
AX = mybir.AxisListType

P = 128
S = 64
B = 64
H = 16
DH = 8
NT = B * S // P
T = 4
G = NT // T
GB = 2 * T
PAIRS = H // 2
VW = 2 * DH + 2
LN_EPS = 1e-5

CONST = {"ident": P, "headmask": H, "cos": S, "sin": S}
WEIGHTS = {
    "a_wq": P, "a_wk": P, "a_wv": P, "a_wo": P, "a_bq": 1, "a_bk": 1, "a_bv": P, "a_bo": P,
    "c_wq": P, "c_wqr": P, "c_wk": P, "c_wkr": P, "c_wv": P, "c_wo": P,
    "e_wr": 8, "e_w1": 576, "e_w2": 640,
    "f_wq": P, "f_wk": P, "f_wv": P, "f_bq": 1, "f_bk": 1, "f_bv": P, "f_proj": P, "f_wo": 1024, "f_bo": 1,
    "l_g1": P, "l_b1": P, "l_g2": P, "l_b2": P,
    "b_w1": 512, "b_w2": 512, "b_n1": P, "b_n2": 512, "b_as": 1, "b_ab": 1,
}


def columns(widths):
    at, where = 0, {}
    for name, width in widths.items():
        where[name] = (at, at + width)
        at += width
    return where, at


class Count:

    def __init__(self, i, per):
        self.i, self.per = i, per

    def __call__(self, n):
        assert 1 <= n <= self.per
        return self.i * self.per + n


class Chain:

    def __init__(self, eng, sem, i, per):
        self.eng, self.sem, self.at, self.n = eng, sem, Count(i, per), 0

    def __call__(self, ins):
        self.n += 1
        ins.then_inc(self.sem, 1)
        self.eng.wait_ge(self.sem, self.at(self.n))


class Norm:

    def __init__(self, sb):
        self.sums, self.stats, self.moments = sb("sums", [P, T, P]), sb("stats", [P, T, 6]), sb("mom", [P, T, 2])


def residual_step(nc, c, norm, step, tile, t, branch, x):
    step(nc.vector.tensor_tensor(norm.sums[:, t, :], branch, x, ALU.add))
    step(nc.vector.bn_stats(norm.stats[:, t, :], norm.sums[:, t, :]))
    nc.vector.tensor_scalar(c["stream"][:, bass.ds(tile, 1), :], norm.sums[:, t, :], 1.0, None, ALU.mult)
    return nc.vector.bn_aggr(norm.moments[:, t, :], norm.stats[:, t, :])


def keep_moments(nc, c, norm, i):
    return nc.vector.tensor_scalar(c["moments"][:, bass.ds(i * T, T), :], norm.moments[:, :, :], 1.0, None, ALU.mult)


def attention_phase(nc, ctx, c, name, cross):
    sb = lambda n, shape, dt=F32: ctx.enter_context(nc.sbuf_tensor(f"{name}_{n}", shape, dt))
    sem = lambda n: c["sem"](f"{name}_{n}")
    w = c["w"]
    k = c["const"]
    stream, moments, rstd, ps = c["stream"], c["moments"], c["rstd"], c["psum"]
    pre = "c_" if cross else "a_"
    scale = float(DH) ** -0.5

    xs = sb("xs", [P, T, P])
    xT = sb("xT", [P, T * P])
    QT = sb("QT", [P, T * P])
    KT = sb("KT", [P, T * P])
    KX = sb("KX", [P, 2, 2, H, S])
    V2 = sb("V2", [P, GB, PAIRS, VW])
    prob = sb("prob", [P, 2, H, S])
    probT = sb("probT", [P, 2, PAIRS, P])
    top = sb("top", [P, 2, H])
    inv = sb("inv", [P, 2, H])
    ao = sb("ao", [P, 2, P])
    aoT = sb("aoT", [P, 2, P])
    norm = Norm(sb)
    if cross:
        cs = sb("cs", [P, T, P])
        cT = sb("cT", [P, T * P])
        ropes = sb("ropes", [P, 4, T * P])

    names = ("staged xT_ps xT_sb proj_ps proj_sb v_ps v_sb kx scores shifted exped pT_ps pT_sb pv_ps "
             "ao_ready aoT_ps aoT_sb out_ps tile_done steps v_zero v_ones turn_done roped bo_added").split()
    s = {n: sem(n) for n in names}
    if cross:
        s["ctx_in"] = sem("ctx_in")
        s["cT_sb"] = sem("cT_sb")
        s["cT_ps"] = sem("cT_ps")
    STEPS = (4 if cross else 5) * T

    with nc.Block() as block:
        if cross:
            @block.sync
            def _(sp):
                sp.dma_start(cs[:, :, :], c["ctx"][:, 0:T, :]).then_inc(s["ctx_in"], 16)
                with sp.Fori(1, G) as i:
                    sp.wait_ge(s["cT_ps"], i)
                    sp.dma_start(cs[:, :, :], c["ctx"][:, bass.ds(i * T, T), :]).then_inc(s["ctx_in"], 16)

        @block.tensor
        def _(pe):
            pe.wait_ge(s["v_ones"], 1)
            with pe.Fori(0, G) as i:
                one, per_tile = Count(i, 1), Count(i, T)
                pe.wait_ge(s["staged"], one(1))
                for t in range(T):
                    last = nc.tensor.transpose(ps[:, 0, t * P:(t + 1) * P], xs[:, t, :], k("ident"))
                last.then_inc(s["xT_ps"], 1)
                if cross:
                    pe.wait_ge(s["ctx_in"], Count(i, 16)(16))
                    for t in range(T):
                        last = nc.tensor.transpose(ps[:, 1, t * P:(t + 1) * P], cs[:, t, :], k("ident"))
                    last.then_inc(s["cT_ps"], 1)
                pe.wait_ge(s["xT_sb"], one(1))
                keysT = xT
                if cross:
                    pe.wait_ge(s["cT_sb"], one(1))
                    keysT = cT
                    nc.tensor.matmul(ps[:, 2, :], w("c_wq"), xT[:, :], start=True, stop=True)
                    nc.tensor.matmul(ps[:, 3, :], w("c_wqr"), xT[:, :], start=True, stop=True)
                    nc.tensor.matmul(ps[:, 6, :], w("c_wk"), cT[:, :], start=True, stop=True)
                    nc.tensor.matmul(ps[:, 7, :], w("c_wkr"), cT[:, :], start=True, stop=True).then_inc(s["proj_ps"], 1)
                else:
                    nc.tensor.matmul(ps[:, 2, :], w("a_wq"), xT[:, :], start=True, stop=True)
                    nc.tensor.matmul(ps[:, 3, :], w("a_wk"), xT[:, :], start=True, stop=True).then_inc(s["proj_ps"], 1)
                for b in range(GB):
                    for par in range(2):
                        last = nc.tensor.matmul(ps[par * S:(par + 1) * S, 4 + b // 4, (b % 4) * P:(b % 4 + 1) * P],
                                                keysT[:, b * S:(b + 1) * S], w(pre + "wv"), start=True, stop=True)
                last.then_inc(s["v_ps"], 1)

                def scores(t):
                    pe.wait_ge(s["kx"], per_tile(t + 1))
                    if t == 0:
                        pe.wait_ge(s["proj_sb"], one(1))
                    if t >= 2:
                        pe.wait_ge(s["shifted"], per_tile(t - 1))
                    for half in range(2):
                        for b in range(2):
                            last = nc.tensor.matmul(
                                ps[b * S:(b + 1) * S, 2 * (t % 2) + half, :], QT[:, t * P + b * S:t * P + (b + 1) * S],
                                KX[:, t % 2, b, half * 8:half * 8 + 8, :], start=True, stop=True)
                    last.then_inc(s["scores"], 1)

                def weigh(t):
                    pe.wait_ge(s["exped"], per_tile(t + 1))
                    if t == 0:
                        pe.wait_ge(s["v_sb"], one(1))
                    else:
                        pe.wait_ge(s["pT_sb"], per_tile(t))
                    for j in range(PAIRS):
                        last = nc.tensor.transpose(ps[:, 4 + j // 4, (j % 4) * P:(j % 4 + 1) * P],
                                                   prob[:, t % 2, 2 * j:2 * j + 2, :], k("ident"))
                    last.then_inc(s["pT_ps"], 1)
                    pe.wait_ge(s["pT_sb"], per_tile(t + 1))
                    if t >= 1:
                        pe.wait_ge(s["ao_ready"], per_tile(t))
                    for j in range(PAIRS):
                        for b in range(2):
                            last = nc.tensor.matmul(ps[b * S:(b + 1) * S, 6, j * VW:(j + 1) * VW],
                                                    probT[:, t % 2, j, b * S:(b + 1) * S],
                                                    V2[:, 2 * t + b, j, :], start=True, stop=True)
                    last.then_inc(s["pv_ps"], 1)

                def project(t):
                    pe.wait_ge(s["ao_ready"], per_tile(t + 1))
                    if t >= 1:
                        pe.wait_ge(s["tile_done"], per_tile(t))
                    nc.tensor.transpose(ps[:, 7, 0:P], ao[:, t % 2, :], k("ident")).then_inc(s["aoT_ps"], 1)
                    pe.wait_ge(s["aoT_sb"], per_tile(t + 1))
                    last = nc.tensor.matmul(ps[:, 7, P:2 * P], aoT[:, t % 2, :], w(pre + "wo"), start=True, stop=True)
                    last.then_inc(s["out_ps"], 1)

                scores(0)
                for t in range(T):
                    if t + 1 < T:
                        scores(t + 1)
                    weigh(t)
                    if t >= 1:
                        project(t - 1)
                project(T - 1)
                pe.wait_ge(s["turn_done"], one(1))

        @block.scalar
        def _(act):
            with act.Fori(0, G) as i:
                one, per_tile = Count(i, 1), Count(i, T)
                act.wait_ge(s["xT_ps"], one(1))
                nc.scalar.copy(xT[:, :], ps[:, 0, :]).then_inc(s["xT_sb"], 1)
                if cross:
                    act.wait_ge(s["cT_ps"], one(1))
                    nc.scalar.copy(cT[:, :], ps[:, 1, :]).then_inc(s["cT_sb"], 1)
                else:
                    act.wait_ge(s["proj_ps"], one(1))
                    nc.scalar.activation(QT[:, :], ps[:, 2, :], ACT.Identity, bias=c["bq_scaled"][:, :],
                                         scale=scale)
                    nc.scalar.activation(KT[:, :], ps[:, 3, :], ACT.Identity, bias=w("a_bk")).then_inc(s["proj_sb"], 1)
                for t in range(T):
                    act.wait_ge(s["shifted"], per_tile(t + 1))
                    nc.scalar.activation(prob[:, t % 2, :, :], prob[:, t % 2, :, :], ACT.Exp,
                                         scale=scale if cross else 1.0).then_inc(s["exped"], 1)
                    act.wait_ge(s["pT_ps"], per_tile(t + 1))
                    if t >= 2:
                        act.wait_ge(s["pv_ps"], per_tile(t - 1))
                    nc.scalar.copy(probT[:, t % 2, :, :], ps[:, 4:6, :].rearrange("p a (b q) -> p (a b) q", b=4)
                                   ).then_inc(s["pT_sb"], 1)
                    for u in ([t - 1] if t >= 1 else []) + ([t] if t == T - 1 else []):
                        act.wait_ge(s["aoT_ps"], per_tile(u + 1))
                        nc.scalar.copy(aoT[:, u % 2, :], ps[:, 7, 0:P]).then_inc(s["aoT_sb"], 1)
                act.wait_ge(s["turn_done"], one(1))

        @block.vector
        def _(dve):
            nc.vector.memset(V2[:, :, :, :], 0.0).then_inc(s["v_zero"], 1)
            dve.wait_ge(s["v_zero"], 1)
            nc.vector.memset(V2[0:S, :, :, 2 * DH:2 * DH + 1], 1.0)
            nc.vector.memset(V2[S:P, :, :, 2 * DH + 1:VW], 1.0).then_inc(s["v_ones"], 1)
            dve.wait_ge(s["v_ones"], 1)
            with dve.Fori(0, G) as i:
                one, per_tile = Count(i, 1), Count(i, T)
                step = Chain(dve, s["steps"], i, STEPS)
                for t in range(T):
                    tile = i * T + t
                    last = nc.vector.tensor_scalar(xs[:, t, :], stream[:, bass.ds(tile, 1), :],
                                                   moments[:, bass.ds(tile, 1), 0], rstd[:, bass.ds(tile, 1)],
                                                   ALU.subtract, ALU.mult)
                last.then_inc(s["staged"], 1)
                dve.wait_ge(s["staged"], one(1))
                if cross:
                    dve.wait_ge(s["proj_ps"], one(1))
                    for n, (bank, tab) in enumerate(((2, "cos"), (3, "sin"), (6, "cos"), (7, "sin"))):
                        last = nc.vector.tensor_tensor(
                            ropes[:, n, :].rearrange("p (b s) -> p b s", s=S), ps[:, bank, :].rearrange("p (b s) -> p b s", s=S),
                            k(tab).unsqueeze(1).to_broadcast([P, GB, S]), ALU.mult)
                    last.then_inc(s["roped"], 1)
                dve.wait_ge(s["v_ps"], one(1))
                for q in range(2):
                    for par in range(2):
                        src = ps[par * S:(par + 1) * S, 4 + q, :].rearrange("p (b j e d) -> p b j e d", b=4, e=2, d=DH)[:, :, :, par, :]
                        dst = V2[par * S:(par + 1) * S, 4 * q:4 * q + 4, :, par * DH:(par + 1) * DH]
                        if cross:
                            last = nc.vector.tensor_copy(dst, src)
                        else:
                            bv = w("a_bv")[par * S:(par + 1) * S, :].rearrange("p (j e d) -> p j e d", e=2, d=DH)[:, :, par, :]
                            last = nc.vector.tensor_tensor(dst, src, bv.unsqueeze(1).to_broadcast([S, 4, PAIRS, DH]), ALU.add)
                last.then_inc(s["v_sb"], 1)

                def soften(t):
                    dve.wait_ge(s["scores"], per_tile(t + 1))
                    if t >= 2:
                        dve.wait_ge(s["pT_ps"], per_tile(t - 1))
                    sc = ps[:, 2 * (t % 2):2 * (t % 2) + 2, :].rearrange("p a (h q) -> p (a h) q", q=S)
                    if not cross:
                        step(nc.vector.tensor_tensor(prob[:, t % 2, :, :], sc, c["relbias"][:, :, :], ALU.add))
                        sc = prob[:, t % 2, :, :]
                    step(nc.vector.tensor_reduce(top[:, t % 2, :], sc, AX.X, ALU.max))
                    nc.vector.tensor_tensor(prob[:, t % 2, :, :], sc, top[:, t % 2, :].unsqueeze(2).to_broadcast([P, H, S]),
                                            ALU.subtract).then_inc(s["shifted"], 1)

                def divide(t):
                    dve.wait_ge(s["pv_ps"], per_tile(t + 1))
                    pv = ps[:, 6, 0:PAIRS * VW].rearrange("p (j v) -> p j v", v=VW)
                    step(nc.vector.reciprocal(inv[:, t % 2, :].rearrange("p (j e) -> p j e", e=2), pv[:, :, 2 * DH:VW]))
                    nc.vector.tensor_tensor(
                        ao[:, t % 2, :].rearrange("p (j e d) -> p j e d", e=2, d=DH),
                        pv[:, :, 0:2 * DH].rearrange("p j (e d) -> p j e d", e=2),
                        inv[:, t % 2, :].rearrange("p (j e) -> p j e", e=2).unsqueeze(3).to_broadcast([P, PAIRS, 2, DH]),
                        ALU.mult).then_inc(s["ao_ready"], 1)

                def residual(t):
                    dve.wait_ge(s["out_ps"], per_tile(t + 1))
                    if t == 0 and not cross:
                        dve.wait_ge(s["bo_added"], one(1))
                    residual_step(nc, c, norm, step, i * T + t, t, ps[:, 7, P:2 * P], xs[:, t, :]).then_inc(s["tile_done"], 1)

                for t in range(T):
                    soften(t)
                    if t >= 1:
                        divide(t - 1)
                    if t >= 2:
                        residual(t - 2)
                divide(T - 1)
                residual(T - 2)
                residual(T - 1)
                dve.wait_ge(s["tile_done"], per_tile(T))
                assert step.n == STEPS, step.n
                keep_moments(nc, c, norm, i).then_inc(s["turn_done"], 1)
                dve.wait_ge(s["turn_done"], one(1))

        @block.gpsimd
        def _(pool):
            with pool.Fori(0, G) as i:
                one, per_tile = Count(i, 1), Count(i, T)
                if cross:
                    pool.wait_ge(s["roped"], one(1))
                    nc.gpsimd.tensor_tensor(QT[:, :], ropes[:, 0, :], ropes[:, 1, :], ALU.add)
                    nc.gpsimd.tensor_tensor(KT[:, :], ropes[:, 2, :], ropes[:, 3, :], ALU.add).then_inc(s["proj_sb"], 1)
                else:
                    pool.wait_ge(s["xT_ps"], one(1))
                    nc.gpsimd.tensor_tensor(xs[:, :, :], xs[:, :, :], w("a_bo").unsqueeze(1).to_broadcast([P, T, P]),
                                            ALU.add).then_inc(s["bo_added"], 1)
                pool.wait_ge(s["proj_sb"], one(1))
                for t in range(T):
                    if t >= 2:
                        pool.wait_ge(s["scores"], per_tile(t - 1))
                    last = nc.gpsimd.tensor_tensor(
                        KX[:, t % 2, :, :, :],
                        KT[:, t * P:(t + 1) * P].rearrange("p (b s) -> p b s", s=S).unsqueeze(2).to_broadcast([P, 2, H, S]),
                        k("headmask").unsqueeze(1).unsqueeze(3).to_broadcast([P, 2, H, S]), ALU.mult)
                    last.then_inc(s["kx"], 1)
                pool.wait_ge(s["turn_done"], one(1))


def stage_tiles(nc, c, xs, i):
    for t in range(T):
        tile = i * T + t
        last = nc.vector.tensor_scalar(xs[:, t, :], c["stream"][:, bass.ds(tile, 1), :], c["moments"][:, bass.ds(tile, 1), 0],
                                       c["rstd"][:, bass.ds(tile, 1)], ALU.subtract, ALU.mult)
    return last


def experts_phase(nc, ctx, c, name):
    sb = lambda n, shape, dt=F32: ctx.enter_context(nc.sbuf_tensor(f"{name}_{n}", shape, dt))
    s = {n: c["sem"](f"{name}_{n}") for n in (
        "staged xT_ps xT_sb logits_ps pad_zero gap expgap prob up pick relu_done gated hidden down_ps down_sb y_ps "
        "steps tile_done turn_done").split()}
    w, ps = c["w"], c["psum"]
    E, F = 8, 64
    C = E * F // P
    xs, xT, norm = sb("xs", [P, T, P]), sb("xT", [P, T * P]), Norm(sb)
    logits, best, gap = sb("logits", [P, T, E]), sb("best", [P, T, E]), sb("gap", [P, T])
    chosen, prob = sb("chosen", [P, T, E]), sb("prob", [P, T, E, F], BF16)
    relu, gated, hid = sb("relu", [P, 2, T * P]), sb("gated", [P, 2, T * P]), sb("hid", [P, C + 1, T * P])
    yT = sb("yT", [P, T * P])
    STEPS = 5 + 2 * T

    with nc.Block() as block:
        @block.tensor
        def _(pe):
            pe.wait_ge(s["pad_zero"], 1)
            with pe.Fori(0, G) as i:
                one, up, down = Count(i, 1), Count(i, C + 1), Count(i, C)
                pe.wait_ge(s["staged"], one(1))
                for t in range(T):
                    last = nc.tensor.transpose(ps[:, 0, t * P:(t + 1) * P], xs[:, t, :], c["const"]("ident"))
                last.then_inc(s["xT_ps"], 1)
                pe.wait_ge(s["xT_sb"], one(1))
                for t in range(T):
                    last = nc.tensor.matmul(ps[:, 1, t * E:(t + 1) * E], xT[:, t * P:(t + 1) * P], w("e_wr"), start=True, stop=True)
                last.then_inc(s["logits_ps"], 1)

                def raise_(n):
                    if n >= 2:
                        pe.wait_ge(s["relu_done"], up(n - 1))
                    rows = P if n < C else F
                    nc.tensor.matmul(ps[0:rows, 2 + n % 2, :], w("e_w1")[:, n * P:n * P + rows], xT[:, :],
                                     start=True, stop=True).then_inc(s["up"], 1)

                def pick(n):
                    if n == 0:
                        pe.wait_ge(s["prob"], one(1))
                    if n >= 2:
                        pe.wait_ge(s["gated"], down(n - 1))
                    for t in range(T):
                        last = nc.tensor.matmul(ps[:, 4 + n % 2, t * P:(t + 1) * P], prob[:, t, 2 * n:2 * n + 2, :],
                                                c["ident16"][:, :], start=True, stop=True)
                    last.then_inc(s["pick"], 1)

                raise_(0)
                raise_(1)
                pick(0)
                pick(1)
                for n in range(C + 1):
                    if n + 2 < C + 1:
                        raise_(n + 2)
                    if n + 2 < C:
                        pick(n + 2)
                    pe.wait_ge(s["hidden"], up(n + 1))
                    last = nc.tensor.matmul(ps[:, 6, :], w("e_w2")[:, n * P:(n + 1) * P], hid[:, n, :],
                                            start=(n == 0), stop=(n == C))
                last.then_inc(s["down_ps"], 1)
                pe.wait_ge(s["down_sb"], one(1))
                for t in range(T):
                    last = nc.tensor.transpose(ps[:, 7, t * P:(t + 1) * P], yT[:, t * P:(t + 1) * P], c["const"]("ident"))
                last.then_inc(s["y_ps"], 1)
                pe.wait_ge(s["turn_done"], one(1))

        @block.scalar
        def _(act):
            with act.Fori(0, G) as i:
                one, up, down = Count(i, 1), Count(i, C + 1), Count(i, C)
                act.wait_ge(s["xT_ps"], one(1))
                nc.scalar.copy(xT[:, :], ps[:, 0, :]).then_inc(s["xT_sb"], 1)
                act.wait_ge(s["gap"], one(1))
                nc.scalar.activation(gap[:, :], gap[:, :], ACT.Exp).then_inc(s["expgap"], 1)

                def relu_of(n):
                    rows = P if n < C else F
                    act.wait_ge(s["up"], up(n + 1))
                    if 2 <= n < C:
                        act.wait_ge(s["gated"], down(n - 1))
                    nc.scalar.activation(relu[0:rows, n % 2, :], ps[0:rows, 2 + n % 2, :], ACT.Relu).then_inc(s["relu_done"], 1)

                relu_of(0)
                for n in range(C + 1):
                    if n + 1 <= C:
                        if n + 1 == C:
                            act.wait_ge(s["gated"], down(C - 1))
                        relu_of(n + 1)
                    if n < C:
                        act.wait_ge(s["gated"], down(n + 1))
                        nc.scalar.activation(hid[:, n, :], gated[:, n % 2, :], ACT.Square).then_inc(s["hidden"], 1)
                    else:
                        act.wait_ge(s["relu_done"], up(C + 1))
                        nc.scalar.activation(hid[0:F, n, :], relu[0:F, n % 2, :], ACT.Square).then_inc(s["hidden"], 1)
                act.wait_ge(s["down_ps"], one(1))
                nc.scalar.copy(yT[:, :], ps[:, 6, :]).then_inc(s["down_sb"], 1)
                act.wait_ge(s["turn_done"], one(1))

        @block.vector
        def _(dve):
            nc.vector.memset(hid[:, C, :], 0.0).then_inc(s["pad_zero"], 1)
            with dve.Fori(0, G) as i:
                one, up, down = Count(i, 1), Count(i, C + 1), Count(i, C)
                step = Chain(dve, s["steps"], i, STEPS)
                stage_tiles(nc, c, xs, i).then_inc(s["staged"], 1)
                dve.wait_ge(s["logits_ps"], one(1))
                nc.vector.tensor_scalar(logits[:, :, :], ps[:, 1, 0:T * E].rearrange("p (t e) -> p t e", e=E), 1.0, None, ALU.mult)
                for t in range(T):
                    last = nc.vector.max(best[:, t, :], ps[:, 1, t * E:(t + 1) * E])
                step(last)
                nc.vector.tensor_tensor(gap[:, :], best[:, :, 1], best[:, :, 0], ALU.subtract).then_inc(s["gap"], 1)
                step(nc.vector.tensor_tensor(chosen[:, :, :], logits[:, :, :], best[:, :, 0:1].to_broadcast([P, T, E]), ALU.is_equal))
                dve.wait_ge(s["expgap"], one(1))
                step(nc.vector.tensor_scalar(gap[:, :], gap[:, :], 1.0, None, ALU.add))
                step(nc.vector.reciprocal(gap[:, :], gap[:, :]))
                step(nc.vector.tensor_scalar(gap[:, :], gap[:, :], 1.0, None, ALU.is_ge))
                nc.vector.tensor_tensor(prob[:, :, :, :], chosen[:, :, :].unsqueeze(3).to_broadcast([P, T, E, F]),
                                        gap[:, :].unsqueeze(2).unsqueeze(3).to_broadcast([P, T, E, F]), ALU.mult).then_inc(s["prob"], 1)
                for n in range(C):
                    dve.wait_ge(s["relu_done"], up(n + 1))
                    dve.wait_ge(s["pick"], down(n + 1))
                    if n >= 2:
                        dve.wait_ge(s["hidden"], up(n - 1))
                    nc.vector.tensor_tensor(gated[:, n % 2, :], ps[:, 4 + n % 2, :], relu[:, n % 2, :], ALU.mult).then_inc(s["gated"], 1)
                for t in range(T):
                    if t == 0:
                        dve.wait_ge(s["y_ps"], one(1))
                    residual_step(nc, c, norm, step, i * T + t, t, ps[:, 7, t * P:(t + 1) * P], xs[:, t, :]).then_inc(s["tile_done"], 1)
                dve.wait_ge(s["tile_done"], Count(i, T)(T))
                assert step.n == STEPS, step.n
                keep_moments(nc, c, norm, i).then_inc(s["turn_done"], 1)
                dve.wait_ge(s["turn_done"], one(1))


def fourier_phase(nc, ctx, c, name):
    sb = lambda n, shape, dt=F32: ctx.enter_context(nc.sbuf_tensor(f"{name}_{n}", shape, dt))
    s = {n: c["sem"](f"{name}_{n}") for n in (
        "consts v_zero staged xT_ps xT_sb qkv_ps qk_sb v_sb z_ps reduced wrapped feats kv_ps kv_sb kvT_ps kvT_sb o_ps o_sb "
        "y_ps yT_sb yt_ps steps tile_done turn_done").split()}
    w, ps = c["w"], c["psum"]
    M = 128
    Q4 = H // 4
    UNIT = 1024
    KU = H * M // UNIT
    UPG = T * KU + Q4 * 2
    MAGIC = 1.5 * 2.0 ** 23
    TWO_PI, HALF_PI = 6.2831850, 1.5707962
    xs, xT, norm = sb("xs", [P, T, P]), sb("xT", [P, T * P]), Norm(sb)
    qT, kT = sb("qT", [P, T * P]), sb("kT", [P, T * P])
    projX = sb("projX", [P, H, M])
    vS = sb("vS", [P, T, H, 32])
    whole, frac, wrap = sb("whole", [P, 2, UNIT]), sb("frac", [P, 2, UNIT]), sb("wrap", [P, 2, UNIT])
    feats = sb("feats", [P, 2, 8, 2, M])
    qf = sb("qf", [P, 2, 4, 2, T * P])
    kvs = sb("kvs", [P, Q4, 2, M])
    kvm = sb("kvm", [P, T, Q4, 2, P])
    oT, yT = sb("oT", [P, Q4, T * P]), sb("yT", [P, T * P])
    half_pi, qb, vb = sb("half_pi", [P, 1]), sb("qb", [P, 1]), sb("vb", [P, P])
    kb = sb("kb", [P, 1])
    turn_scale = float(DH) ** -0.5 / (2 * np.pi)
    STEPS = UPG + 2 * T

    with nc.Block() as block:
        @block.tensor
        def _(pe):
            pe.wait_ge(s["consts"], 6)
            with pe.Fori(0, G) as i:
                one, per_tile, unit, quarter = Count(i, 1), Count(i, T), Count(i, UPG), Count(i, Q4)
                pe.wait_ge(s["staged"], one(1))
                for t in range(T):
                    last = nc.tensor.transpose(ps[:, 6, t * P:(t + 1) * P], xs[:, t, :], c["const"]("ident"))
                last.then_inc(s["xT_ps"], 1)
                pe.wait_ge(s["xT_sb"], one(1))
                nc.tensor.matmul(ps[:, 4, :], w("f_wq"), xT[:, :], start=True, stop=True)
                nc.tensor.matmul(ps[:, 5, :], w("f_wk"), xT[:, :], start=True, stop=True)
                for t in range(T):
                    last = nc.tensor.matmul(ps[:, 7, t * P:(t + 1) * P], xT[:, t * P:(t + 1) * P], w("f_wv"), start=True, stop=True)
                last.then_inc(s["qkv_ps"], 1)

                def key_angles(n):
                    t, u = divmod(n, KU)
                    if n >= 2:
                        pe.wait_ge(s["reduced"], unit(n - 1))
                    for q in range(2):
                        h = u * 8 + q * 4
                        last = nc.tensor.matmul(ps[:, 2 * (n % 2) + q, :], kT[:, t * P:(t + 1) * P], projX[:, h:h + 4, :],
                                                start=True, stop=True)
                    last.then_inc(s["z_ps"], 1)

                def query_angles(n):
                    pe.wait_ge(s["reduced"], unit(n - 1))
                    for q in range(2):
                        h = 2 * (n - T * KU) + q
                        last = nc.tensor.matmul(ps[:, 2 * (n % 2) + q, :], projX[:, h, :], qT[:, :], start=True, stop=True)
                    last.then_inc(s["z_ps"], 1)

                def angles(n):
                    if n < T * KU:
                        key_angles(n)
                    elif n < UPG:
                        query_angles(n)

                def key_values(t):
                    if t >= 1:
                        pe.wait_ge(s["kv_sb"], per_tile(t))
                    for u in range(KU):
                        pe.wait_ge(s["feats"], unit(t * KU + u + 1))
                        if t == 0 and u == 0:
                            pe.wait_ge(s["v_sb"], one(1))
                        for h in range(8 * u, 8 * u + 8):
                            q, r = divmod(h, 4)
                            last = nc.tensor.matmul(ps[32 * r:32 * r + 32, 4 + q // 2, (q % 2) * 256:(q % 2 + 1) * 256],
                                                    vS[:, t, h, :], feats[:, (t * KU + u) % 2, h % 8, :, :], start=True, stop=True)
                    last.then_inc(s["kv_ps"], 1)

                def turn_key_values(t):
                    pe.wait_ge(s["kv_sb"], per_tile(t + 1))
                    if t >= 1:
                        pe.wait_ge(s["kvT_sb"], per_tile(t))
                    for q in range(Q4):
                        for e in range(2):
                            n = 2 * q + e
                            last = nc.tensor.transpose(ps[:, 6 + n // 4, (n % 4) * P:(n % 4 + 1) * P], kvs[:, q, e, :], c["const"]("ident"))
                    last.then_inc(s["kvT_ps"], 1)

                def outputs(q):
                    pe.wait_ge(s["feats"], unit(T * KU + 2 * q + 2))
                    if q == 0:
                        pe.wait_ge(s["kvT_sb"], per_tile(T))
                    if q >= 2:
                        pe.wait_ge(s["o_sb"], quarter(q - 1))
                    for t in range(T):
                        for e in range(2):
                            for r in range(4):
                                last = nc.tensor.matmul(ps[32 * r:32 * r + 32, 4 + q % 2, t * P:(t + 1) * P],
                                                        kvm[:, t, q, e, 32 * r:32 * r + 32], qf[:, q % 2, r, e, t * P:(t + 1) * P],
                                                        start=(e == 0), stop=(e == 1))
                    last.then_inc(s["o_ps"], 1)

                pe.wait_ge(s["qk_sb"], one(1))
                angles(0)
                angles(1)
                for t in range(T):
                    angles(2 * t + 2)
                    key_values(t)
                    angles(2 * t + 3)
                    if t >= 1:
                        turn_key_values(t - 1)
                turn_key_values(T - 1)
                for q in range(Q4):
                    angles(T * KU + 2 * q + 2)
                    angles(T * KU + 2 * q + 3)
                    outputs(q)
                for par in range(2):
                    for q in range(Q4):
                        if par == 0:
                            pe.wait_ge(s["o_sb"], quarter(q + 1))
                        at = (par * Q4 + q) * P
                        toks = oT[:, q, :].rearrange("p (t b s) -> p t b s", b=2, s=S)[:, :, par, :]
                        last = nc.tensor.matmul(ps[:, 6, par * 256:(par + 1) * 256], w("f_wo")[:, at:at + P], toks,
                                                start=(q == 0), stop=(q == Q4 - 1))
                last.then_inc(s["y_ps"], 1)
                pe.wait_ge(s["yT_sb"], one(1))
                for t in range(T):
                    last = nc.tensor.transpose(ps[:, 7, t * P:(t + 1) * P], yT[:, t * P:(t + 1) * P], c["const"]("ident"))
                last.then_inc(s["yt_ps"], 1)
                pe.wait_ge(s["turn_done"], one(1))

        @block.scalar
        def _(act):
            nc.scalar.mul(qb[:, :], w("f_bq"), turn_scale).then_inc(s["consts"], 1)
            nc.scalar.mul(kb[:, :], w("f_bk"), turn_scale).then_inc(s["consts"], 1)
            nc.scalar.mul(vb[:, :], w("f_bv"), 1.0 / M).then_inc(s["consts"], 1)
            act.wait_ge(s["consts"], 6)
            with act.Fori(0, G) as i:
                one, per_tile, unit, quarter = Count(i, 1), Count(i, T), Count(i, UPG), Count(i, Q4)
                act.wait_ge(s["xT_ps"], one(1))
                nc.scalar.copy(xT[:, :], ps[:, 6, :]).then_inc(s["xT_sb"], 1)
                act.wait_ge(s["qkv_ps"], one(1))
                nc.scalar.activation(qT[:, :], ps[:, 4, :], ACT.Identity, bias=qb[:, :], scale=turn_scale)
                nc.scalar.activation(kT[:, :], ps[:, 5, :], ACT.Identity, bias=kb[:, :], scale=turn_scale).then_inc(s["qk_sb"], 1)

                def features(n):
                    act.wait_ge(s["reduced"], unit(n + 1))
                    if n < T * KU:
                        if n >= 2 and n % KU == 0:
                            act.wait_ge(s["kv_ps"], per_tile(n // KU))
                        sin = feats[:, n % 2, :, 1, :]
                        cos = feats[:, n % 2, :, 0, :]
                        view = lambda a: a.rearrange("p (h m) -> p h m", m=M)
                    else:
                        v = n - T * KU
                        if v >= 4 and v % 2 == 0:
                            act.wait_ge(s["o_ps"], quarter(v // 2 - 1))
                        h = (v % 2) * 2
                        sin = qf[:, (v // 2) % 2, h:h + 2, 1, :]
                        cos = qf[:, (v // 2) % 2, h:h + 2, 0, :]
                        view = lambda a: a.rearrange("p (h m) -> p h m", h=2)
                    nc.scalar.activation(sin, view(frac[:, n % 2, :]), ACT.Sin, scale=TWO_PI)
                    act.wait_ge(s["wrapped"], unit(n + 1))
                    nc.scalar.activation(cos, view(wrap[:, n % 2, :]), ACT.Sin, bias=half_pi[:, :], scale=-TWO_PI).then_inc(s["feats"], 1)

                for n in range(UPG):
                    features(n)
                    v = n - T * KU
                    if n < T * KU:
                        if n % 2 == 0 and n >= 2:
                            t = n // 2 - 1
                            act.wait_ge(s["kv_ps"], per_tile(t + 1))
                            if t >= 1:
                                act.wait_ge(s["kvT_ps"], per_tile(t))
                            nc.scalar.copy(kvs[:, :, :, :], ps[:, 4:6, :].rearrange("p a (b e m) -> p (a b) e m", b=2, e=2)).then_inc(s["kv_sb"], 1)
                    elif v == 0:
                        act.wait_ge(s["kv_ps"], per_tile(T))
                        act.wait_ge(s["kvT_ps"], per_tile(T - 1))
                        nc.scalar.copy(kvs[:, :, :, :], ps[:, 4:6, :].rearrange("p a (b e m) -> p (a b) e m", b=2, e=2)).then_inc(s["kv_sb"], 1)
                act.wait_ge(s["y_ps"], one(1))
                nc.scalar.activation(yT[:, :].rearrange("p (t b s) -> p b t s", b=2, s=S),
                                     ps[:, 6, :].rearrange("p (b t s) -> p b t s", b=2, s=S), ACT.Identity,
                                     bias=w("f_bo")).then_inc(s["yT_sb"], 1)
                act.wait_ge(s["turn_done"], one(1))

        @block.vector
        def _(dve):
            nc.vector.memset(half_pi[:, :], HALF_PI).then_inc(s["consts"], 1)
            nc.vector.memset(vS[:, :, :, :], 0.0).then_inc(s["consts"], 1)
            dve.wait_ge(s["consts"], 6)
            with dve.Fori(0, G) as i:
                one, per_tile, unit, quarter = Count(i, 1), Count(i, T), Count(i, UPG), Count(i, Q4)
                step = Chain(dve, s["steps"], i, STEPS)
                stage_tiles(nc, c, xs, i).then_inc(s["staged"], 1)
                dve.wait_ge(s["qkv_ps"], one(1))
                for b in range(2):
                    half = slice(b * S, (b + 1) * S)
                    last = nc.vector.scalar_tensor_tensor(
                        vS[half, :, :, b * DH:(b + 1) * DH], ps[half, 7, :].rearrange("p (t h d) -> p t h d", h=H, d=DH), 1.0 / M,
                        vb[half, :].rearrange("p (h d) -> p h d", d=DH).unsqueeze(1).to_broadcast([S, T, H, DH]), ALU.mult, ALU.add)
                last.then_inc(s["v_sb"], 1)

                def reduce_(n):
                    dve.wait_ge(s["z_ps"], unit(n + 1))
                    z = ps[:, 2 * (n % 2):2 * (n % 2) + 2, :].rearrange("p a b -> p (a b)")
                    step(nc.vector.tensor_scalar(whole[:, n % 2, :], z, MAGIC, MAGIC, ALU.add, ALU.subtract))
                    if n >= 2:
                        dve.wait_ge(s["feats"], unit(n - 1))
                    nc.vector.tensor_tensor(frac[:, n % 2, :], z, whole[:, n % 2, :], ALU.subtract).then_inc(s["reduced"], 1)
                    dve.wait_ge(s["reduced"], unit(n + 1))
                    nc.vector.tensor_scalar(wrap[:, n % 2, :].bitcast(I32), frac[:, n % 2, :].bitcast(I32), 0x7FFFFFFF, None, ALU.bitwise_and).then_inc(s["wrapped"], 1)

                def keep_kv(t):
                    dve.wait_ge(s["kvT_ps"], per_tile(t + 1))
                    nc.vector.tensor_copy(kvm[:, t, :, :, :], ps[:, 6:8, :].rearrange("p a (b e m) -> p (a b) e m", b=2, e=2)).then_inc(s["kvT_sb"], 1)

                def keep_o(q):
                    dve.wait_ge(s["o_ps"], quarter(q + 1))
                    nc.vector.tensor_copy(oT[:, q, :], ps[:, 4 + q % 2, :]).then_inc(s["o_sb"], 1)

                for n in range(UPG):
                    reduce_(n)
                    if n < T * KU and n % 2 == 1 and n >= 5:
                        keep_kv((n - 5) // 2)
                    v = n - T * KU
                    if v == 0:
                        keep_kv(T - 2)
                    if v == 2:
                        keep_kv(T - 1)
                    if v >= 4 and v % 2 == 0:
                        keep_o(v // 2 - 2)
                keep_o(Q4 - 2)
                keep_o(Q4 - 1)
                for t in range(T):
                    if t == 0:
                        dve.wait_ge(s["yt_ps"], one(1))
                    residual_step(nc, c, norm, step, i * T + t, t, ps[:, 7, t * P:(t + 1) * P], xs[:, t, :]).then_inc(s["tile_done"], 1)
                dve.wait_ge(s["tile_done"], per_tile(T))
                assert step.n == STEPS, step.n
                keep_moments(nc, c, norm, i).then_inc(s["turn_done"], 1)
                dve.wait_ge(s["turn_done"], one(1))

        @block.gpsimd
        def _(pool):
            nc.gpsimd.tensor_tensor(projX[:, :, :], w("f_proj").unsqueeze(1).to_broadcast([P, H, M]),
                                    c["const"]("headmask").unsqueeze(2).to_broadcast([P, H, M]), ALU.mult).then_inc(s["consts"], 1)


def latents_phase(nc, ctx, c, name):
    sb = lambda n, shape, dt=F32: ctx.enter_context(nc.sbuf_tensor(f"{name}_{n}", shape, dt))
    s = {n: c["sem"](f"{name}_{n}") for n in (
        "mats_in ab_ps ab_sb stats2 root2 ctx_in prep prep_steps consts staged scaled latT_ps latT_sb ctxT_ps XT_sb X_ps X_sb "
        "th_ps th_sb th16 rough top diag scores exped sums share px_ps px_sb recip y_ps yT_sb yt_ps steps tile_done turn_done pool_steps taken XT16").split()}
    w, ps = c["w"], c["psum"]
    norm = Norm(sb)
    lat, cx = sb("lat", [P, T, P]), sb("cx", [P, T, P])
    mom2, momc = sb("mom2", [P, NT, 2]), sb("momc", [P, NT, 2])
    rstd2, rstdc = sb("rstd2", [P, NT]), sb("rstdc", [P, NT])
    keep, drop, bias = sb("keep", [P, NT]), sb("drop", [P, NT]), sb("bias", [P, B])
    A, N = sb("A", [P, H, P]), sb("N", [P, H, P])
    ident, ident16 = c["const"]("ident"), c["ident16"]
    ones16, ones32 = sb("ones16", [P, P], BF16), sb("ones32", [P, P])
    with ExitStack() as early:
        load = lambda n, shape, dt=F32: early.enter_context(nc.sbuf_tensor(f"{name}_{n}", shape, dt))
        mats = load("mats", [P, 4, PAIRS, P])
        cs = load("cs", [P, NT, P])
        mask = load("mask", [P, NT + B], mybir.dt.uint8)
        stats = load("stats2", [P, 4, 6])
        xn = load("xn", [P, 4, P])
        momt = load("momt", [P, 4, 2])
        with nc.Block() as block:
            @block.sync
            def _(sp):
                sp.dma_start(mats[:, :, :, :], c["l_mats"]).then_inc(s["mats_in"], 16)
                sp.dma_start(mask[:, :], c["mask"]).then_inc(s["mats_in"], 16)
                sp.dma_start(cs[:, :, :], c["ctx"]).then_inc(s["ctx_in"], 16)

            @block.tensor
            def _(pe):
                pe.wait_ge(s["mats_in"], 32)
                for h in range(H):
                    if h == 8:
                        pe.wait_ge(s["ab_sb"], 4)
                    par = h % 2
                    r = slice(par * S, par * S + S)
                    at = (h % 8 // 2) * P
                    nc.tensor.matmul(ps[:, par, at:at + P], mats[r, 0, h // 2, :], mats[r, 1, h // 2, :], start=True, stop=True)
                    last = nc.tensor.matmul(ps[:, 2 + par, at:at + P], mats[r, 2, h // 2, :], mats[r, 3, h // 2, :], start=True, stop=True)
                    if h % 8 == 7:
                        last.then_inc(s["ab_ps"], 1)

            @block.scalar
            def _(act):
                for q in range(2):
                    act.wait_ge(s["ab_ps"], q + 1)
                    for par in range(2):
                        heads = slice(8 * q + par, 8 * q + 8, 2)
                        nc.scalar.activation(A[:, heads, :], ps[:, par, :].rearrange("p (h d) -> p h d", d=P), ACT.Copy,
                                             scale=0.125).then_inc(s["ab_sb"], 1)
                        nc.scalar.copy(N[:, heads, :], ps[:, 2 + par, :].rearrange("p (h d) -> p h d", d=P)).then_inc(s["ab_sb"], 1)
                act.wait_ge(s["stats2"], 1)
                nc.scalar.activation(rstd2[:, :], rstd2[:, :], ACT.Sqrt)
                nc.scalar.activation(rstdc[:, :], rstdc[:, :], ACT.Sqrt).then_inc(s["root2"], 1)

            @block.vector
            def _(dve):
                nc.vector.memset(ones16[:, :], 1.0)
                nc.vector.memset(ones32[:, :], 1.0)
                dve.wait_ge(s["mats_in"], 32)
                nc.vector.tensor_scalar(keep[:, :], mask[:, 0:NT], 1.0, None, ALU.mult)
                nc.vector.tensor_scalar(drop[:, :], mask[:, 0:NT], -1.0, 1.0, ALU.mult, ALU.add)
                nc.vector.tensor_scalar(bias[:, :], mask[:, NT:NT + B], 1e30, 1e30, ALU.mult, ALU.subtract)
                dve.wait_ge(s["ctx_in"], 16)
                with dve.Fori(0, NT // 2) as i:
                    step = Chain(dve, s["prep_steps"], i, 3)
                    for u in range(2):
                        tile = i * 2 + u
                        nc.vector.tensor_scalar(xn[:, u, :], c["stream"][:, bass.ds(tile, 1), :], c["moments"][:, bass.ds(tile, 1), 0],
                                                c["rstd"][:, bass.ds(tile, 1)], ALU.subtract, ALU.mult)
                    step(nc.vector.tensor_scalar(xn[:, 2:4, :], cs[:, bass.ds(i * 2, 2), :], 1.0, None, ALU.mult))
                    nc.vector.tensor_scalar(c["stream"][:, bass.ds(i * 2, 2), :], xn[:, 0:2, :], 1.0, None, ALU.mult)
                    for u in range(4):
                        last = nc.vector.bn_stats(stats[:, u, :], xn[:, u, :])
                    step(last)
                    dve.sem_inc(s["taken"], 1)
                    for u in range(4):
                        last = nc.vector.bn_aggr(momt[:, u, :], stats[:, u, :])
                    step(last)
                    nc.vector.tensor_scalar(mom2[:, bass.ds(i * 2, 2), :], momt[:, 0:2, :], 1.0, None, ALU.mult)
                    nc.vector.tensor_scalar(momc[:, bass.ds(i * 2, 2), :], momt[:, 2:4, :], 1.0, None, ALU.mult).then_inc(s["prep"], 1)
                dve.wait_ge(s["prep"], NT // 2)
                nc.vector.tensor_scalar(rstd2[:, :], mom2[:, :, 1], LN_EPS, None, ALU.add)
                nc.vector.tensor_scalar(rstdc[:, :], momc[:, :, 1], LN_EPS, None, ALU.add).then_inc(s["stats2"], 1)
                dve.wait_ge(s["root2"], 1)
                nc.vector.reciprocal(rstd2[:, :], rstd2[:, :])
                nc.vector.reciprocal(rstdc[:, :], rstdc[:, :])

    bias_now = sb("bias_now", [P, 2, GB])
    craw = sb("craw", [P, T, P])
    gx = sb("gx", [P, 2, T, P])
    XT, XT16 = sb("XT", [P, GB, 2, S]), sb("XT16", [P, GB, 2 * S], BF16)
    X = sb("X", [P, GB, P])
    th, th16 = sb("th", [P, GB, H, S]), sb("th16", [P, GB, H, S], BF16)
    top, diag = sb("top", [P, 2, PAIRS]), sb("diag", [P, PAIRS, P], BF16)
    prob = sb("prob", [P, 4, 2, 512])
    recip = sb("recip", [P, 2, 512])
    share = sb("share", [P, 2, 2, 2, 512])
    px = sb("px", [P, H, GB, S])
    yT = sb("yT", [P, T * P])
    STEPS = 2 * T
    BP = GB // 2

    with nc.Block() as block:
        @block.sync
        def _(sp):
            sp.dma_start(craw[:, :, :], c["ctx"][:, 0:T, :]).then_inc(s["ctx_in"], 16)
            with sp.Fori(1, G) as i:
                sp.wait_ge(s["scaled"], i)
                sp.dma_start(craw[:, :, :], c["ctx"][:, bass.ds(i * T, T), :]).then_inc(s["ctx_in"], 16)

        @block.tensor
        def _(pe):
            def heads(g):
                one, head = Count(g, 1), Count(g, H)
                pe.wait_ge(s["staged"], one(1))
                for t in range(T):
                    nc.tensor.transpose(ps[:, 0, t * P:(t + 1) * P], lat[:, t, :], ident)
                for t in range(T):
                    last = nc.tensor.transpose(ps[:, 1, t * P:(t + 1) * P], cx[:, t, :], ident)
                last.then_inc(s["latT_ps"], 1)
                pe.wait_ge(s["XT_sb"], one(1))
                for h in range(H):
                    if h >= 4:
                        pe.wait_ge(s["th_sb"], head(h - 3))
                    nc.tensor.matmul(ps[:, h % 4, :], A[:, h, :], XT[:, :, 1, :], start=True, stop=True).then_inc(s["th_ps"], 1)

            def keys_back(g):
                for b in range(GB):
                    last = nc.tensor.transpose(ps[:, 4 + b // 4, (b % 4) * P:(b % 4 + 1) * P], XT[:, b, :, :], ident)
                last.then_inc(s["X_ps"], 1)

            def main(g):
                one, batch, head, pair = Count(g, 1), Count(g, GB), Count(g, H), Count(g, BP)

                def rough(b):
                    if b == 0:
                        pe.wait_ge(s["th_sb"], head(H))
                        pe.wait_ge(s["th16"], head(H))
                        pe.wait_ge(s["XT16"], one(1))
                    else:
                        pe.wait_ge(s["top"], batch(b))
                    for j in range(PAIRS):
                        last = nc.tensor.matmul(ps[:, j // 4, (j % 4) * P:(j % 4 + 1) * P], th16[:, b, 2 * j:2 * j + 2, :],
                                                XT16[:, b, :], start=True, stop=True)
                    last.then_inc(s["rough"], 1)

                def scores(b):
                    if b >= 1:
                        pe.wait_ge(s["exped"], batch(b))
                    for q in range(2):
                        nc.tensor.matmul(ps[:, 2 + q, :], XT[:, b, :, :], th[:, b, 8 * q:8 * q + 8, :], start=True, stop=False)
                    pe.wait_ge(s["diag"], batch(b + 1))
                    for q in range(2):
                        last = nc.tensor.matmul(ps[:, 2 + q, :], ones16[:, :], diag[:, 4 * q:4 * q + 4, :], start=False, stop=True)
                    last.then_inc(s["scores"], 1)

                def sums(p):
                    pe.wait_ge(s["exped"], batch(2 * p + 2))
                    if p >= 2:
                        pe.wait_ge(s["recip"], pair(p - 1))
                    for b in range(2):
                        for q in range(2):
                            at = 32 * (2 * b + q)
                            last = nc.tensor.matmul(ps[at:at + 32, 6 + p % 2, :], ones32[:, 0:32], prob[:, (2 * p + b) % 4, q, :],
                                                    start=True, stop=True)
                    last.then_inc(s["sums"], 1)

                def gather(b):
                    if b == 0:
                        pe.wait_ge(s["X_sb"], one(1))
                    else:
                        pe.wait_ge(s["px_sb"], batch(b))
                    for q in range(2):
                        last = nc.tensor.matmul(ps[:, 4 + q, :], X[:, b, :], prob[:, b % 4, q, :], start=True, stop=True)
                    last.then_inc(s["px_ps"], 1)

                rough(0)
                for b in range(GB):
                    scores(b)
                    if b + 1 < GB:
                        rough(b + 1)
                    if b % 2 == 0 and b >= 2:
                        gather(b - 2)
                    if b % 2 == 1:
                        sums(b // 2)
                        if b >= 3:
                            gather(b - 2)

                def close(b):
                    gather(b)
                return close

            def finish(g, close):
                one, batch = Count(g, 1), Count(g, GB)
                close(GB - 2)
                close(GB - 1)
                pe.wait_ge(s["px_sb"], batch(GB))
                for h in range(H):
                    last = nc.tensor.matmul(ps[:, 6, :], N[:, h, :], px[:, h, :, :], start=(h == 0), stop=(h == H - 1))
                last.then_inc(s["y_ps"], 1)
                pe.wait_ge(s["yT_sb"], one(1))
                for t in range(T):
                    last = nc.tensor.transpose(ps[:, 7, t * P:(t + 1) * P], yT[:, t * P:(t + 1) * P], ident)
                last.then_inc(s["yt_ps"], 1)

            heads(0)
            keys_back(0)
            with pe.Fori(0, G - 1) as g:
                close = main(g)
                heads(g + 1)
                finish(g, close)
                keys_back(g + 1)
                pe.wait_ge(s["turn_done"], Count(g, 1)(1))
            finish(G - 1, main(G - 1))

        @block.scalar
        def _(act):
            def heads(g):
                one, head = Count(g, 1), Count(g, H)
                act.wait_ge(s["latT_ps"], one(1))
                nc.scalar.copy(XT[:, :, 1, :], ps[:, 0, :].rearrange("p (b s) -> p b s", s=S))
                nc.scalar.copy(XT[:, :, 0, :], ps[:, 1, :].rearrange("p (b s) -> p b s", s=S)).then_inc(s["XT_sb"], 1)
                for h in range(H):
                    act.wait_ge(s["th_ps"], head(h + 1))
                    nc.scalar.copy(th[:, :, h, :], ps[:, h % 4, :].rearrange("p (b s) -> p b s", s=S)).then_inc(s["th_sb"], 1)
                    if h == 0:
                        act.wait_ge(s["XT_sb"], one(1))
                        nc.scalar.copy(XT16[:, :, :], XT[:, :, :, :].rearrange("p b a s -> p b (a s)")).then_inc(s["XT16"], 1)

            def main(g):
                batch = Count(g, GB)
                for b in range(GB):
                    act.wait_ge(s["scores"], batch(b + 1))
                    if b >= 4:
                        act.wait_ge(s["px_ps"], batch(b - 3))
                    nc.scalar.activation(prob[:, b % 4, :, :], ps[:, 2:4, :], ACT.Exp,
                                         bias=bias_now[:, 0, b:b + 1]).then_inc(s["exped"], 1)

            def finish(g):
                act.wait_ge(s["y_ps"], Count(g, 1)(1))
                nc.scalar.copy(yT[:, :], ps[:, 6, :]).then_inc(s["yT_sb"], 1)

            heads(0)
            with act.Fori(0, G - 1) as g:
                main(g)
                heads(g + 1)
                finish(g)
                act.wait_ge(s["turn_done"], Count(g, 1)(1))
            main(G - 1)
            finish(G - 1)

        @block.vector
        def _(dve):
            def prepare(g, after):
                if after is not None:
                    dve.wait_ge(s["latT_ps"], after)
                dve.wait_ge(s["ctx_in"], 16 * g + 32)
                for t in range(T):
                    tile = g * T + t
                    nc.vector.tensor_scalar(lat[:, t, :], c["stream"][:, bass.ds(tile, 1), :], mom2[:, bass.ds(tile, 1), 0],
                                            rstd2[:, bass.ds(tile, 1)], ALU.subtract, ALU.mult)
                for t in range(T):
                    tile = g * T + t
                    last = nc.vector.tensor_scalar(cx[:, t, :], craw[:, t, :], momc[:, bass.ds(tile, 1), 0],
                                                   rstdc[:, bass.ds(tile, 1)], ALU.subtract, ALU.mult)
                last.then_inc(s["scaled"], 1)

            def heads(g):
                head = Count(g, H)
                for h in range(H):
                    dve.wait_ge(s["th_sb"], head(h + 1))
                    nc.vector.tensor_copy(th16[:, :, h, :], th[:, :, h, :]).then_inc(s["th16"], 1)

            def divide(g, b):
                batch = Count(g, GB)
                dve.wait_ge(s["px_ps"], batch(b + 1))
                dve.wait_ge(s["share"], Count(g, 2 * GB)(2 * b + 2))
                nc.vector.tensor_tensor(px[:, :, b, :], ps[:, 4:6, :].rearrange("p a (h s) -> p (a h) s", s=S),
                                        share[:, (b // 2) % 2, b % 2, :, :].rearrange("p a (h s) -> p (a h) s", s=S),
                                        ALU.mult).then_inc(s["px_sb"], 1)

            def main(g, prepare_next):
                one, batch, pair = Count(g, 1), Count(g, GB), Count(g, BP)

                def row_tops(b):
                    dve.wait_ge(s["rough"], batch(b + 1))
                    nc.vector.tensor_reduce(top[:, b % 2, :], ps[:, 0:2, :].rearrange("p a (j n) -> p (a j) n", n=P), AX.X, ALU.max,
                                            negate=True).then_inc(s["top"], 1)

                def invert(p):
                    dve.wait_ge(s["sums"], pair(p + 1))
                    if p >= 2:
                        dve.wait_ge(s["share"], Count(g, 2 * GB)(4 * p - 4))
                    nc.vector.reciprocal(recip[:, p % 2, :], ps[:, 6 + p % 2, :]).then_inc(s["recip"], 1)

                row_tops(0)
                dve.wait_ge(s["X_ps"], one(1))
                nc.vector.tensor_copy(X[:, :, :], ps[:, 4:6, :].rearrange("p a (b d) -> p (a b) d", d=P)).then_inc(s["X_sb"], 1)
                row_tops(1)
                for b in range(GB):
                    if b + 2 < GB:
                        row_tops(b + 2)
                    if b % 2 == 0 and b >= 2:
                        divide(g, b - 2)
                    if b % 2 == 1:
                        invert(b // 2)
                        if b >= 3:
                            divide(g, b - 2)
                    if b == 1 and prepare_next:
                        prepare(g + 1, one(1))

            def finish(g):
                step = Chain(dve, s["steps"], g, STEPS)
                divide(g, GB - 2)
                divide(g, GB - 1)
                for t in range(T):
                    if t == 0:
                        dve.wait_ge(s["yt_ps"], Count(g, 1)(1))
                    residual_step(nc, c, norm, step, g * T + t, t, ps[:, 7, t * P:(t + 1) * P],
                                  c["stream"][:, bass.ds(g * T + t, 1), :]).then_inc(s["tile_done"], 1)
                dve.wait_ge(s["tile_done"], Count(g, T)(T))
                assert step.n == STEPS, step.n
                keep_moments(nc, c, norm, g).then_inc(s["turn_done"], 1)

            prepare(0, None)
            nc.vector.tensor_scalar(bias_now[:, 0, :], bias[:, 0:GB], 1.0, None, ALU.mult)
            heads(0)
            with dve.Fori(0, G - 1) as g:
                main(g, True)
                dve.wait_ge(s["exped"], Count(g, GB)(GB))
                nc.vector.tensor_scalar(bias_now[:, 0, :], bias[:, bass.ds((g + 1) * GB, GB)], 1.0, None, ALU.mult)
                heads(g + 1)
                finish(g)
                dve.wait_ge(s["turn_done"], Count(g, 1)(1))
            main(G - 1, False)
            finish(G - 1)

        @block.gpsimd
        def _(pool):
            wide = lambda a: a.unsqueeze(1).to_broadcast([P, T, P])

            def prepare(g):
                prep = Chain(pool, s["pool_steps"], g, 3)
                pool.wait_ge(s["scaled"], Count(g, 1)(1))
                nc.gpsimd.tensor_tensor(gx[:, 0, :, :], lat[:, :, :], wide(w("l_g2")), ALU.mult)
                prep(nc.gpsimd.tensor_tensor(gx[:, 1, :, :], cx[:, :, :], wide(w("l_g1")), ALU.mult))
                nc.gpsimd.tensor_tensor(lat[:, :, :], gx[:, 0, :, :], wide(w("l_b2")), ALU.add)
                prep(nc.gpsimd.tensor_tensor(cx[:, :, :], gx[:, 1, :, :], wide(w("l_b1")), ALU.add))
                group = lambda a: a[:, bass.ds(g * T, T)].unsqueeze(2).to_broadcast([P, T, P])
                nc.gpsimd.tensor_tensor(gx[:, 0, :, :], cx[:, :, :], group(keep), ALU.mult)
                prep(nc.gpsimd.tensor_tensor(gx[:, 1, :, :], lat[:, :, :], group(drop), ALU.mult))
                nc.gpsimd.tensor_tensor(cx[:, :, :], gx[:, 0, :, :], gx[:, 1, :, :], ALU.add).then_inc(s["staged"], 1)

            def main(g, prepare_next):
                batch, pair = Count(g, GB), Count(g, BP)

                def spread(p):
                    pool.wait_ge(s["recip"], pair(p + 1))
                    if p >= 2:
                        pool.wait_ge(s["px_sb"], batch(2 * p - 2))
                    pool.sem_inc(s["taken"], 1)
                    for b in range(2):
                        for q in range(2):
                            at = 32 * (2 * b + q)
                            nc.gpsimd.partition_broadcast(share[:, p % 2, b, q, :], recip[at:at + 1, p % 2, :], P
                                                          ).then_inc(s["share"], 1)
                            pool.wait_ge(s["share"], Count(g, 2 * GB)(4 * p + 2 * b + q + 1))
                            pool.sem_inc(s["taken"], 1)

                for b in range(GB):
                    pool.wait_ge(s["top"], batch(b + 1))
                    if b >= 1:
                        pool.wait_ge(s["scores"], batch(b))
                    nc.gpsimd.tensor_tensor(diag[:, :, :], ident16[:, :].unsqueeze(1).to_broadcast([P, PAIRS, P]),
                                            top[:, b % 2, :].unsqueeze(2).to_broadcast([P, PAIRS, P]), ALU.mult).then_inc(s["diag"], 1)
                    if b % 2 == 0 and b >= 2:
                        spread(b // 2 - 1)
                    if b == 3 and prepare_next:
                        prepare(g + 1)
                spread(BP - 1)

            prepare(0)
            with pool.Fori(0, G - 1) as g:
                main(g, True)
                pool.wait_ge(s["turn_done"], Count(g, 1)(1))
            main(G - 1, False)


def bitlinear_phase(nc, ctx, c, name):
    sb = lambda n, shape, dt=F32: ctx.enter_context(nc.sbuf_tensor(f"{name}_{n}", shape, dt))
    s = {n: c["sem"](f"{name}_{n}") for n in (
        "mags mag_ps quant ws_ready staged ss1 root1 x_ready x_ps x_sb h_ps r_sb h_sb g_sb ss2 root2 q_ready q_ps q_sb y_ps "
        "tile_done turn_done steps wsteps taken out1").split()}
    w, ps = c["w"], c["psum"]
    HID = 512
    HC = HID // P
    MAGIC = 1.5 * 2.0 ** 23
    EPS_NORM, EPS_Q = 1e-8, 1e-5
    xs, norm = sb("xs", [P, T, P]), Norm(sb)
    wq, wtmp = sb("wq", [P, 2, HID], BF16), sb("wtmp", [P, 2, HID])
    mags, wmean, wscale, ones = sb("mags", [P, 2]), sb("wmean", [P, 2]), sb("wscale", [P, 2]), sb("ones", [P, P])
    sq, ss1, ss2 = sb("sq", [P, T, HID]), sb("ss1", [P, T]), sb("ss2", [P, T])
    xn, amax, xscale, deq = sb("xn", [P, T, P]), sb("amax", [P, T]), sb("xscale", [P, T]), sb("deq", [P, T])
    xi, xiT = sb("xi", [P, T, P], BF16), sb("xiT", [P, T * P], BF16)
    r, hh, hn = sb("r", [P, T, HID]), sb("hh", [P, T, HID]), sb("hn", [P, T, HID])
    amax2, hscale, deq2 = sb("amax2", [P, T]), sb("hscale", [P, T]), sb("deq2", [P, T])
    hi, hiT = sb("hi", [P, T, HID], BF16), sb("hiT", [P, 2, HID], BF16)
    eps = sb("eps", [P, 1])
    raw = [w("b_w1"), w("b_w2")]
    EARLY, STEPS = 4, 2 * (3 + 6) + 3 * T

    def quantise(link, values, out, scales, deqs, biggest, width, weight_mean):
        wide = lambda a: a.unsqueeze(2).to_broadcast([P, T, width])
        link(nc.vector.tensor_reduce(biggest[:, :], values, AX.X, ALU.max, apply_absolute_value=True))
        link(nc.vector.tensor_scalar(biggest[:, :], biggest[:, :], EPS_Q, None, ALU.max))
        link(nc.vector.reciprocal(scales[:, :], biggest[:, :]))
        nc.vector.tensor_scalar(deqs[:, :], biggest[:, :], 1.0 / 127.0, weight_mean, ALU.mult, ALU.mult)
        link(nc.vector.tensor_scalar(scales[:, :], scales[:, :], 127.0, None, ALU.mult))
        link(nc.vector.tensor_tensor(values, values, wide(scales[:, :]), ALU.mult))
        link(nc.vector.tensor_scalar(values, values, -128.0, 127.0, ALU.max, ALU.min))
        return nc.vector.tensor_scalar(out, values, MAGIC, MAGIC, ALU.add, ALU.subtract)

    with nc.Block() as block:
        def down(pe, per_tile, t):
            pe.wait_ge(s["q_sb"], per_tile(t + 1))
            for n in range(HC):
                last = nc.tensor.matmul(ps[:, 7, t * P:(t + 1) * P], hiT[:, t % 2, n * P:(n + 1) * P], wq[:, 1, n * P:(n + 1) * P],
                                        start=(n == 0), stop=(n == HC - 1))
            if t == T - 1:
                last.then_inc(s["y_ps"], 1)

        @block.tensor
        def _(pe):
            pe.wait_ge(s["mags"], 1)
            nc.tensor.matmul(ps[:, 0, 0:2], ones[:, :], mags[:, :], start=True, stop=True).then_inc(s["mag_ps"], 1)
            pe.wait_ge(s["quant"], 1)
            with pe.Fori(0, G) as i:
                one, per_tile = Count(i, 1), Count(i, T)
                pe.wait_ge(s["x_ready"], one(1))
                for t in range(T):
                    last = nc.tensor.matmul(ps[:, 0, t * P:(t + 1) * P], xi[:, t, :], c["ident16"][:, :], start=True, stop=True)
                last.then_inc(s["x_ps"], 1)
                pe.wait_ge(s["x_sb"], one(1))
                for t in range(T):
                    nc.tensor.matmul(ps[:, 1 + t, :], xiT[:, t * P:(t + 1) * P], wq[:, 0, :], start=True, stop=True
                                     ).then_inc(s["h_ps"], 1)
                pe.wait_ge(s["q_ready"], one(1))
                for t in range(T):
                    if t >= 2:
                        pe.wait_ge(s["q_sb"], per_tile(t - 1))
                    for n in range(HC):
                        last = nc.tensor.matmul(ps[:, 5 + t % 2, n * P:(n + 1) * P], hi[:, t, n * P:(n + 1) * P], c["ident16"][:, :],
                                                start=True, stop=True)
                    last.then_inc(s["q_ps"], 1)
                    if t >= 1:
                        down(pe, per_tile, t - 1)
                down(pe, per_tile, T - 1)
                pe.wait_ge(s["turn_done"], one(1))

        @block.scalar
        def _(act):
            with act.Fori(0, G) as i:
                one, per_tile = Count(i, 1), Count(i, T)
                act.wait_ge(s["staged"], one(1))
                for t in range(T):
                    last = nc.scalar.activation(sq[:, t, 0:P], xs[:, t, :], ACT.Square, accum_out=ss1[:, t:t + 1])
                last.then_inc(s["ss1"], 1)
                act.wait_ge(s["ss1"], one(1))
                nc.scalar.activation(ss1[:, :], ss1[:, :], ACT.Sqrt, bias=eps[:, :], scale=1.0 / P).then_inc(s["root1"], 1)
                act.wait_ge(s["x_ps"], one(1))
                nc.scalar.copy(xiT[:, :], ps[:, 0, :]).then_inc(s["x_sb"], 1)
                for t in range(T):
                    act.wait_ge(s["h_ps"], per_tile(t + 1))
                    nc.scalar.activation(r[:, t, :], ps[:, 1 + t, :], ACT.Relu, scale=deq[:, t:t + 1]).then_inc(s["r_sb"], 1)
                for t in range(T):
                    act.wait_ge(s["r_sb"], per_tile(t + 1))
                    nc.scalar.activation(r[:, t, :], r[:, t, :], ACT.Square).then_inc(s["h_sb"], 1)
                act.wait_ge(s["root1"], one(1))
                for t in range(T):
                    act.wait_ge(s["g_sb"], per_tile(t + 1))
                    last = nc.scalar.activation(sq[:, t, :], hh[:, t, :], ACT.Square, accum_out=ss2[:, t:t + 1])
                last.then_inc(s["ss2"], 1)
                act.wait_ge(s["ss2"], one(1))
                nc.scalar.activation(ss2[:, :], ss2[:, :], ACT.Sqrt, bias=eps[:, :], scale=1.0 / HID).then_inc(s["root2"], 1)
                for t in range(T):
                    act.wait_ge(s["q_ps"], per_tile(t + 1))
                    nc.scalar.copy(hiT[:, t % 2, :], ps[:, 5 + t % 2, :]).then_inc(s["q_sb"], 1)
                act.wait_ge(s["turn_done"], one(1))

        @block.vector
        def _(dve):
            early = Chain(dve, s["wsteps"], 0, EARLY)
            nc.vector.memset(ones[:, :], 1.0)
            nc.vector.memset(eps[:, :], EPS_NORM)
            for n in range(2):
                last = nc.vector.tensor_reduce(mags[:, n:n + 1], raw[n], AX.X, ALU.add, apply_absolute_value=True)
            last.then_inc(s["mags"], 1)
            dve.wait_ge(s["mag_ps"], 1)
            early(nc.vector.tensor_scalar(wmean[:, :], ps[:, 0, 0:2], 1.0 / (P * HID), EPS_Q, ALU.mult, ALU.max))
            early(nc.vector.reciprocal(wscale[:, :], wmean[:, :]))
            for n in range(2):
                last = nc.vector.tensor_scalar(wtmp[:, n, :], raw[n], wscale[:, n:n + 1], None, ALU.mult)
            early(last)
            early(nc.vector.tensor_scalar(wtmp[:, :, :], wtmp[:, :, :], MAGIC, MAGIC, ALU.add, ALU.subtract))
            nc.vector.tensor_scalar(wq[:, :, :], wtmp[:, :, :], -1.0, 1.0, ALU.max, ALU.min).then_inc(s["quant"], 1)
            dve.wait_ge(s["quant"], 1)
            with dve.Fori(0, G) as i:
                one, per_tile = Count(i, 1), Count(i, T)
                step = Chain(dve, s["steps"], i, STEPS)
                wide = lambda a, n: a.unsqueeze(2).to_broadcast([P, T, n])
                stage_tiles(nc, c, xs, i).then_inc(s["staged"], 1)
                dve.wait_ge(s["root1"], one(1))
                step(nc.vector.reciprocal(ss1[:, :], ss1[:, :]))
                step(nc.vector.tensor_tensor(xn[:, :, :], xs[:, :, :], wide(ss1[:, :], P), ALU.mult))
                step(nc.vector.tensor_tensor(xn[:, :, :], xn[:, :, :], w("b_n1").unsqueeze(1).to_broadcast([P, T, P]), ALU.mult))
                quantise(step, xn[:, :, :], xi[:, :, :], xscale, deq, amax, P, wmean[:, 0:1]).then_inc(s["x_ready"], 1)
                for t in range(T):
                    dve.wait_ge(s["h_sb"], per_tile(t + 1))
                    nc.vector.tensor_scalar(hh[:, t, :], r[:, t, :], w("b_as"), w("b_ab"), ALU.mult, ALU.add).then_inc(s["g_sb"], 1)
                dve.wait_ge(s["root2"], one(1))
                step(nc.vector.reciprocal(ss2[:, :], ss2[:, :]))
                step(nc.vector.tensor_tensor(hn[:, :, :], hh[:, :, :], wide(ss2[:, :], HID), ALU.mult))
                step(nc.vector.tensor_tensor(hn[:, :, :], hn[:, :, :], w("b_n2").unsqueeze(1).to_broadcast([P, T, HID]), ALU.mult))
                quantise(step, hn[:, :, :], hi[:, :, :], hscale, deq2, amax2, HID, wmean[:, 1:2]).then_inc(s["q_ready"], 1)
                dve.wait_ge(s["y_ps"], one(1))
                for t in range(T):
                    step(nc.vector.tensor_scalar(xn[:, t, :], ps[:, 7, t * P:(t + 1) * P], deq2[:, t:t + 1], None, ALU.mult))
                    residual_step(nc, c, norm, step, i * T + t, t, xn[:, t, :], xs[:, t, :]).then_inc(s["tile_done"], 1)
                dve.wait_ge(s["tile_done"], per_tile(T))
                assert step.n == STEPS, step.n
                keep_moments(nc, c, norm, i).then_inc(s["turn_done"], 1)
                dve.wait_ge(s["turn_done"], one(1))


def norm_phase(nc, ctx, c, name):
    var_ready = c["sem"](f"{name}_var_ready")
    root_ready = c["sem"](f"{name}_root_ready")
    rstd = c["rstd"]
    with nc.Block() as block:
        @block.vector
        def _(dve):
            nc.vector.tensor_scalar(rstd[:, :], c["moments"][:, :, 1], LN_EPS, None, ALU.add).then_inc(var_ready, 1)
            dve.wait_ge(root_ready, 1)
            nc.vector.reciprocal(rstd[:, :], rstd[:, :])

        @block.scalar
        def _(act):
            act.wait_ge(var_ready, 1)
            nc.scalar.activation(rstd[:, :], rstd[:, :], ACT.Sqrt).then_inc(root_ready, 1)


def output_phase(nc, ctx, c, out):
    normed = c["sem"]("normed")
    stored = c["sem"]("stored")
    y = ctx.enter_context(nc.sbuf_tensor("y_out", [P, NT, P], F32))
    out = out.rearrange("(n k) s d -> (k s) n d", k=2)
    with nc.Block() as block:
        @block.vector
        def _(dve):
            with dve.Fori(0, NT) as i:
                nc.vector.tensor_scalar(y[:, bass.ds(i, 1), :], c["stream"][:, bass.ds(i, 1), :], c["moments"][:, bass.ds(i, 1), 0],
                                        c["rstd"][:, bass.ds(i, 1)], ALU.subtract, ALU.mult).then_inc(normed, 1)

        @block.sync
        def _(sp):
            with sp.Fori(0, G) as i:
                sp.wait_ge(normed, i * T + T)
                sp.dma_start(out[:, bass.ds(i * T, T), :], y[:, bass.ds(i * T, T), :]).then_inc(stored, 16)
            sp.wait_ge(stored, 16 * G)


def build(nc, ins, out, upto=6, start=0):
    where_w, n_w = columns(WEIGHTS)
    n_early = where_w["l_g1"][0]
    where_c, n_c = columns(CONST)
    with ExitStack() as ctx:
        sb = lambda n, shape, dt=F32: ctx.enter_context(nc.sbuf_tensor(n, shape, dt))
        late, const = sb("late_weights", [P, n_w - n_early]), sb("const", [P, n_c])

        def weight(n):
            lo, hi = where_w[n]
            return early[:, lo:hi] if hi <= n_early else late[:, lo - n_early:hi - n_early]

        taken = []

        def semaphore(n):
            taken.append(nc.alloc_semaphore(name=n))
            return taken[-1]

        def phase_end():
            nc.clear_and_free_semaphores(taken)
            nc.all_engine_barrier()
            taken.clear()

        c = {
            "sem": semaphore,
            "w": weight, "const": lambda n: const[:, slice(*where_c[n])],
            "stream": sb("stream", [P, NT, P]), "moments": sb("moments", [P, NT, 2]), "rstd": sb("rstd", [P, NT]),
            "bq_scaled": sb("bq_scaled", [P, 1]), "ident16": sb("ident16", [P, P], BF16),
            "psum": ctx.enter_context(nc.psum_tensor("psum", [P, 8, 512], F32)),
            "l_mats": ins["l_mats"], "mask": ins["mask"],
            "ctx": ins["ctx"].rearrange("(n k) s d -> (k s) n d", k=2),
        }
        loaded = ctx.enter_context(nc.semaphore("loaded"))
        early_room = ExitStack()
        early = early_room.enter_context(nc.sbuf_tensor("early_weights", [P, n_early], F32))
        c["relbias"] = early_room.enter_context(nc.sbuf_tensor("relbias", [P, H, S], F32))
        with nc.Block() as block:
            @block.sync
            def _(sp):
                sp.dma_start(early[:, :], ins["weights"][:, 0:n_early]).then_inc(loaded, 16)
                sp.dma_start(late[:, :], ins["weights"][:, n_early:n_w]).then_inc(loaded, 16)
                sp.dma_start(c["stream"][:, :, :], ins["x"].rearrange("(n k) s d -> (k s) n d", k=2)).then_inc(loaded, 16)

            @block.scalar
            def _(act):
                act.dma_start(const[:, :], ins["const"]).then_inc(loaded, 16)
                act.dma_start(c["relbias"][:, :, :], ins["relbias"]).then_inc(loaded, 16)
                act.wait_ge(loaded, 80)
                nc.scalar.copy(c["ident16"][:, :], c["const"]("ident"))
                nc.scalar.mul(c["bq_scaled"][:, :], c["w"]("a_bq"), float(DH) ** -0.5)

            @block.vector
            def _(dve):
                nc.vector.memset(c["moments"][:, :, :], 0.0)
                nc.vector.memset(c["rstd"][:, :], 1.0)

        phases = [lambda x: attention_phase(nc, x, c, "a", False), lambda x: attention_phase(nc, x, c, "c", True),
                  lambda x: experts_phase(nc, x, c, "e"), lambda x: fourier_phase(nc, x, c, "f"),
                  lambda x: latents_phase(nc, x, c, "l"), lambda x: bitlinear_phase(nc, x, c, "b")]
        for n, phase in enumerate(phases[:upto]):
            if n == 4:
                early_room.close()
            if n < start:
                continue
            with ExitStack() as own:
                phase(own)
                norm_phase(nc, own, c, f"n{n}")
                phase_end()
        with ExitStack() as own:
            output_phase(nc, own, c, out)


def laid_out(inp):
    f = {k: np.asarray(v) for k, v in inp.items()}
    col = lambda v: np.reshape(v, (-1, 1))
    rows = lambda v: np.broadcast_to(np.reshape(v, (1, -1)), (P, np.size(v)))
    turned = lambda wt: wt.reshape(H, 2, DH // 2, P)[:, ::-1].reshape(P, P).T
    w = {
        "a_wq": f["L0_attn_Wq"].T, "a_wk": f["L0_attn_Wk"].T, "a_wv": f["L0_attn_Wv"].T, "a_wo": f["L0_attn_Wo"].T,
        "a_bq": col(f["L0_attn_bq"]), "a_bk": col(f["L0_attn_bk"]), "a_bv": rows(f["L0_attn_bv"]), "a_bo": rows(f["L0_attn_bo"]),
        "c_wq": f["L0_xattn_Wq"].T, "c_wqr": turned(f["L0_xattn_Wq"]), "c_wk": f["L0_xattn_Wk"].T,
        "c_wkr": turned(f["L0_xattn_Wk"]), "c_wv": f["L0_xattn_Wv"].T, "c_wo": f["L0_xattn_Wo"].T,
    }
    w["e_wr"] = f["L0_ffn_Wr"]
    w["e_w1"] = np.concatenate([np.moveaxis(f["L0_ffn_W1"], 0, 1).reshape(P, 512), f["L0_ffn_Ws1"]], 1)
    w2 = np.concatenate([f["L0_ffn_W2"].reshape(512, P), f["L0_ffn_Ws2"], np.zeros((64, P), np.float32)])
    w["e_w2"] = np.moveaxis(w2.reshape(5, P, P), 0, 1).reshape(P, 640)
    w["f_wq"], w["f_wk"], w["f_wv"] = f["L1_attn_Wq"].T, f["L1_attn_Wk"].T, f["L1_attn_Wv"].T
    w["f_bq"], w["f_bk"], w["f_bv"] = col(f["L1_attn_bq"]), col(f["L1_attn_bk"]), rows(f["L1_attn_bv"])
    w["f_proj"] = np.tile(f["L1_attn_proj_mat"], (H, 1))
    wo = np.zeros((2, 4, 4, 4, DH, P), np.float32)
    for par in range(2):
        wo[par, :, :, par] = f["L1_attn_Wo"].T.reshape(4, 4, DH, P)
    w["f_wo"] = np.moveaxis(wo.reshape(8, P, P), 0, 1).reshape(P, 1024)
    w["f_bo"] = col(f["L1_attn_bo"])
    for n in ("g1", "b1", "g2", "b2"):
        w[f"l_{n}"] = rows(f[f"L1_xattn_{n}"])
    w["b_w1"] = f["L1_ffn_w1"].T
    w["b_w2"] = np.moveaxis(f["L1_ffn_w2"].T.reshape(4, P, P), 0, 1).reshape(P, 512)
    w["b_n1"], w["b_n2"] = rows(f["L1_ffn_norm1_w"]), rows(f["L1_ffn_norm2_w"])
    w["b_as"], w["b_ab"] = rows(f["L1_ffn_act_scale"]), rows(f["L1_ffn_act_bias"])
    assert list(w) == list(WEIGHTS)
    by_pair = lambda a: np.moveaxis(a.reshape(PAIRS, P, P), 0, 1)
    kv = f["L1_xattn_Wkv"].T
    mats = np.stack([by_pair(f["L1_xattn_Wq"].T), by_pair(kv[:1024]), by_pair(kv[1024:]), by_pair(f["L1_xattn_Wout"])], 1)
    m = f["mask_BxS2_bk0"]
    mask = np.concatenate([m.reshape(NT, P).T, np.concatenate([m.T, np.ones((S, B), bool)])], 1)
    d = np.arange(P) % DH
    angle = np.outer(1.0 / 10000.0 ** (2 * (d % (DH // 2)) / DH), np.arange(S))
    t = {
        "ident": np.eye(P), "headmask": np.arange(P)[:, None] // DH == np.arange(H), "cos": np.cos(angle),
        "sin": np.where(d[:, None] < DH // 2, -np.sin(angle), np.sin(angle)),
    }
    q, kk = np.arange(P)[:, None] % S, np.arange(S)[None, :]
    return {
        "x": f["x"], "ctx": f["ctx_1024"],
        "weights": np.ascontiguousarray(np.concatenate([w[n] for n in WEIGHTS], 1)),
        "l_mats": np.ascontiguousarray(mats), "mask": np.ascontiguousarray(mask),
        "const": np.concatenate([np.asarray(t[n], np.float32) for n in CONST], 1),
        "relbias": np.ascontiguousarray(np.moveaxis(f["L0_attn_rel_bias"][:, np.clip(q - kk, -128, 128) + 128], 0, 1)),
    }


def kernel(**inputs):
    import concourse.bacc as bacc
    from concourse.bass_utils import run_bass_kernel_spmd

    nc = bacc.Bacc("TRN2", target_bir_lowering=False, num_devices=1)
    arrays = laid_out(inputs)
    ins = {n: nc.dram_tensor(f"in_{n}", a.shape, mybir.dt.from_np(a.dtype), kind="ExternalInput").ap() for n, a in arrays.items()}
    out = nc.dram_tensor("out", (B, S, P), F32, kind="ExternalOutput").ap()
    build(nc, ins, out)
    return run_bass_kernel_spmd(nc, [{f"in_{n}": a for n, a in arrays.items()}], core_ids=[0]).results[0]["out"]
```

```python
from contextlib import ExitStack

import numpy as np

import concourse.bass as bass
from concourse import mybir

F32 = mybir.dt.float32
BF16 = mybir.dt.bfloat16
I32 = mybir.dt.int32
ALU = mybir.AluOpType
ACT = mybir.ActivationFunctionType
AX = mybir.AxisListType

P = 128
S = 64
B = 64
H = 16
DH = 8
NT = B * S // P
T = 4
G = NT // T
GB = 2 * T
PAIRS = H // 2
VW = 2 * DH + 2
LN_EPS = 1e-5

CONST = {"ident": P, "headmask": H, "cos": S, "sin": S}
WEIGHTS = {
    "a_wq": P, "a_wk": P, "a_wv": P, "a_wo": P, "a_bq": 1, "a_bk": 1, "a_bv": P, "a_bo": P,
    "c_wq": P, "c_wqr": P, "c_wk": P, "c_wkr": P, "c_wv": P, "c_wo": P,
    "e_wr": 8, "e_w1": 576, "e_w2": 640,
    "f_wq": P, "f_wk": P, "f_wv": P, "f_bq": 1, "f_bk": 1, "f_bv": P, "f_proj": P, "f_wo": 1024, "f_bo": 1,
    "l_g1": P, "l_b1": P, "l_g2": P, "l_b2": P,
    "b_w1": 512, "b_w2": 512, "b_n1": P, "b_n2": 512, "b_as": 1, "b_ab": 1,
}


def columns(widths):
    at, where = 0, {}
    for name, width in widths.items():
        where[name] = (at, at + width)
        at += width
    return where, at


class Count:

    def __init__(self, i, per):
        self.i, self.per = i, per

    def __call__(self, n):
        assert 1 <= n <= self.per
        return self.i * self.per + n


class Chain:

    def __init__(self, eng, sem, i, per):
        self.eng, self.sem, self.at, self.n = eng, sem, Count(i, per), 0

    def __call__(self, ins):
        self.n += 1
        ins.then_inc(self.sem, 1)
        self.eng.wait_ge(self.sem, self.at(self.n))


class Norm:

    def __init__(self, sb):
        self.sums, self.stats, self.moments = sb("sums", [P, T, P]), sb("stats", [P, T, 6]), sb("mom", [P, T, 2])


def residual_step(nc, c, norm, step, tile, t, branch, x):
    step(nc.vector.tensor_tensor(norm.sums[:, t, :], branch, x, ALU.add))
    step(nc.vector.bn_stats(norm.stats[:, t, :], norm.sums[:, t, :]))
    nc.vector.tensor_scalar(c["stream"][:, bass.ds(tile, 1), :], norm.sums[:, t, :], 1.0, None, ALU.mult)
    return nc.vector.bn_aggr(norm.moments[:, t, :], norm.stats[:, t, :])


def residual_group(nc, c, norm, step, i, branch, x):
    step(nc.vector.tensor_tensor(norm.sums[:, :, :], branch, x, ALU.add))
    for t in range(T):
        last = nc.vector.bn_stats(norm.stats[:, t, :], norm.sums[:, t, :])
    step(last)
    nc.vector.tensor_scalar(c["stream"][:, bass.ds(i * T, T), :], norm.sums[:, :, :], 1.0, None, ALU.mult)
    for t in range(T):
        last = nc.vector.bn_aggr(norm.moments[:, t, :], norm.stats[:, t, :])
    step(last)
    return keep_moments(nc, c, norm, i)


def keep_moments(nc, c, norm, i):
    return nc.vector.tensor_scalar(c["moments"][:, bass.ds(i * T, T), :], norm.moments[:, :, :], 1.0, None, ALU.mult)


def attention_phase(nc, ctx, c, name, cross):
    sb = lambda n, shape, dt=F32: ctx.enter_context(nc.sbuf_tensor(f"{name}_{n}", shape, dt))
    sem = lambda n: c["sem"](f"{name}_{n}")
    w = c["w"]
    k = c["const"]
    stream, moments, rstd, ps = c["stream"], c["moments"], c["rstd"], c["psum"]
    pre = "c_" if cross else "a_"
    scale = float(DH) ** -0.5

    xs = sb("xs", [P, T, P])
    xT = sb("xT", [P, T * P])
    QT = sb("QT", [P, T * P])
    KT = sb("KT", [P, T * P])
    KX = sb("KX", [P, 2, 2, H, S])
    V2 = sb("V2", [P, GB, PAIRS, VW])
    prob = sb("prob", [P, 2, H, S])
    probT = sb("probT", [P, 2, PAIRS, P])
    top = sb("top", [P, 2, H])
    inv = sb("inv", [P, 2, H])
    ao = sb("ao", [P, 2, P])
    aoT = sb("aoT", [P, 2, P])
    norm = Norm(sb)
    if cross:
        cs = sb("cs", [P, T, P])
        cT = sb("cT", [P, T * P])
        ropes = sb("ropes", [P, 4, T * P])

    names = ("staged xT_ps xT_sb proj_ps proj_sb v_ps v_sb kx scores softening shifted exped pT_ps pT_sb pv_ps inverse "
             "ao_ready aoT_ps aoT_sb out_ps steps v_zero v_ones").split()
    s = {n: sem(n) for n in names + ("ctx_in cT_sb cT_ps roped".split() if cross else [])}
    SOFTENING = 1 if cross else 2

    with nc.Block() as block:
        if cross:
            @block.sync
            def _(sp):
                sp.dma_start(cs[:, :, :], c["ctx"][:, 0:T, :]).then_inc(s["ctx_in"], 16)
                with sp.Fori(1, G) as i:
                    sp.wait_ge(s["cT_ps"], i)
                    sp.dma_start(cs[:, :, :], c["ctx"][:, bass.ds(i * T, T), :]).then_inc(s["ctx_in"], 16)

        @block.tensor
        def _(pe):
            def columns_of(g):
                pe.wait_ge(s["staged"], Count(g, 1)(1))
                for t in range(T):
                    last = nc.tensor.transpose(ps[:, 0, t * P:(t + 1) * P], xs[:, t, :], k("ident"))
                last.then_inc(s["xT_ps"], 1)
                if cross:
                    pe.wait_ge(s["ctx_in"], Count(g, 16)(16))
                    for t in range(T):
                        last = nc.tensor.transpose(ps[:, 1, t * P:(t + 1) * P], cs[:, t, :], k("ident"))
                    last.then_inc(s["cT_ps"], 1)

            def project_in(g):
                pe.wait_ge(s["xT_sb"], Count(g, 1)(1))
                if cross:
                    pe.wait_ge(s["cT_sb"], Count(g, 1)(1))
                    for bank, (weight, columns) in enumerate((("c_wq", xT), ("c_wqr", xT), ("c_wk", cT), ("c_wkr", cT))):
                        last = nc.tensor.matmul(ps[:, bank, :], w(weight), columns[:, :], start=True, stop=True)
                else:
                    nc.tensor.matmul(ps[:, 1, :], w("a_wq"), xT[:, :], start=True, stop=True)
                    last = nc.tensor.matmul(ps[:, 0, :], w("a_wk"), xT[:, :], start=True, stop=True)
                last.then_inc(s["proj_ps"], 1)

            def values(g):
                if cross:
                    pe.wait_ge(s["roped"], Count(g, 1)(1))
                for b in range(GB):
                    for par in range(2):
                        last = nc.tensor.matmul(ps[par * S:(par + 1) * S, 2 + b // 4, (b % 4) * P:(b % 4 + 1) * P],
                                                (cT if cross else xT)[:, b * S:(b + 1) * S], w(pre + "wv"), start=True, stop=True)
                last.then_inc(s["v_ps"], 1)

            def scores(g, t):
                tile = Count(g, T)
                pe.wait_ge(s["kx"], tile(t + 1))
                if t == 0:
                    pe.wait_ge(s["proj_sb"], Count(g, 2)(2))
                elif t == 1:
                    pe.wait_ge(s["v_sb"], Count(g, 1)(1))
                else:
                    pe.wait_ge(s["shifted"], tile(t - 1))
                for half in range(2):
                    for b in range(2):
                        last = nc.tensor.matmul(
                            ps[b * S:(b + 1) * S, 2 * (t % 2) + half, :], QT[:, t * P + b * S:t * P + (b + 1) * S],
                            KX[:, t % 2, b, half * 8:half * 8 + 8, :], start=True, stop=True)
                last.then_inc(s["scores"], 1)

            def turn_probs(g, t):
                pe.wait_ge(s["exped"], Count(g, T)(t + 1))
                if t >= 1:
                    pe.wait_ge(s["pT_sb"], Count(g, T)(t))
                for j in range(PAIRS):
                    last = nc.tensor.transpose(ps[:, 4 + j // 4, (j % 4) * P:(j % 4 + 1) * P],
                                               prob[:, t % 2, 2 * j:2 * j + 2, :], k("ident"))
                last.then_inc(s["pT_ps"], 1)

            def turn_out(g, t):
                pe.wait_ge(s["ao_ready"], Count(g, T)(t + 1))
                nc.tensor.transpose(ps[:, 6, 256:256 + P], ao[:, t % 2, :], k("ident")).then_inc(s["aoT_ps"], 1)

            def project_out(g, t):
                pe.wait_ge(s["aoT_sb"], Count(g, T)(t + 1))
                last = nc.tensor.matmul(ps[:, 7, t * P:(t + 1) * P], aoT[:, t % 2, :], w(pre + "wo"), start=True, stop=True)
                if t == T - 1:
                    last.then_inc(s["out_ps"], 1)

            def weigh(g, t):
                pe.wait_ge(s["pT_sb"], Count(g, T)(t + 1))
                for j in range(PAIRS):
                    for b in range(2):
                        last = nc.tensor.matmul(ps[b * S:(b + 1) * S, 6, j * VW:(j + 1) * VW],
                                                probT[:, t % 2, j, b * S:(b + 1) * S],
                                                V2[:, 2 * t + b, j, :], start=True, stop=True)
                last.then_inc(s["pv_ps"], 1)

            def main(g, ahead):
                for t in range(T):
                    if t + 1 < T:
                        scores(g, t + 1)
                    if t == T - 1 and ahead:
                        pe.wait_ge(s["shifted"], Count(g, T)(T - 1))
                        columns_of(g + 1)
                    turn_probs(g, t)
                    if t == T - 1 and ahead:
                        project_in(g + 1)
                    if t >= 1:
                        turn_out(g, t - 1)
                    if t == T - 1 and ahead and not cross:
                        values(g + 1)
                    if t >= 1:
                        project_out(g, t - 1)
                    weigh(g, t)
                if ahead and cross:
                    values(g + 1)
                turn_out(g, T - 1)
                project_out(g, T - 1)
                if ahead:
                    scores(g + 1, 0)

            pe.wait_ge(s["v_ones"], 1)
            columns_of(0)
            project_in(0)
            values(0)
            scores(0, 0)
            with pe.Fori(0, G - 1) as g:
                main(g, True)
            main(G - 1, False)

        @block.scalar
        def _(act):
            def columns_of(g):
                act.wait_ge(s["xT_ps"], Count(g, 1)(1))
                nc.scalar.copy(xT[:, :], ps[:, 0, :]).then_inc(s["xT_sb"], 1)
                if cross:
                    act.wait_ge(s["cT_ps"], Count(g, 1)(1))
                    nc.scalar.copy(cT[:, :], ps[:, 1, :]).then_inc(s["cT_sb"], 1)

            def project_in(g):
                if not cross:
                    act.wait_ge(s["proj_ps"], Count(g, 1)(1))
                    nc.scalar.activation(KT[:, :], ps[:, 0, :], ACT.Identity, bias=w("a_bk")).then_inc(s["proj_sb"], 1)
                    nc.scalar.activation(QT[:, :], ps[:, 1, :], ACT.Identity, bias=c["bq_scaled"][:, :],
                                         scale=scale).then_inc(s["proj_sb"], 1)

            def exponent(g, t):
                act.wait_ge(s["shifted"], Count(g, T)(t + 1))
                nc.scalar.activation(prob[:, t % 2, :, :], prob[:, t % 2, :, :], ACT.Exp,
                                     scale=scale if cross else 1.0).then_inc(s["exped"], 1)

            def turned_probs(g, t):
                act.wait_ge(s["pT_ps"], Count(g, T)(t + 1))
                nc.scalar.copy(probT[:, t % 2, :, :], ps[:, 4:6, :].rearrange("p a (b q) -> p (a b) q", b=4)
                               ).then_inc(s["pT_sb"], 1)

            def turned_out(g, t):
                act.wait_ge(s["aoT_ps"], Count(g, T)(t + 1))
                nc.scalar.copy(aoT[:, t % 2, :], ps[:, 6, 256:256 + P]).then_inc(s["aoT_sb"], 1)

            def main(g, ahead):
                for t in range(T):
                    if t == T - 1 and ahead:
                        columns_of(g + 1)
                    turned_probs(g, t)
                    if t == T - 1 and ahead:
                        project_in(g + 1)
                    if t >= 1:
                        turned_out(g, t - 1)
                    if t + 1 < T:
                        exponent(g, t + 1)
                turned_out(g, T - 1)
                if ahead:
                    exponent(g + 1, 0)

            columns_of(0)
            project_in(0)
            exponent(0, 0)
            with act.Fori(0, G - 1) as g:
                main(g, True)
            main(G - 1, False)

        @block.vector
        def _(dve):
            def stage(g):
                for t in range(T):
                    tile = g * T + t
                    last = nc.vector.tensor_scalar(xs[:, t, :], stream[:, bass.ds(tile, 1), :],
                                                   moments[:, bass.ds(tile, 1), 0], rstd[:, bass.ds(tile, 1)],
                                                   ALU.subtract, ALU.mult)
                last.then_inc(s["staged"], 1)
                dve.wait_ge(s["staged"], Count(g, 1)(1))
                if cross:
                    nc.vector.tensor_scalar(stream[:, bass.ds(g * T, T), :], xs[:, :, :], 1.0, None, ALU.mult)
                else:
                    nc.vector.tensor_tensor(stream[:, bass.ds(g * T, T), :], xs[:, :, :],
                                            w("a_bo").unsqueeze(1).to_broadcast([P, T, P]), ALU.add)

            def rope(g):
                dve.wait_ge(s["proj_ps"], Count(g, 1)(1))
                for n, tab in enumerate(("cos", "sin", "cos", "sin")):
                    last = nc.vector.tensor_tensor(
                        ropes[:, n, :].rearrange("p (b s) -> p b s", s=S), ps[:, n, :].rearrange("p (b s) -> p b s", s=S),
                        k(tab).unsqueeze(1).to_broadcast([P, GB, S]), ALU.mult)
                last.then_inc(s["roped"], 1)

            def values(g):
                dve.wait_ge(s["v_ps"], Count(g, 1)(1))
                for q in range(2):
                    for par in range(2):
                        src = ps[par * S:(par + 1) * S, 2 + q, :].rearrange("p (b j e d) -> p b j e d", b=4, e=2, d=DH)[:, :, :, par, :]
                        dst = V2[par * S:(par + 1) * S, 4 * q:4 * q + 4, :, par * DH:(par + 1) * DH]
                        if cross:
                            last = nc.vector.tensor_copy(dst, src)
                        else:
                            bv = w("a_bv")[par * S:(par + 1) * S, :].rearrange("p (j e d) -> p j e d", e=2, d=DH)[:, :, par, :]
                            last = nc.vector.tensor_tensor(dst, src, bv.unsqueeze(1).to_broadcast([S, 4, PAIRS, DH]), ALU.add)
                last.then_inc(s["v_sb"], 1)

            def soften(g, t):
                step = Chain(dve, s["softening"], g * T + t, SOFTENING)
                dve.wait_ge(s["scores"], Count(g, T)(t + 1))
                if t >= 2:
                    dve.wait_ge(s["pT_ps"], Count(g, T)(t - 1))
                sc = ps[:, 2 * (t % 2):2 * (t % 2) + 2, :].rearrange("p a (h q) -> p (a h) q", q=S)
                if not cross:
                    step(nc.vector.tensor_tensor(prob[:, t % 2, :, :], sc, c["relbias"][:, :, :], ALU.add))
                    sc = prob[:, t % 2, :, :]
                step(nc.vector.tensor_reduce(top[:, t % 2, :], sc, AX.X, ALU.max))
                nc.vector.tensor_tensor(prob[:, t % 2, :, :], sc, top[:, t % 2, :].unsqueeze(2).to_broadcast([P, H, S]),
                                        ALU.subtract).then_inc(s["shifted"], 1)

            def divide(g, t):
                dve.wait_ge(s["pv_ps"], Count(g, T)(t + 1))
                pv = ps[:, 6, 0:PAIRS * VW].rearrange("p (j v) -> p j v", v=VW)
                nc.vector.reciprocal(inv[:, t % 2, :].rearrange("p (j e) -> p j e", e=2), pv[:, :, 2 * DH:VW]
                                     ).then_inc(s["inverse"], 1)
                dve.wait_ge(s["inverse"], Count(g, T)(t + 1))
                nc.vector.tensor_tensor(
                    ao[:, t % 2, :].rearrange("p (j e d) -> p j e d", e=2, d=DH),
                    pv[:, :, 0:2 * DH].rearrange("p j (e d) -> p j e d", e=2),
                    inv[:, t % 2, :].rearrange("p (j e) -> p j e", e=2).unsqueeze(3).to_broadcast([P, PAIRS, 2, DH]),
                    ALU.mult).then_inc(s["ao_ready"], 1)

            def main(g, ahead):
                for t in range(T):
                    if t + 1 < T:
                        soften(g, t + 1)
                    if t == T - 1 and ahead and cross:
                        rope(g + 1)
                    divide(g, t)
                    if t == 0 and ahead:
                        stage(g + 1)
                if ahead:
                    values(g + 1)
                dve.wait_ge(s["out_ps"], Count(g, 1)(1))
                residual_group(nc, c, norm, Chain(dve, s["steps"], g, 3), g, ps[:, 7, :].rearrange("p (t d) -> p t d", d=P),
                               stream[:, bass.ds(g * T, T), :])
                if ahead:
                    soften(g + 1, 0)

            nc.vector.memset(V2[:, :, :, :], 0.0).then_inc(s["v_zero"], 1)
            dve.wait_ge(s["v_zero"], 1)
            nc.vector.memset(V2[0:S, :, :, 2 * DH:2 * DH + 1], 1.0)
            nc.vector.memset(V2[S:P, :, :, 2 * DH + 1:VW], 1.0).then_inc(s["v_ones"], 1)
            dve.wait_ge(s["v_ones"], 1)
            stage(0)
            if cross:
                rope(0)
            values(0)
            soften(0, 0)
            with dve.Fori(0, G - 1) as g:
                main(g, True)
            main(G - 1, False)

        @block.gpsimd
        def _(pool):
            def keys(g, t):
                if t == 0:
                    if cross:
                        pool.wait_ge(s["roped"], Count(g, 1)(1))
                        nc.gpsimd.tensor_tensor(KT[:, :], ropes[:, 2, :], ropes[:, 3, :], ALU.add).then_inc(s["proj_sb"], 1)
                        nc.gpsimd.tensor_tensor(QT[:, :], ropes[:, 0, :], ropes[:, 1, :], ALU.add).then_inc(s["proj_sb"], 1)
                    pool.wait_ge(s["proj_sb"], Count(g, 2)(1))
                if t >= 2:
                    pool.wait_ge(s["scores"], Count(g, T)(t - 1))
                nc.gpsimd.tensor_tensor(
                    KX[:, t % 2, :, :, :],
                    KT[:, t * P:(t + 1) * P].rearrange("p (b s) -> p b s", s=S).unsqueeze(2).to_broadcast([P, 2, H, S]),
                    k("headmask").unsqueeze(1).unsqueeze(3).to_broadcast([P, 2, H, S]), ALU.mult).then_inc(s["kx"], 1)

            def main(g, ahead):
                for t in range(1, T):
                    keys(g, t)
                if ahead:
                    if cross:
                        pool.wait_ge(s["scores"], Count(g, T)(T))
                    keys(g + 1, 0)

            keys(0, 0)
            with pool.Fori(0, G - 1) as g:
                main(g, True)
            main(G - 1, False)


def stage_tiles(nc, c, xs, i):
    for t in range(T):
        tile = i * T + t
        last = nc.vector.tensor_scalar(xs[:, t, :], c["stream"][:, bass.ds(tile, 1), :], c["moments"][:, bass.ds(tile, 1), 0],
                                       c["rstd"][:, bass.ds(tile, 1)], ALU.subtract, ALU.mult)
    return last


def experts_phase(nc, ctx, c, name):
    sb = lambda n, shape, dt=F32: ctx.enter_context(nc.sbuf_tensor(f"{name}_{n}", shape, dt))
    s = {n: c["sem"](f"{name}_{n}") for n in (
        "staged xT_ps xT_sb logits_ps pad_zero gap expgap prob up pick relu_done gated hidden down_ps down_sb y_ps "
        "steps tile_done turn_done").split()}
    w, ps = c["w"], c["psum"]
    E, F = 8, 64
    C = E * F // P
    xs, xT, norm = sb("xs", [P, T, P]), sb("xT", [P, T * P]), Norm(sb)
    logits, best, gap = sb("logits", [P, T, E]), sb("best", [P, T, E]), sb("gap", [P, T])
    chosen, prob = sb("chosen", [P, T, E]), sb("prob", [P, T, E, F], BF16)
    relu, gated, hid = sb("relu", [P, 2, T * P]), sb("gated", [P, 2, T * P]), sb("hid", [P, C + 1, T * P])
    yT = sb("yT", [P, T * P])
    STEPS = 5 + 2 * T

    with nc.Block() as block:
        @block.tensor
        def _(pe):
            pe.wait_ge(s["pad_zero"], 1)
            with pe.Fori(0, G) as i:
                one, up, down = Count(i, 1), Count(i, C + 1), Count(i, C)
                pe.wait_ge(s["staged"], one(1))
                for t in range(T):
                    last = nc.tensor.transpose(ps[:, 0, t * P:(t + 1) * P], xs[:, t, :], c["const"]("ident"))
                last.then_inc(s["xT_ps"], 1)
                pe.wait_ge(s["xT_sb"], one(1))
                for t in range(T):
                    last = nc.tensor.matmul(ps[:, 1, t * E:(t + 1) * E], xT[:, t * P:(t + 1) * P], w("e_wr"), start=True, stop=True)
                last.then_inc(s["logits_ps"], 1)

                def raise_(n):
                    if n >= 2:
                        pe.wait_ge(s["relu_done"], up(n - 1))
                    rows = P if n < C else F
                    nc.tensor.matmul(ps[0:rows, 2 + n % 2, :], w("e_w1")[:, n * P:n * P + rows], xT[:, :],
                                     start=True, stop=True).then_inc(s["up"], 1)

                def pick(n):
                    if n == 0:
                        pe.wait_ge(s["prob"], one(1))
                    if n >= 2:
                        pe.wait_ge(s["gated"], down(n - 1))
                    for t in range(T):
                        last = nc.tensor.matmul(ps[:, 4 + n % 2, t * P:(t + 1) * P], prob[:, t, 2 * n:2 * n + 2, :],
                                                c["ident16"][:, :], start=True, stop=True)
                    last.then_inc(s["pick"], 1)

                raise_(0)
                raise_(1)
                pick(0)
                pick(1)
                for n in range(C + 1):
                    if n + 2 < C + 1:
                        raise_(n + 2)
                    if n + 2 < C:
                        pick(n + 2)
                    pe.wait_ge(s["hidden"], up(n + 1))
                    last = nc.tensor.matmul(ps[:, 6, :], w("e_w2")[:, n * P:(n + 1) * P], hid[:, n, :],
                                            start=(n == 0), stop=(n == C))
                last.then_inc(s["down_ps"], 1)
                pe.wait_ge(s["down_sb"], one(1))
                for t in range(T):
                    last = nc.tensor.transpose(ps[:, 7, t * P:(t + 1) * P], yT[:, t * P:(t + 1) * P], c["const"]("ident"))
                last.then_inc(s["y_ps"], 1)
                pe.wait_ge(s["turn_done"], one(1))

        @block.scalar
        def _(act):
            with act.Fori(0, G) as i:
                one, up, down = Count(i, 1), Count(i, C + 1), Count(i, C)
                act.wait_ge(s["xT_ps"], one(1))
                nc.scalar.copy(xT[:, :], ps[:, 0, :]).then_inc(s["xT_sb"], 1)
                act.wait_ge(s["gap"], one(1))
                nc.scalar.activation(gap[:, :], gap[:, :], ACT.Exp).then_inc(s["expgap"], 1)

                def relu_of(n):
                    rows = P if n < C else F
                    act.wait_ge(s["up"], up(n + 1))
                    if 2 <= n < C:
                        act.wait_ge(s["gated"], down(n - 1))
                    nc.scalar.activation(relu[0:rows, n % 2, :], ps[0:rows, 2 + n % 2, :], ACT.Relu).then_inc(s["relu_done"], 1)

                relu_of(0)
                for n in range(C + 1):
                    if n + 1 <= C:
                        if n + 1 == C:
                            act.wait_ge(s["gated"], down(C - 1))
                        relu_of(n + 1)
                    if n < C:
                        act.wait_ge(s["gated"], down(n + 1))
                        nc.scalar.activation(hid[:, n, :], gated[:, n % 2, :], ACT.Square).then_inc(s["hidden"], 1)
                    else:
                        act.wait_ge(s["relu_done"], up(C + 1))
                        nc.scalar.activation(hid[0:F, n, :], relu[0:F, n % 2, :], ACT.Square).then_inc(s["hidden"], 1)
                act.wait_ge(s["down_ps"], one(1))
                nc.scalar.copy(yT[:, :], ps[:, 6, :]).then_inc(s["down_sb"], 1)
                act.wait_ge(s["turn_done"], one(1))

        @block.vector
        def _(dve):
            nc.vector.memset(hid[:, C, :], 0.0).then_inc(s["pad_zero"], 1)
            with dve.Fori(0, G) as i:
                one, up, down = Count(i, 1), Count(i, C + 1), Count(i, C)
                step = Chain(dve, s["steps"], i, STEPS)
                stage_tiles(nc, c, xs, i).then_inc(s["staged"], 1)
                dve.wait_ge(s["logits_ps"], one(1))
                nc.vector.tensor_scalar(logits[:, :, :], ps[:, 1, 0:T * E].rearrange("p (t e) -> p t e", e=E), 1.0, None, ALU.mult)
                for t in range(T):
                    last = nc.vector.max(best[:, t, :], ps[:, 1, t * E:(t + 1) * E])
                step(last)
                nc.vector.tensor_tensor(gap[:, :], best[:, :, 1], best[:, :, 0], ALU.subtract).then_inc(s["gap"], 1)
                step(nc.vector.tensor_tensor(chosen[:, :, :], logits[:, :, :], best[:, :, 0:1].to_broadcast([P, T, E]), ALU.is_equal))
                dve.wait_ge(s["expgap"], one(1))
                step(nc.vector.tensor_scalar(gap[:, :], gap[:, :], 1.0, None, ALU.add))
                step(nc.vector.reciprocal(gap[:, :], gap[:, :]))
                step(nc.vector.tensor_scalar(gap[:, :], gap[:, :], 1.0, None, ALU.is_ge))
                nc.vector.tensor_tensor(prob[:, :, :, :], chosen[:, :, :].unsqueeze(3).to_broadcast([P, T, E, F]),
                                        gap[:, :].unsqueeze(2).unsqueeze(3).to_broadcast([P, T, E, F]), ALU.mult).then_inc(s["prob"], 1)
                for n in range(C):
                    dve.wait_ge(s["relu_done"], up(n + 1))
                    dve.wait_ge(s["pick"], down(n + 1))
                    if n >= 2:
                        dve.wait_ge(s["hidden"], up(n - 1))
                    nc.vector.tensor_tensor(gated[:, n % 2, :], ps[:, 4 + n % 2, :], relu[:, n % 2, :], ALU.mult).then_inc(s["gated"], 1)
                for t in range(T):
                    if t == 0:
                        dve.wait_ge(s["y_ps"], one(1))
                    residual_step(nc, c, norm, step, i * T + t, t, ps[:, 7, t * P:(t + 1) * P], xs[:, t, :]).then_inc(s["tile_done"], 1)
                dve.wait_ge(s["tile_done"], Count(i, T)(T))
                assert step.n == STEPS, step.n
                keep_moments(nc, c, norm, i).then_inc(s["turn_done"], 1)
                dve.wait_ge(s["turn_done"], one(1))


def fourier_phase(nc, ctx, c, name):
    sb = lambda n, shape, dt=F32: ctx.enter_context(nc.sbuf_tensor(f"{name}_{n}", shape, dt))
    s = {n: c["sem"](f"{name}_{n}") for n in (
        "consts v_zero staged xT_ps xT_sb qkv_ps qk_sb v_sb z_ps reduced wrapped feats kv_ps kv_sb kvT_ps kvT_sb o_ps o_sb "
        "y_ps yT_sb yt_ps steps tile_done turn_done").split()}
    w, ps = c["w"], c["psum"]
    M = 128
    Q4 = H // 4
    UNIT = 1024
    KU = H * M // UNIT
    UPG = T * KU + Q4 * 2
    MAGIC = 1.5 * 2.0 ** 23
    TWO_PI, HALF_PI = 6.2831850, 1.5707962
    xs, xT, norm = sb("xs", [P, T, P]), sb("xT", [P, T * P]), Norm(sb)
    qT, kT = sb("qT", [P, T * P]), sb("kT", [P, T * P])
    projX = sb("projX", [P, H, M])
    vS = sb("vS", [P, T, H, 32])
    whole, frac, wrap = sb("whole", [P, 2, UNIT]), sb("frac", [P, 2, UNIT]), sb("wrap", [P, 2, UNIT])
    feats = sb("feats", [P, 2, 8, 2, M])
    qf = sb("qf", [P, 2, 4, 2, T * P])
    kvs = sb("kvs", [P, Q4, 2, M])
    kvm = sb("kvm", [P, T, Q4, 2, P])
    oT, yT = sb("oT", [P, Q4, T * P]), sb("yT", [P, T * P])
    half_pi, qb, vb = sb("half_pi", [P, 1]), sb("qb", [P, 1]), sb("vb", [P, P])
    kb = sb("kb", [P, 1])
    turn_scale = float(DH) ** -0.5 / (2 * np.pi)
    STEPS = UPG + 2 * T

    with nc.Block() as block:
        @block.tensor
        def _(pe):
            pe.wait_ge(s["consts"], 6)
            with pe.Fori(0, G) as i:
                one, per_tile, unit, quarter = Count(i, 1), Count(i, T), Count(i, UPG), Count(i, Q4)
                pe.wait_ge(s["staged"], one(1))
                for t in range(T):
                    last = nc.tensor.transpose(ps[:, 6, t * P:(t + 1) * P], xs[:, t, :], c["const"]("ident"))
                last.then_inc(s["xT_ps"], 1)
                pe.wait_ge(s["xT_sb"], one(1))
                nc.tensor.matmul(ps[:, 4, :], w("f_wq"), xT[:, :], start=True, stop=True)
                nc.tensor.matmul(ps[:, 5, :], w("f_wk"), xT[:, :], start=True, stop=True)
                for t in range(T):
                    last = nc.tensor.matmul(ps[:, 7, t * P:(t + 1) * P], xT[:, t * P:(t + 1) * P], w("f_wv"), start=True, stop=True)
                last.then_inc(s["qkv_ps"], 1)

                def key_angles(n):
                    t, u = divmod(n, KU)
                    if n >= 2:
                        pe.wait_ge(s["reduced"], unit(n - 1))
                    for q in range(2):
                        h = u * 8 + q * 4
                        last = nc.tensor.matmul(ps[:, 2 * (n % 2) + q, :], kT[:, t * P:(t + 1) * P], projX[:, h:h + 4, :],
                                                start=True, stop=True)
                    last.then_inc(s["z_ps"], 1)

                def query_angles(n):
                    pe.wait_ge(s["reduced"], unit(n - 1))
                    for q in range(2):
                        h = 2 * (n - T * KU) + q
                        last = nc.tensor.matmul(ps[:, 2 * (n % 2) + q, :], projX[:, h, :], qT[:, :], start=True, stop=True)
                    last.then_inc(s["z_ps"], 1)

                def angles(n):
                    if n < T * KU:
                        key_angles(n)
                    elif n < UPG:
                        query_angles(n)

                def key_values(t):
                    if t >= 1:
                        pe.wait_ge(s["kv_sb"], per_tile(t))
                    for u in range(KU):
                        pe.wait_ge(s["feats"], unit(t * KU + u + 1))
                        if t == 0 and u == 0:
                            pe.wait_ge(s["v_sb"], one(1))
                        for h in range(8 * u, 8 * u + 8):
                            q, r = divmod(h, 4)
                            last = nc.tensor.matmul(ps[32 * r:32 * r + 32, 4 + q // 2, (q % 2) * 256:(q % 2 + 1) * 256],
                                                    vS[:, t, h, :], feats[:, (t * KU + u) % 2, h % 8, :, :], start=True, stop=True)
                    last.then_inc(s["kv_ps"], 1)

                def turn_key_values(t):
                    pe.wait_ge(s["kv_sb"], per_tile(t + 1))
                    if t >= 1:
                        pe.wait_ge(s["kvT_sb"], per_tile(t))
                    for q in range(Q4):
                        for e in range(2):
                            n = 2 * q + e
                            last = nc.tensor.transpose(ps[:, 6 + n // 4, (n % 4) * P:(n % 4 + 1) * P], kvs[:, q, e, :], c["const"]("ident"))
                    last.then_inc(s["kvT_ps"], 1)

                def outputs(q):
                    pe.wait_ge(s["feats"], unit(T * KU + 2 * q + 2))
                    if q == 0:
                        pe.wait_ge(s["kvT_sb"], per_tile(T))
                    if q >= 2:
                        pe.wait_ge(s["o_sb"], quarter(q - 1))
                    for t in range(T):
                        for e in range(2):
                            for r in range(4):
                                last = nc.tensor.matmul(ps[32 * r:32 * r + 32, 4 + q % 2, t * P:(t + 1) * P],
                                                        kvm[:, t, q, e, 32 * r:32 * r + 32], qf[:, q % 2, r, e, t * P:(t + 1) * P],
                                                        start=(e == 0), stop=(e == 1))
                    last.then_inc(s["o_ps"], 1)

                pe.wait_ge(s["qk_sb"], one(1))
                angles(0)
                angles(1)
                for t in range(T):
                    angles(2 * t + 2)
                    key_values(t)
                    angles(2 * t + 3)
                    if t >= 1:
                        turn_key_values(t - 1)
                turn_key_values(T - 1)
                for q in range(Q4):
                    angles(T * KU + 2 * q + 2)
                    angles(T * KU + 2 * q + 3)
                    outputs(q)
                for par in range(2):
                    for q in range(Q4):
                        if par == 0:
                            pe.wait_ge(s["o_sb"], quarter(q + 1))
                        at = (par * Q4 + q) * P
                        toks = oT[:, q, :].rearrange("p (t b s) -> p t b s", b=2, s=S)[:, :, par, :]
                        last = nc.tensor.matmul(ps[:, 6, par * 256:(par + 1) * 256], w("f_wo")[:, at:at + P], toks,
                                                start=(q == 0), stop=(q == Q4 - 1))
                last.then_inc(s["y_ps"], 1)
                pe.wait_ge(s["yT_sb"], one(1))
                for t in range(T):
                    last = nc.tensor.transpose(ps[:, 7, t * P:(t + 1) * P], yT[:, t * P:(t + 1) * P], c["const"]("ident"))
                last.then_inc(s["yt_ps"], 1)
                pe.wait_ge(s["turn_done"], one(1))

        @block.scalar
        def _(act):
            nc.scalar.mul(qb[:, :], w("f_bq"), turn_scale).then_inc(s["consts"], 1)
            nc.scalar.mul(kb[:, :], w("f_bk"), turn_scale).then_inc(s["consts"], 1)
            nc.scalar.mul(vb[:, :], w("f_bv"), 1.0 / M).then_inc(s["consts"], 1)
            act.wait_ge(s["consts"], 6)
            with act.Fori(0, G) as i:
                one, per_tile, unit, quarter = Count(i, 1), Count(i, T), Count(i, UPG), Count(i, Q4)
                act.wait_ge(s["xT_ps"], one(1))
                nc.scalar.copy(xT[:, :], ps[:, 6, :]).then_inc(s["xT_sb"], 1)
                act.wait_ge(s["qkv_ps"], one(1))
                nc.scalar.activation(qT[:, :], ps[:, 4, :], ACT.Identity, bias=qb[:, :], scale=turn_scale)
                nc.scalar.activation(kT[:, :], ps[:, 5, :], ACT.Identity, bias=kb[:, :], scale=turn_scale).then_inc(s["qk_sb"], 1)

                def features(n):
                    act.wait_ge(s["reduced"], unit(n + 1))
                    if n < T * KU:
                        if n >= 2 and n % KU == 0:
                            act.wait_ge(s["kv_ps"], per_tile(n // KU))
                        sin = feats[:, n % 2, :, 1, :]
                        cos = feats[:, n % 2, :, 0, :]
                        view = lambda a: a.rearrange("p (h m) -> p h m", m=M)
                    else:
                        v = n - T * KU
                        if v >= 4 and v % 2 == 0:
                            act.wait_ge(s["o_ps"], quarter(v // 2 - 1))
                        h = (v % 2) * 2
                        sin = qf[:, (v // 2) % 2, h:h + 2, 1, :]
                        cos = qf[:, (v // 2) % 2, h:h + 2, 0, :]
                        view = lambda a: a.rearrange("p (h m) -> p h m", h=2)
                    nc.scalar.activation(sin, view(frac[:, n % 2, :]), ACT.Sin, scale=TWO_PI)
                    act.wait_ge(s["wrapped"], unit(n + 1))
                    nc.scalar.activation(cos, view(wrap[:, n % 2, :]), ACT.Sin, bias=half_pi[:, :], scale=-TWO_PI).then_inc(s["feats"], 1)

                for n in range(UPG):
                    features(n)
                    v = n - T * KU
                    if n < T * KU:
                        if n % 2 == 0 and n >= 2:
                            t = n // 2 - 1
                            act.wait_ge(s["kv_ps"], per_tile(t + 1))
                            if t >= 1:
                                act.wait_ge(s["kvT_ps"], per_tile(t))
                            nc.scalar.copy(kvs[:, :, :, :], ps[:, 4:6, :].rearrange("p a (b e m) -> p (a b) e m", b=2, e=2)).then_inc(s["kv_sb"], 1)
                    elif v == 0:
                        act.wait_ge(s["kv_ps"], per_tile(T))
                        act.wait_ge(s["kvT_ps"], per_tile(T - 1))
                        nc.scalar.copy(kvs[:, :, :, :], ps[:, 4:6, :].rearrange("p a (b e m) -> p (a b) e m", b=2, e=2)).then_inc(s["kv_sb"], 1)
                act.wait_ge(s["y_ps"], one(1))
                nc.scalar.activation(yT[:, :].rearrange("p (t b s) -> p b t s", b=2, s=S),
                                     ps[:, 6, :].rearrange("p (b t s) -> p b t s", b=2, s=S), ACT.Identity,
                                     bias=w("f_bo")).then_inc(s["yT_sb"], 1)
                act.wait_ge(s["turn_done"], one(1))

        @block.vector
        def _(dve):
            nc.vector.memset(half_pi[:, :], HALF_PI).then_inc(s["consts"], 1)
            nc.vector.memset(vS[:, :, :, :], 0.0).then_inc(s["consts"], 1)
            dve.wait_ge(s["consts"], 6)
            with dve.Fori(0, G) as i:
                one, per_tile, unit, quarter = Count(i, 1), Count(i, T), Count(i, UPG), Count(i, Q4)
                step = Chain(dve, s["steps"], i, STEPS)
                stage_tiles(nc, c, xs, i).then_inc(s["staged"], 1)
                dve.wait_ge(s["qkv_ps"], one(1))
                for b in range(2):
                    half = slice(b * S, (b + 1) * S)
                    last = nc.vector.scalar_tensor_tensor(
                        vS[half, :, :, b * DH:(b + 1) * DH], ps[half, 7, :].rearrange("p (t h d) -> p t h d", h=H, d=DH), 1.0 / M,
                        vb[half, :].rearrange("p (h d) -> p h d", d=DH).unsqueeze(1).to_broadcast([S, T, H, DH]), ALU.mult, ALU.add)
                last.then_inc(s["v_sb"], 1)

                def reduce_(n):
                    dve.wait_ge(s["z_ps"], unit(n + 1))
                    z = ps[:, 2 * (n % 2):2 * (n % 2) + 2, :].rearrange("p a b -> p (a b)")
                    step(nc.vector.tensor_scalar(whole[:, n % 2, :], z, MAGIC, MAGIC, ALU.add, ALU.subtract))
                    if n >= 2:
                        dve.wait_ge(s["feats"], unit(n - 1))
                    nc.vector.tensor_tensor(frac[:, n % 2, :], z, whole[:, n % 2, :], ALU.subtract).then_inc(s["reduced"], 1)
                    dve.wait_ge(s["reduced"], unit(n + 1))
                    nc.vector.tensor_scalar(wrap[:, n % 2, :].bitcast(I32), frac[:, n % 2, :].bitcast(I32), 0x7FFFFFFF, None, ALU.bitwise_and).then_inc(s["wrapped"], 1)

                def keep_kv(t):
                    dve.wait_ge(s["kvT_ps"], per_tile(t + 1))
                    nc.vector.tensor_copy(kvm[:, t, :, :, :], ps[:, 6:8, :].rearrange("p a (b e m) -> p (a b) e m", b=2, e=2)).then_inc(s["kvT_sb"], 1)

                def keep_o(q):
                    dve.wait_ge(s["o_ps"], quarter(q + 1))
                    nc.vector.tensor_copy(oT[:, q, :], ps[:, 4 + q % 2, :]).then_inc(s["o_sb"], 1)

                for n in range(UPG):
                    reduce_(n)
                    if n < T * KU and n % 2 == 1 and n >= 5:
                        keep_kv((n - 5) // 2)
                    v = n - T * KU
                    if v == 0:
                        keep_kv(T - 2)
                    if v == 2:
                        keep_kv(T - 1)
                    if v >= 4 and v % 2 == 0:
                        keep_o(v // 2 - 2)
                keep_o(Q4 - 2)
                keep_o(Q4 - 1)
                for t in range(T):
                    if t == 0:
                        dve.wait_ge(s["yt_ps"], one(1))
                    residual_step(nc, c, norm, step, i * T + t, t, ps[:, 7, t * P:(t + 1) * P], xs[:, t, :]).then_inc(s["tile_done"], 1)
                dve.wait_ge(s["tile_done"], per_tile(T))
                assert step.n == STEPS, step.n
                keep_moments(nc, c, norm, i).then_inc(s["turn_done"], 1)
                dve.wait_ge(s["turn_done"], one(1))

        @block.gpsimd
        def _(pool):
            nc.gpsimd.tensor_tensor(projX[:, :, :], w("f_proj").unsqueeze(1).to_broadcast([P, H, M]),
                                    c["const"]("headmask").unsqueeze(2).to_broadcast([P, H, M]), ALU.mult).then_inc(s["consts"], 1)


def latents_phase(nc, ctx, c, name):
    sb = lambda n, shape, dt=F32: ctx.enter_context(nc.sbuf_tensor(f"{name}_{n}", shape, dt))
    s = {n: c["sem"](f"{name}_{n}") for n in (
        "mats_in ab_ps ab_sb stats2 root2 ctx_in prep prep_steps consts staged scaled latT_ps latT_sb ctxT_ps XT_sb X_ps X_sb "
        "th_ps th_sb th16 rough top diag scores exped sums share px_ps px_sb recip y_ps yT_sb yt_ps steps out_read prep0 prep1 prep2 taken XT16").split()}
    w, ps = c["w"], c["psum"]
    norm = Norm(sb)
    lat, cx = sb("lat", [P, T, P]), sb("cx", [P, T, P])
    momc = sb("momc", [P, NT, 2])
    rstd2, rstdc = sb("rstd2", [P, NT]), sb("rstdc", [P, NT])
    keep, drop, bias = sb("keep", [P, NT]), sb("drop", [P, NT]), sb("bias", [P, B])
    A, N = sb("A", [P, H, P]), sb("N", [P, H, P])
    ident, ident16 = c["const"]("ident"), c["ident16"]
    ones16, ones32 = sb("ones16", [P, P], BF16), sb("ones32", [P, P])
    with ExitStack() as early:
        load = lambda n, shape, dt=F32: early.enter_context(nc.sbuf_tensor(f"{name}_{n}", shape, dt))
        mats = load("mats", [P, 4, PAIRS, P])
        cs = load("cs", [P, NT, P])
        mask = load("mask", [P, NT + B], mybir.dt.uint8)
        stats, momt = load("stats2", [P, T, 6]), load("momt", [P, T, 2])
        with nc.Block() as block:
            @block.sync
            def _(sp):
                sp.dma_start(mats[:, :, :, :], c["l_mats"]).then_inc(s["mats_in"], 16)
                sp.dma_start(mask[:, :], c["mask"]).then_inc(s["mats_in"], 16)
                sp.dma_start(cs[:, :, :], c["ctx"]).then_inc(s["ctx_in"], 16)

            @block.tensor
            def _(pe):
                pe.wait_ge(s["mats_in"], 32)
                for h in range(H):
                    if h == 8:
                        pe.wait_ge(s["ab_sb"], 4)
                    par = h % 2
                    r = slice(par * S, par * S + S)
                    at = (h % 8 // 2) * P
                    nc.tensor.matmul(ps[:, par, at:at + P], mats[r, 0, h // 2, :], mats[r, 1, h // 2, :], start=True, stop=True)
                    last = nc.tensor.matmul(ps[:, 2 + par, at:at + P], mats[r, 2, h // 2, :], mats[r, 3, h // 2, :], start=True, stop=True)
                    if h % 8 == 7:
                        last.then_inc(s["ab_ps"], 1)

            @block.scalar
            def _(act):
                for q in range(2):
                    act.wait_ge(s["ab_ps"], q + 1)
                    for par in range(2):
                        heads = slice(8 * q + par, 8 * q + 8, 2)
                        nc.scalar.activation(A[:, heads, :], ps[:, par, :].rearrange("p (h d) -> p h d", d=P), ACT.Copy,
                                             scale=0.125).then_inc(s["ab_sb"], 1)
                        nc.scalar.copy(N[:, heads, :], ps[:, 2 + par, :].rearrange("p (h d) -> p h d", d=P)).then_inc(s["ab_sb"], 1)
                act.wait_ge(s["stats2"], 1)
                nc.scalar.activation(rstd2[:, :], rstd2[:, :], ACT.Sqrt)
                nc.scalar.activation(rstdc[:, :], rstdc[:, :], ACT.Sqrt).then_inc(s["root2"], 1)

            @block.vector
            def _(dve):
                nc.vector.memset(ones16[:, :], 1.0)
                nc.vector.memset(ones32[:, :], 1.0)
                dve.wait_ge(s["mats_in"], 32)
                nc.vector.tensor_scalar(keep[:, :], mask[:, 0:NT], 1.0, None, ALU.mult)
                nc.vector.tensor_scalar(drop[:, :], mask[:, 0:NT], -1.0, 1.0, ALU.mult, ALU.add)
                nc.vector.tensor_scalar(bias[:, :], mask[:, NT:NT + B], 1e30, 1e30, ALU.mult, ALU.subtract)
                nc.vector.tensor_tensor(rstd2[:, :], c["moments"][:, :, 1], c["rstd"][:, :], ALU.mult).then_inc(s["prep"], 1)
                dve.wait_ge(s["prep"], 1)
                nc.vector.tensor_tensor(rstd2[:, :], rstd2[:, :], c["rstd"][:, :], ALU.mult).then_inc(s["prep"], 1)
                dve.wait_ge(s["prep"], 2)
                nc.vector.tensor_scalar(rstd2[:, :], rstd2[:, :], LN_EPS, None, ALU.add)
                dve.wait_ge(s["ctx_in"], 16)
                with dve.Fori(0, G) as i:
                    step = Chain(dve, s["prep_steps"], i, 2)
                    for t in range(T):
                        last = nc.vector.bn_stats(stats[:, t, :], cs[:, bass.ds(i * T + t, 1), :])
                    step(last)
                    dve.sem_inc(s["taken"], 1)
                    for t in range(T):
                        last = nc.vector.bn_aggr(momt[:, t, :], stats[:, t, :])
                    step(last)
                    nc.vector.tensor_scalar(momc[:, bass.ds(i * T, T), :], momt[:, :, :], 1.0, None, ALU.mult).then_inc(s["prep"], 1)
                dve.wait_ge(s["prep"], G + 2)
                nc.vector.tensor_scalar(rstdc[:, :], momc[:, :, 1], LN_EPS, None, ALU.add).then_inc(s["stats2"], 1)
                dve.wait_ge(s["root2"], 1)
                nc.vector.reciprocal(rstd2[:, :], rstd2[:, :]).then_inc(s["prep"], 1)
                nc.vector.reciprocal(rstdc[:, :], rstdc[:, :])
                dve.wait_ge(s["prep"], G + 3)
                nc.vector.tensor_tensor(rstd2[:, :], rstd2[:, :], c["rstd"][:, :], ALU.mult)

    bias_now = sb("bias_now", [P, GB])
    craw, xs = sb("craw", [P, T, P]), sb("xs", [P, T, P])
    gx = sb("gx", [P, 2, T, P])
    XT, XT16 = sb("XT", [P, GB, 2, S]), sb("XT16", [P, GB, 2 * S], BF16)
    X = sb("X", [P, GB, P])
    th, th16 = sb("th", [P, GB, H, S]), sb("th16", [P, GB, H, S], BF16)
    top, diag = sb("top", [P, 4, PAIRS]), sb("diag", [P, 3, PAIRS, P], BF16)
    prob = sb("prob", [P, 4, 2, 512])
    recip = sb("recip", [P, 2, 512])
    share = sb("share", [P, 2, 2, 2, 512])
    px = sb("px", [P, H, GB, S])
    yT = sb("yT", [P, T * P])
    BP = GB // 2
    LAG = 3
    BETWEEN = {3: GB - 3, 8: GB - 2, 13: GB - 1}

    with nc.Block() as block:
        @block.sync
        def _(sp):
            sp.dma_start(craw[:, :, :], c["ctx"][:, 0:T, :]).then_inc(s["ctx_in"], 16)
            with sp.Fori(1, G) as i:
                sp.wait_ge(s["scaled"], i)
                sp.dma_start(craw[:, :, :], c["ctx"][:, bass.ds(i * T, T), :]).then_inc(s["ctx_in"], 16)

        @block.tensor
        def _(pe):
            def heads(g, gathered):
                one, head = Count(g, 1), Count(g, H)
                pe.wait_ge(s["staged"], one(1))
                for t in range(T):
                    nc.tensor.transpose(ps[:, 0, t * P:(t + 1) * P], lat[:, t, :], ident)
                for t in range(T):
                    last = nc.tensor.transpose(ps[:, 1, t * P:(t + 1) * P], cx[:, t, :], ident)
                last.then_inc(s["latT_ps"], 1)
                pe.wait_ge(s["XT_sb"], one(1))
                for h in range(H):
                    if h in BETWEEN and gathered is not None:
                        gather(gathered, BETWEEN[h])
                    if h >= 4:
                        pe.wait_ge(s["th_sb"], head(h - 3))
                    nc.tensor.matmul(ps[:, h % 4, :], A[:, h, :], XT[:, :, 1, :], start=True, stop=True).then_inc(s["th_ps"], 1)

            def keys_back(g):
                for b in range(GB):
                    last = nc.tensor.transpose(ps[:, 4 + b // 4, (b % 4) * P:(b % 4 + 1) * P], XT[:, b, :, :], ident)
                last.then_inc(s["X_ps"], 1)

            def rough(g, b):
                if b == 0:
                    pe.wait_ge(s["th16"], Count(g, H)(H))
                    pe.wait_ge(s["XT16"], Count(g, 1)(1))
                else:
                    pe.wait_ge(s["top"], Count(g, GB)(b))
                for j in range(PAIRS):
                    last = nc.tensor.matmul(ps[:, j // 4, (j % 4) * P:(j % 4 + 1) * P], th16[:, b, 2 * j:2 * j + 2, :],
                                            XT16[:, b, :], start=True, stop=True)
                last.then_inc(s["rough"], 1)

            def scores(g, b):
                batch = Count(g, GB)
                if b >= 1:
                    pe.wait_ge(s["exped"], batch(b))
                for q in range(2):
                    nc.tensor.matmul(ps[:, 2 + q, :], XT[:, b, :, :], th[:, b, 8 * q:8 * q + 8, :], start=True, stop=False)
                pe.wait_ge(s["diag"], batch(b + 1))
                for q in range(2):
                    last = nc.tensor.matmul(ps[:, 2 + q, :], ones16[:, :], diag[:, b % 3, 4 * q:4 * q + 4, :], start=False, stop=True)
                last.then_inc(s["scores"], 1)

            def sums(g, p):
                pe.wait_ge(s["exped"], Count(g, GB)(2 * p + 2))
                if p >= 2:
                    pe.wait_ge(s["recip"], Count(g, BP)(p - 1))
                if p == 1:
                    pe.wait_ge(s["out_read"], Count(g, 1)(1))
                for b in range(2):
                    for q in range(2):
                        at = 32 * (2 * b + q)
                        last = nc.tensor.matmul(ps[at:at + 32, 6 + p % 2, :], ones32[:, 0:32], prob[:, (2 * p + b) % 4, q, :],
                                                start=True, stop=True)
                last.then_inc(s["sums"], 1)

            def gather(g, b):
                if b == 0:
                    pe.wait_ge(s["X_sb"], Count(g, 1)(1))
                else:
                    pe.wait_ge(s["px_sb"], Count(g, GB)(b))
                for q in range(2):
                    last = nc.tensor.matmul(ps[:, 4 + q, :], X[:, b, :], prob[:, b % 4, q, :], start=True, stop=True)
                last.then_inc(s["px_ps"], 1)

            def start(g):
                keys_back(g)
                rough(g, 0)
                rough(g, 1)

            def main(g):
                for b in range(GB):
                    scores(g, b)
                    if b + 2 < GB:
                        rough(g, b + 2)
                    if b % 2 == 1:
                        sums(g, b // 2)
                    if b >= LAG:
                        gather(g, b - LAG)

            def combine(g):
                pe.wait_ge(s["px_sb"], Count(g, GB)(GB))
                for h in range(H):
                    last = nc.tensor.matmul(ps[:, 6, :], N[:, h, :], px[:, h, :, :], start=(h == 0), stop=(h == H - 1))
                last.then_inc(s["y_ps"], 1)

            def finish(g):
                pe.wait_ge(s["yT_sb"], Count(g, 1)(1))
                for t in range(T):
                    last = nc.tensor.transpose(ps[:, 7, t * P:(t + 1) * P], yT[:, t * P:(t + 1) * P], ident)
                last.then_inc(s["yt_ps"], 1)

            heads(0, None)
            start(0)
            with pe.Fori(0, G - 1) as g:
                main(g)
                heads(g + 1, g)
                combine(g)
                start(g + 1)
                finish(g)
            main(G - 1)
            for b in range(GB - LAG, GB):
                gather(G - 1, b)
            combine(G - 1)
            finish(G - 1)

        @block.scalar
        def _(act):
            def heads(g):
                one, head = Count(g, 1), Count(g, H)
                act.wait_ge(s["latT_ps"], one(1))
                nc.scalar.copy(XT[:, :, 1, :], ps[:, 0, :].rearrange("p (b s) -> p b s", s=S))
                nc.scalar.copy(XT[:, :, 0, :], ps[:, 1, :].rearrange("p (b s) -> p b s", s=S)).then_inc(s["XT_sb"], 1)
                for h in range(H):
                    act.wait_ge(s["th_ps"], head(h + 1))
                    nc.scalar.copy(th[:, :, h, :], ps[:, h % 4, :].rearrange("p (b s) -> p b s", s=S)).then_inc(s["th_sb"], 1)
                    if h == 0:
                        act.wait_ge(s["XT_sb"], one(1))
                        nc.scalar.copy(XT16[:, :, :], XT[:, :, :, :].rearrange("p b a s -> p b (a s)")).then_inc(s["XT16"], 1)

            def main(g):
                batch = Count(g, GB)
                for b in range(GB):
                    act.wait_ge(s["scores"], batch(b + 1))
                    if b >= 4:
                        act.wait_ge(s["px_ps"], batch(b - 3))
                    nc.scalar.activation(prob[:, b % 4, :, :], ps[:, 2:4, :], ACT.Exp,
                                         bias=bias_now[:, b:b + 1]).then_inc(s["exped"], 1)

            def finish(g):
                act.wait_ge(s["y_ps"], Count(g, 1)(1))
                nc.scalar.copy(yT[:, :], ps[:, 6, :]).then_inc(s["yT_sb"], 1)

            heads(0)
            with act.Fori(0, G - 1) as g:
                main(g)
                heads(g + 1)
                finish(g)
            main(G - 1)
            finish(G - 1)

        @block.vector
        def _(dve):
            def prepare(g, after):
                if after is not None:
                    dve.wait_ge(s["latT_ps"], after)
                dve.wait_ge(s["ctx_in"], 16 * g + 32)
                for t in range(T):
                    tile = g * T + t
                    nc.vector.tensor_scalar(lat[:, t, :], c["stream"][:, bass.ds(tile, 1), :], c["moments"][:, bass.ds(tile, 1), 0],
                                            rstd2[:, bass.ds(tile, 1)], ALU.subtract, ALU.mult)
                    nc.vector.tensor_scalar(xs[:, t, :], c["stream"][:, bass.ds(tile, 1), :], c["moments"][:, bass.ds(tile, 1), 0],
                                            c["rstd"][:, bass.ds(tile, 1)], ALU.subtract, ALU.mult)
                for t in range(T):
                    tile = g * T + t
                    last = nc.vector.tensor_scalar(cx[:, t, :], craw[:, t, :], momc[:, bass.ds(tile, 1), 0],
                                                   rstdc[:, bass.ds(tile, 1)], ALU.subtract, ALU.mult)
                last.then_inc(s["scaled"], 1)
                dve.wait_ge(s["scaled"], Count(g, 1)(1))
                nc.vector.tensor_scalar(c["stream"][:, bass.ds(g * T, T), :], xs[:, :, :], 1.0, None, ALU.mult)

            def heads(g, gathered):
                head = Count(g, H)
                for h in range(H):
                    if h in BETWEEN and gathered is not None:
                        divide(gathered, BETWEEN[h])
                    dve.wait_ge(s["th_sb"], head(h + 1))
                    nc.vector.tensor_copy(th16[:, :, h, :], th[:, :, h, :]).then_inc(s["th16"], 1)

            def divide(g, b):
                batch = Count(g, GB)
                dve.wait_ge(s["px_ps"], batch(b + 1))
                dve.wait_ge(s["share"], Count(g, 2 * GB)(2 * b + 2))
                nc.vector.tensor_tensor(px[:, :, b, :], ps[:, 4:6, :].rearrange("p a (h s) -> p (a h) s", s=S),
                                        share[:, (b // 2) % 2, b % 2, :, :].rearrange("p a (h s) -> p (a h) s", s=S),
                                        ALU.mult).then_inc(s["px_sb"], 1)

            def row_tops(g, b):
                dve.wait_ge(s["rough"], Count(g, GB)(b + 1))
                nc.vector.tensor_reduce(top[:, b % 4, :], ps[:, 0:2, :].rearrange("p a (j n) -> p (a j) n", n=P), AX.X, ALU.max,
                                        negate=True).then_inc(s["top"], 1)

            def invert(g, p):
                dve.wait_ge(s["sums"], Count(g, BP)(p + 1))
                if p >= 2:
                    dve.wait_ge(s["share"], Count(g, 2 * GB)(4 * p - 4))
                nc.vector.reciprocal(recip[:, p % 2, :], ps[:, 6 + p % 2, :]).then_inc(s["recip"], 1)

            def start(g):
                dve.wait_ge(s["X_ps"], Count(g, 1)(1))
                nc.vector.tensor_copy(X[:, :, :], ps[:, 4:6, :].rearrange("p a (b d) -> p (a b) d", d=P)).then_inc(s["X_sb"], 1)
                row_tops(g, 0)
                row_tops(g, 1)

            def main(g, prepare_next):
                for b in range(GB):
                    if b + 2 < GB:
                        row_tops(g, b + 2)
                    if b % 2 == 1:
                        invert(g, b // 2)
                    if b >= LAG:
                        divide(g, b - LAG)
                    if b == 0 and prepare_next:
                        prepare(g + 1, Count(g, 1)(1))

            def finish(g):
                step = Chain(dve, s["steps"], g, 3)
                dve.wait_ge(s["yt_ps"], Count(g, 1)(1))
                residual_group(nc, c, norm, step, g, ps[:, 7, :].rearrange("p (t d) -> p t d", d=P),
                               c["stream"][:, bass.ds(g * T, T), :]).then_inc(s["out_read"], 1)

            dve.sem_inc(s["out_read"], 1)
            prepare(0, None)
            nc.vector.tensor_scalar(bias_now[:, :], bias[:, 0:GB], 1.0, None, ALU.mult)
            heads(0, None)
            start(0)
            with dve.Fori(0, G - 1) as g:
                main(g, True)
                dve.wait_ge(s["exped"], Count(g, GB)(GB))
                nc.vector.tensor_scalar(bias_now[:, :], bias[:, bass.ds((g + 1) * GB, GB)], 1.0, None, ALU.mult)
                heads(g + 1, g)
                start(g + 1)
                finish(g)
            main(G - 1, False)
            for b in range(GB - LAG, GB):
                divide(G - 1, b)
            finish(G - 1)

        @block.gpsimd
        def _(pool):
            wide = lambda a: a.unsqueeze(1).to_broadcast([P, T, P])

            group = lambda a, g: a[:, bass.ds(g * T, T)].unsqueeze(2).to_broadcast([P, T, P])

            def prepare(g, part):
                if part == 0:
                    pool.wait_ge(s["scaled"], Count(g, 1)(1))
                    nc.gpsimd.tensor_tensor(gx[:, 0, :, :], lat[:, :, :], wide(w("l_g2")), ALU.mult)
                elif part == 1:
                    nc.gpsimd.tensor_tensor(gx[:, 1, :, :], cx[:, :, :], wide(w("l_g1")), ALU.mult).then_inc(s["prep0"], 1)
                elif part == 2:
                    pool.wait_ge(s["prep0"], Count(g, 1)(1))
                    nc.gpsimd.tensor_tensor(lat[:, :, :], gx[:, 0, :, :], wide(w("l_b2")), ALU.add)
                elif part == 3:
                    nc.gpsimd.tensor_tensor(cx[:, :, :], gx[:, 1, :, :], wide(w("l_b1")), ALU.add).then_inc(s["prep1"], 1)
                elif part == 4:
                    pool.wait_ge(s["prep1"], Count(g, 1)(1))
                    nc.gpsimd.tensor_tensor(gx[:, 0, :, :], cx[:, :, :], group(keep, g), ALU.mult)
                elif part == 5:
                    nc.gpsimd.tensor_tensor(gx[:, 1, :, :], lat[:, :, :], group(drop, g), ALU.mult).then_inc(s["prep2"], 1)
                elif part == 6:
                    pool.wait_ge(s["prep2"], Count(g, 1)(1))
                    nc.gpsimd.tensor_tensor(cx[:, :, :], gx[:, 0, :, :], gx[:, 1, :, :], ALU.add).then_inc(s["staged"], 1)

            def shift(g, b):
                pool.wait_ge(s["top"], Count(g, GB)(b + 1))
                if b >= 3:
                    pool.wait_ge(s["scores"], Count(g, GB)(b - 2))
                nc.gpsimd.tensor_tensor(diag[:, b % 3, :, :], ident16[:, :].unsqueeze(1).to_broadcast([P, PAIRS, P]),
                                        top[:, b % 4, :].unsqueeze(2).to_broadcast([P, PAIRS, P]), ALU.mult).then_inc(s["diag"], 1)

            def spread(g, p):
                pool.wait_ge(s["recip"], Count(g, BP)(p + 1))
                if p >= 2:
                    pool.wait_ge(s["px_sb"], Count(g, GB)(2 * p - 2))
                pool.sem_inc(s["taken"], 1)
                for n in range(4):
                    nc.gpsimd.partition_broadcast(share[:, p % 2, n // 2, n % 2, :], recip[32 * n:32 * n + 1, p % 2, :], P
                                                  ).then_inc(s["share"], 1)
                    pool.wait_ge(s["share"], Count(g, 2 * GB)(4 * p + n + 1))
                    pool.sem_inc(s["taken"], 1)

            def start(g):
                shift(g, 0)
                shift(g, 1)

            def main(g, prepare_next):
                for b in range(GB):
                    if b + 2 < GB:
                        shift(g, b + 2)
                    if b % 2 == 1:
                        spread(g, b // 2)
                    if prepare_next and b < 7:
                        prepare(g + 1, b)

            for part in range(7):
                prepare(0, part)
            start(0)
            with pool.Fori(0, G - 1) as g:
                main(g, True)
                start(g + 1)
            main(G - 1, False)


def bitlinear_phase(nc, ctx, c, name):
    sb = lambda n, shape, dt=F32: ctx.enter_context(nc.sbuf_tensor(f"{name}_{n}", shape, dt))
    s = {n: c["sem"](f"{name}_{n}") for n in (
        "mags mag_ps quant ws_ready staged ss1 root1 x_ready x_ps x_sb h_ps r_sb h_sb g_sb ss2 root2 q_ready q_ps q_sb y_ps "
        "tile_done turn_done steps wsteps taken out1").split()}
    w, ps = c["w"], c["psum"]
    HID = 512
    HC = HID // P
    MAGIC = 1.5 * 2.0 ** 23
    EPS_NORM, EPS_Q = 1e-8, 1e-5
    xs, norm = sb("xs", [P, T, P]), Norm(sb)
    wq, wtmp = sb("wq", [P, 2, HID], BF16), sb("wtmp", [P, 2, HID])
    mags, wmean, wscale, ones = sb("mags", [P, 2]), sb("wmean", [P, 2]), sb("wscale", [P, 2]), sb("ones", [P, P])
    sq, ss1, ss2 = sb("sq", [P, T, HID]), sb("ss1", [P, T]), sb("ss2", [P, T])
    xn, amax, xscale, deq = sb("xn", [P, T, P]), sb("amax", [P, T]), sb("xscale", [P, T]), sb("deq", [P, T])
    xi, xiT = sb("xi", [P, T, P], BF16), sb("xiT", [P, T * P], BF16)
    r, hh, hn = sb("r", [P, T, HID]), sb("hh", [P, T, HID]), sb("hn", [P, T, HID])
    amax2, hscale, deq2 = sb("amax2", [P, T]), sb("hscale", [P, T]), sb("deq2", [P, T])
    hi, hiT = sb("hi", [P, T, HID], BF16), sb("hiT", [P, 2, HID], BF16)
    eps = sb("eps", [P, 1])
    raw = [w("b_w1"), w("b_w2")]
    EARLY, STEPS = 4, 2 * (3 + 6) + 3 * T

    def quantise(link, values, out, scales, deqs, biggest, width, weight_mean):
        wide = lambda a: a.unsqueeze(2).to_broadcast([P, T, width])
        link(nc.vector.tensor_reduce(biggest[:, :], values, AX.X, ALU.max, apply_absolute_value=True))
        link(nc.vector.tensor_scalar(biggest[:, :], biggest[:, :], EPS_Q, None, ALU.max))
        link(nc.vector.reciprocal(scales[:, :], biggest[:, :]))
        nc.vector.tensor_scalar(deqs[:, :], biggest[:, :], 1.0 / 127.0, weight_mean, ALU.mult, ALU.mult)
        link(nc.vector.tensor_scalar(scales[:, :], scales[:, :], 127.0, None, ALU.mult))
        link(nc.vector.tensor_tensor(values, values, wide(scales[:, :]), ALU.mult))
        link(nc.vector.tensor_scalar(values, values, -128.0, 127.0, ALU.max, ALU.min))
        return nc.vector.tensor_scalar(out, values, MAGIC, MAGIC, ALU.add, ALU.subtract)

    with nc.Block() as block:
        def down(pe, per_tile, t):
            pe.wait_ge(s["q_sb"], per_tile(t + 1))
            for n in range(HC):
                last = nc.tensor.matmul(ps[:, 7, t * P:(t + 1) * P], hiT[:, t % 2, n * P:(n + 1) * P], wq[:, 1, n * P:(n + 1) * P],
                                        start=(n == 0), stop=(n == HC - 1))
            if t == T - 1:
                last.then_inc(s["y_ps"], 1)

        @block.tensor
        def _(pe):
            pe.wait_ge(s["mags"], 1)
            nc.tensor.matmul(ps[:, 0, 0:2], ones[:, :], mags[:, :], start=True, stop=True).then_inc(s["mag_ps"], 1)
            pe.wait_ge(s["quant"], 1)
            with pe.Fori(0, G) as i:
                one, per_tile = Count(i, 1), Count(i, T)
                pe.wait_ge(s["x_ready"], one(1))
                for t in range(T):
                    last = nc.tensor.matmul(ps[:, 0, t * P:(t + 1) * P], xi[:, t, :], c["ident16"][:, :], start=True, stop=True)
                last.then_inc(s["x_ps"], 1)
                pe.wait_ge(s["x_sb"], one(1))
                for t in range(T):
                    nc.tensor.matmul(ps[:, 1 + t, :], xiT[:, t * P:(t + 1) * P], wq[:, 0, :], start=True, stop=True
                                     ).then_inc(s["h_ps"], 1)
                pe.wait_ge(s["q_ready"], one(1))
                for t in range(T):
                    if t >= 2:
                        pe.wait_ge(s["q_sb"], per_tile(t - 1))
                    for n in range(HC):
                        last = nc.tensor.matmul(ps[:, 5 + t % 2, n * P:(n + 1) * P], hi[:, t, n * P:(n + 1) * P], c["ident16"][:, :],
                                                start=True, stop=True)
                    last.then_inc(s["q_ps"], 1)
                    if t >= 1:
                        down(pe, per_tile, t - 1)
                down(pe, per_tile, T - 1)
                pe.wait_ge(s["turn_done"], one(1))

        @block.scalar
        def _(act):
            with act.Fori(0, G) as i:
                one, per_tile = Count(i, 1), Count(i, T)
                act.wait_ge(s["staged"], one(1))
                for t in range(T):
                    last = nc.scalar.activation(sq[:, t, 0:P], xs[:, t, :], ACT.Square, accum_out=ss1[:, t:t + 1])
                last.then_inc(s["ss1"], 1)
                act.wait_ge(s["ss1"], one(1))
                nc.scalar.activation(ss1[:, :], ss1[:, :], ACT.Sqrt, bias=eps[:, :], scale=1.0 / P).then_inc(s["root1"], 1)
                act.wait_ge(s["x_ps"], one(1))
                nc.scalar.copy(xiT[:, :], ps[:, 0, :]).then_inc(s["x_sb"], 1)
                for t in range(T):
                    act.wait_ge(s["h_ps"], per_tile(t + 1))
                    nc.scalar.activation(r[:, t, :], ps[:, 1 + t, :], ACT.Relu, scale=deq[:, t:t + 1]).then_inc(s["r_sb"], 1)
                for t in range(T):
                    act.wait_ge(s["r_sb"], per_tile(t + 1))
                    nc.scalar.activation(r[:, t, :], r[:, t, :], ACT.Square).then_inc(s["h_sb"], 1)
                act.wait_ge(s["root1"], one(1))
                for t in range(T):
                    act.wait_ge(s["g_sb"], per_tile(t + 1))
                    last = nc.scalar.activation(sq[:, t, :], hh[:, t, :], ACT.Square, accum_out=ss2[:, t:t + 1])
                last.then_inc(s["ss2"], 1)
                act.wait_ge(s["ss2"], one(1))
                nc.scalar.activation(ss2[:, :], ss2[:, :], ACT.Sqrt, bias=eps[:, :], scale=1.0 / HID).then_inc(s["root2"], 1)
                for t in range(T):
                    act.wait_ge(s["q_ps"], per_tile(t + 1))
                    nc.scalar.copy(hiT[:, t % 2, :], ps[:, 5 + t % 2, :]).then_inc(s["q_sb"], 1)
                act.wait_ge(s["turn_done"], one(1))

        @block.vector
        def _(dve):
            early = Chain(dve, s["wsteps"], 0, EARLY)
            nc.vector.memset(ones[:, :], 1.0)
            nc.vector.memset(eps[:, :], EPS_NORM)
            for n in range(2):
                last = nc.vector.tensor_reduce(mags[:, n:n + 1], raw[n], AX.X, ALU.add, apply_absolute_value=True)
            last.then_inc(s["mags"], 1)
            dve.wait_ge(s["mag_ps"], 1)
            early(nc.vector.tensor_scalar(wmean[:, :], ps[:, 0, 0:2], 1.0 / (P * HID), EPS_Q, ALU.mult, ALU.max))
            early(nc.vector.reciprocal(wscale[:, :], wmean[:, :]))
            for n in range(2):
                last = nc.vector.tensor_scalar(wtmp[:, n, :], raw[n], wscale[:, n:n + 1], None, ALU.mult)
            early(last)
            early(nc.vector.tensor_scalar(wtmp[:, :, :], wtmp[:, :, :], MAGIC, MAGIC, ALU.add, ALU.subtract))
            nc.vector.tensor_scalar(wq[:, :, :], wtmp[:, :, :], -1.0, 1.0, ALU.max, ALU.min).then_inc(s["quant"], 1)
            dve.wait_ge(s["quant"], 1)
            with dve.Fori(0, G) as i:
                one, per_tile = Count(i, 1), Count(i, T)
                step = Chain(dve, s["steps"], i, STEPS)
                wide = lambda a, n: a.unsqueeze(2).to_broadcast([P, T, n])
                stage_tiles(nc, c, xs, i).then_inc(s["staged"], 1)
                dve.wait_ge(s["root1"], one(1))
                step(nc.vector.reciprocal(ss1[:, :], ss1[:, :]))
                step(nc.vector.tensor_tensor(xn[:, :, :], xs[:, :, :], wide(ss1[:, :], P), ALU.mult))
                step(nc.vector.tensor_tensor(xn[:, :, :], xn[:, :, :], w("b_n1").unsqueeze(1).to_broadcast([P, T, P]), ALU.mult))
                quantise(step, xn[:, :, :], xi[:, :, :], xscale, deq, amax, P, wmean[:, 0:1]).then_inc(s["x_ready"], 1)
                for t in range(T):
                    dve.wait_ge(s["h_sb"], per_tile(t + 1))
                    nc.vector.tensor_scalar(hh[:, t, :], r[:, t, :], w("b_as"), w("b_ab"), ALU.mult, ALU.add).then_inc(s["g_sb"], 1)
                dve.wait_ge(s["root2"], one(1))
                step(nc.vector.reciprocal(ss2[:, :], ss2[:, :]))
                step(nc.vector.tensor_tensor(hn[:, :, :], hh[:, :, :], wide(ss2[:, :], HID), ALU.mult))
                step(nc.vector.tensor_tensor(hn[:, :, :], hn[:, :, :], w("b_n2").unsqueeze(1).to_broadcast([P, T, HID]), ALU.mult))
                quantise(step, hn[:, :, :], hi[:, :, :], hscale, deq2, amax2, HID, wmean[:, 1:2]).then_inc(s["q_ready"], 1)
                dve.wait_ge(s["y_ps"], one(1))
                for t in range(T):
                    step(nc.vector.tensor_scalar(xn[:, t, :], ps[:, 7, t * P:(t + 1) * P], deq2[:, t:t + 1], None, ALU.mult))
                    residual_step(nc, c, norm, step, i * T + t, t, xn[:, t, :], xs[:, t, :]).then_inc(s["tile_done"], 1)
                dve.wait_ge(s["tile_done"], per_tile(T))
                assert step.n == STEPS, step.n
                keep_moments(nc, c, norm, i).then_inc(s["turn_done"], 1)
                dve.wait_ge(s["turn_done"], one(1))


def norm_phase(nc, ctx, c, name):
    var_ready = c["sem"](f"{name}_var_ready")
    root_ready = c["sem"](f"{name}_root_ready")
    rstd = c["rstd"]
    with nc.Block() as block:
        @block.vector
        def _(dve):
            nc.vector.tensor_scalar(rstd[:, :], c["moments"][:, :, 1], LN_EPS, None, ALU.add).then_inc(var_ready, 1)
            dve.wait_ge(root_ready, 1)
            nc.vector.reciprocal(rstd[:, :], rstd[:, :])

        @block.scalar
        def _(act):
            act.wait_ge(var_ready, 1)
            nc.scalar.activation(rstd[:, :], rstd[:, :], ACT.Sqrt).then_inc(root_ready, 1)


def output_phase(nc, ctx, c, out):
    normed = c["sem"]("normed")
    stored = c["sem"]("stored")
    y = ctx.enter_context(nc.sbuf_tensor("y_out", [P, NT, P], F32))
    out = out.rearrange("(n k) s d -> (k s) n d", k=2)
    with nc.Block() as block:
        @block.vector
        def _(dve):
            with dve.Fori(0, NT) as i:
                nc.vector.tensor_scalar(y[:, bass.ds(i, 1), :], c["stream"][:, bass.ds(i, 1), :], c["moments"][:, bass.ds(i, 1), 0],
                                        c["rstd"][:, bass.ds(i, 1)], ALU.subtract, ALU.mult).then_inc(normed, 1)

        @block.sync
        def _(sp):
            with sp.Fori(0, G) as i:
                sp.wait_ge(normed, i * T + T)
                sp.dma_start(out[:, bass.ds(i * T, T), :], y[:, bass.ds(i * T, T), :]).then_inc(stored, 16)
            sp.wait_ge(stored, 16 * G)


def build(nc, ins, out, upto=6, start=0):
    where_w, n_w = columns(WEIGHTS)
    n_early = where_w["l_g1"][0]
    where_c, n_c = columns(CONST)
    with ExitStack() as ctx:
        sb = lambda n, shape, dt=F32: ctx.enter_context(nc.sbuf_tensor(n, shape, dt))
        late, const = sb("late_weights", [P, n_w - n_early]), sb("const", [P, n_c])

        def weight(n):
            lo, hi = where_w[n]
            return early[:, lo:hi] if hi <= n_early else late[:, lo - n_early:hi - n_early]

        taken = []

        def semaphore(n):
            taken.append(nc.alloc_semaphore(name=n))
            return taken[-1]

        def phase_end():
            nc.clear_and_free_semaphores(taken)
            nc.all_engine_barrier()
            taken.clear()

        c = {
            "sem": semaphore,
            "w": weight, "const": lambda n: const[:, slice(*where_c[n])],
            "stream": sb("stream", [P, NT, P]), "moments": sb("moments", [P, NT, 2]), "rstd": sb("rstd", [P, NT]),
            "bq_scaled": sb("bq_scaled", [P, 1]), "ident16": sb("ident16", [P, P], BF16),
            "psum": ctx.enter_context(nc.psum_tensor("psum", [P, 8, 512], F32)),
            "l_mats": ins["l_mats"], "mask": ins["mask"],
            "ctx": ins["ctx"].rearrange("(n k) s d -> (k s) n d", k=2),
        }
        loaded = ctx.enter_context(nc.semaphore("loaded"))
        early_room = ExitStack()
        early = early_room.enter_context(nc.sbuf_tensor("early_weights", [P, n_early], F32))
        c["relbias"] = early_room.enter_context(nc.sbuf_tensor("relbias", [P, H, S], F32))
        with nc.Block() as block:
            @block.sync
            def _(sp):
                sp.dma_start(early[:, :], ins["weights"][:, 0:n_early]).then_inc(loaded, 16)
                sp.dma_start(late[:, :], ins["weights"][:, n_early:n_w]).then_inc(loaded, 16)
                sp.dma_start(c["stream"][:, :, :], ins["x"].rearrange("(n k) s d -> (k s) n d", k=2)).then_inc(loaded, 16)

            @block.scalar
            def _(act):
                act.dma_start(const[:, :], ins["const"]).then_inc(loaded, 16)
                act.dma_start(c["relbias"][:, :, :], ins["relbias"]).then_inc(loaded, 16)
                act.wait_ge(loaded, 80)
                nc.scalar.copy(c["ident16"][:, :], c["const"]("ident"))
                nc.scalar.mul(c["bq_scaled"][:, :], c["w"]("a_bq"), float(DH) ** -0.5)

            @block.vector
            def _(dve):
                nc.vector.memset(c["moments"][:, :, 0], 0.0)
                nc.vector.memset(c["moments"][:, :, 1], 1.0)
                nc.vector.memset(c["rstd"][:, :], 1.0)

        phases = [lambda x: attention_phase(nc, x, c, "a", False), lambda x: attention_phase(nc, x, c, "c", True),
                  lambda x: experts_phase(nc, x, c, "e"), lambda x: fourier_phase(nc, x, c, "f"),
                  lambda x: latents_phase(nc, x, c, "l"), lambda x: bitlinear_phase(nc, x, c, "b")]
        for n, phase in enumerate(phases[:upto]):
            if n == 4:
                early_room.close()
            if n < start:
                continue
            with ExitStack() as own:
                phase(own)
                norm_phase(nc, own, c, f"n{n}")
                phase_end()
        early_room.close()
        with ExitStack() as own:
            output_phase(nc, own, c, out)


def laid_out(inp):
    f = {k: np.asarray(v) for k, v in inp.items()}
    col = lambda v: np.reshape(v, (-1, 1))
    rows = lambda v: np.broadcast_to(np.reshape(v, (1, -1)), (P, np.size(v)))
    turned = lambda wt: wt.reshape(H, 2, DH // 2, P)[:, ::-1].reshape(P, P).T
    w = {
        "a_wq": f["L0_attn_Wq"].T, "a_wk": f["L0_attn_Wk"].T, "a_wv": f["L0_attn_Wv"].T, "a_wo": f["L0_attn_Wo"].T,
        "a_bq": col(f["L0_attn_bq"]), "a_bk": col(f["L0_attn_bk"]), "a_bv": rows(f["L0_attn_bv"]), "a_bo": rows(f["L0_attn_bo"]),
        "c_wq": f["L0_xattn_Wq"].T, "c_wqr": turned(f["L0_xattn_Wq"]), "c_wk": f["L0_xattn_Wk"].T,
        "c_wkr": turned(f["L0_xattn_Wk"]), "c_wv": f["L0_xattn_Wv"].T, "c_wo": f["L0_xattn_Wo"].T,
    }
    w["e_wr"] = f["L0_ffn_Wr"]
    w["e_w1"] = np.concatenate([np.moveaxis(f["L0_ffn_W1"], 0, 1).reshape(P, 512), f["L0_ffn_Ws1"]], 1)
    w2 = np.concatenate([f["L0_ffn_W2"].reshape(512, P), f["L0_ffn_Ws2"], np.zeros((64, P), np.float32)])
    w["e_w2"] = np.moveaxis(w2.reshape(5, P, P), 0, 1).reshape(P, 640)
    w["f_wq"], w["f_wk"], w["f_wv"] = f["L1_attn_Wq"].T, f["L1_attn_Wk"].T, f["L1_attn_Wv"].T
    w["f_bq"], w["f_bk"], w["f_bv"] = col(f["L1_attn_bq"]), col(f["L1_attn_bk"]), rows(f["L1_attn_bv"])
    w["f_proj"] = np.tile(f["L1_attn_proj_mat"], (H, 1))
    wo = np.zeros((2, 4, 4, 4, DH, P), np.float32)
    for par in range(2):
        wo[par, :, :, par] = f["L1_attn_Wo"].T.reshape(4, 4, DH, P)
    w["f_wo"] = np.moveaxis(wo.reshape(8, P, P), 0, 1).reshape(P, 1024)
    w["f_bo"] = col(f["L1_attn_bo"])
    for n in ("g1", "b1", "g2", "b2"):
        w[f"l_{n}"] = rows(f[f"L1_xattn_{n}"])
    w["b_w1"] = f["L1_ffn_w1"].T
    w["b_w2"] = np.moveaxis(f["L1_ffn_w2"].T.reshape(4, P, P), 0, 1).reshape(P, 512)
    w["b_n1"], w["b_n2"] = rows(f["L1_ffn_norm1_w"]), rows(f["L1_ffn_norm2_w"])
    w["b_as"], w["b_ab"] = rows(f["L1_ffn_act_scale"]), rows(f["L1_ffn_act_bias"])
    assert list(w) == list(WEIGHTS)
    by_pair = lambda a: np.moveaxis(a.reshape(PAIRS, P, P), 0, 1)
    kv = f["L1_xattn_Wkv"].T
    mats = np.stack([by_pair(f["L1_xattn_Wq"].T), by_pair(kv[:1024]), by_pair(kv[1024:]), by_pair(f["L1_xattn_Wout"])], 1)
    m = f["mask_BxS2_bk0"]
    mask = np.concatenate([m.reshape(NT, P).T, np.concatenate([m.T, np.ones((S, B), bool)])], 1)
    d = np.arange(P) % DH
    angle = np.outer(1.0 / 10000.0 ** (2 * (d % (DH // 2)) / DH), np.arange(S))
    t = {
        "ident": np.eye(P), "headmask": np.arange(P)[:, None] // DH == np.arange(H), "cos": np.cos(angle),
        "sin": np.where(d[:, None] < DH // 2, -np.sin(angle), np.sin(angle)),
    }
    q, kk = np.arange(P)[:, None] % S, np.arange(S)[None, :]
    return {
        "x": f["x"], "ctx": f["ctx_1024"],
        "weights": np.ascontiguousarray(np.concatenate([w[n] for n in WEIGHTS], 1)),
        "l_mats": np.ascontiguousarray(mats), "mask": np.ascontiguousarray(mask),
        "const": np.concatenate([np.asarray(t[n], np.float32) for n in CONST], 1),
        "relbias": np.ascontiguousarray(np.moveaxis(f["L0_attn_rel_bias"][:, np.clip(q - kk, -128, 128) + 128], 0, 1)),
    }


def kernel(**inputs):
    import concourse.bacc as bacc
    from concourse.bass_utils import run_bass_kernel_spmd

    nc = bacc.Bacc("TRN2", target_bir_lowering=False, num_devices=1)
    arrays = laid_out(inputs)
    ins = {n: nc.dram_tensor(f"in_{n}", a.shape, mybir.dt.from_np(a.dtype), kind="ExternalInput").ap() for n, a in arrays.items()}
    out = nc.dram_tensor("out", (B, S, P), F32, kind="ExternalOutput").ap()
    build(nc, ins, out)
    return run_bass_kernel_spmd(nc, [{f"in_{n}": a for n, a in arrays.items()}], core_ids=[0]).results[0]["out"]
```

```python
from contextlib import ExitStack

import numpy as np

import concourse.bass as bass
from concourse import mybir

F32 = mybir.dt.float32
BF16 = mybir.dt.bfloat16
I32 = mybir.dt.int32
ALU = mybir.AluOpType
ACT = mybir.ActivationFunctionType
AX = mybir.AxisListType

P = 128
S = 64
B = 64
H = 16
DH = 8
NT = B * S // P
T = 4
G = NT // T
GB = 2 * T
PAIRS = H // 2
VW = 2 * DH + 2
LN_EPS = 1e-5

CONST = {"ident": P, "headmask": H, "cos": S, "sin": S}
WEIGHTS = {
    "a_wq": P, "a_wk": P, "a_wv": P, "a_wo": P, "a_bq": 1, "a_bk": 1, "a_bv": P, "a_bo": P,
    "c_wq": P, "c_wqr": P, "c_wk": P, "c_wkr": P, "c_wv": P, "c_wo": P,
    "e_wr": 8, "e_w1": 576, "e_w2": 640,
    "f_wq": P, "f_wk": P, "f_wv": P, "f_bq": 1, "f_bk": 1, "f_bv": P, "f_proj": P, "f_wo": 1024, "f_bo": P,
    "l_g1": P, "l_b1": P, "l_g2": P, "l_b2": P,
    "b_w1": 512, "b_w2": 512, "b_n1": P, "b_n2": 512, "b_as": 1, "b_ab": 1,
}


def columns(widths):
    at, where = 0, {}
    for name, width in widths.items():
        where[name] = (at, at + width)
        at += width
    return where, at


class Count:

    def __init__(self, i, per):
        self.i, self.per = i, per

    def __call__(self, n):
        assert 1 <= n <= self.per
        return self.i * self.per + n


class Chain:

    def __init__(self, eng, sem, i, per):
        self.eng, self.sem, self.at, self.n = eng, sem, Count(i, per), 0

    def __call__(self, ins):
        self.n += 1
        ins.then_inc(self.sem, 1)
        self.eng.wait_ge(self.sem, self.at(self.n))


class Norm:

    def __init__(self, sb):
        self.sums, self.stats, self.moments = sb("sums", [P, T, P]), sb("stats", [P, T, 6]), sb("mom", [P, T, 2])


def residual_group(nc, c, norm, step, i, branch, x):
    step(nc.vector.tensor_tensor(norm.sums[:, :, :], branch, x, ALU.add))
    for t in range(T):
        last = nc.vector.bn_stats(norm.stats[:, t, :], norm.sums[:, t, :])
    step(last)
    nc.vector.tensor_scalar(c["stream"][:, bass.ds(i * T, T), :], norm.sums[:, :, :], 1.0, None, ALU.mult)
    for t in range(T):
        last = nc.vector.bn_aggr(norm.moments[:, t, :], norm.stats[:, t, :])
    step(last)
    return keep_moments(nc, c, norm, i)


def keep_moments(nc, c, norm, i):
    return nc.vector.tensor_scalar(c["moments"][:, bass.ds(i * T, T), :], norm.moments[:, :, :], 1.0, None, ALU.mult)


def attention_phase(nc, ctx, c, name, cross):
    sb = lambda n, shape, dt=F32: ctx.enter_context(nc.sbuf_tensor(f"{name}_{n}", shape, dt))
    sem = lambda n: c["sem"](f"{name}_{n}")
    w = c["w"]
    k = c["const"]
    stream, moments, rstd, ps = c["stream"], c["moments"], c["rstd"], c["psum"]
    pre = "c_" if cross else "a_"
    scale = float(DH) ** -0.5

    xs = sb("xs", [P, T, P])
    xT = sb("xT", [P, T * P])
    QT = sb("QT", [P, T * P])
    KT = sb("KT", [P, T * P])
    KX = sb("KX", [P, 2, 2, H, S])
    V2 = sb("V2", [P, GB, PAIRS, VW])
    prob = sb("prob", [P, 2, H, S])
    probT = sb("probT", [P, 2, PAIRS, P])
    top = sb("top", [P, 2, H])
    inv = sb("inv", [P, 2, H])
    ao = sb("ao", [P, 2, P])
    aoT = sb("aoT", [P, 2, P])
    norm = Norm(sb)
    if cross:
        cs = sb("cs", [P, T, P])
        cT = sb("cT", [P, T * P])
        ropes = sb("ropes", [P, 4, T * P])
        cstats, cmoments = sb("cstats", [P, T, 6]), sb("cmoments", [P, T, 2])

    names = ("staged xT_ps xT_sb proj_ps proj_sb v_ps v_sb kx scores softening shifted exped pT_ps pT_sb pv_ps inverse "
             "ao_ready aoT_ps aoT_sb out_ps steps v_zero v_ones").split()
    s = {n: sem(n) for n in names + ("ctx_in cT_sb cT_ps roped ctx_read measured moments_kept taken".split() if cross else [])}
    SOFTENING = 1 if cross else 2

    with nc.Block() as block:
        if cross:
            @block.sync
            def _(sp):
                sp.dma_start(cs[:, :, :], c["ctx"][:, 0:T, :]).then_inc(s["ctx_in"], 16)
                with sp.Fori(1, G) as i:
                    sp.wait_ge(s["cT_ps"], i)
                    sp.wait_ge(s["ctx_read"], i)
                    sp.dma_start(cs[:, :, :], c["ctx"][:, bass.ds(i * T, T), :]).then_inc(s["ctx_in"], 16)

        @block.tensor
        def _(pe):
            def columns_of(g):
                pe.wait_ge(s["staged"], Count(g, 1)(1))
                for t in range(T):
                    last = nc.tensor.transpose(ps[:, 0, t * P:(t + 1) * P], xs[:, t, :], k("ident"))
                last.then_inc(s["xT_ps"], 1)
                if cross:
                    pe.wait_ge(s["ctx_in"], Count(g, 16)(16))
                    for t in range(T):
                        last = nc.tensor.transpose(ps[:, 1, t * P:(t + 1) * P], cs[:, t, :], k("ident"))
                    last.then_inc(s["cT_ps"], 1)

            def project_in(g):
                pe.wait_ge(s["xT_sb"], Count(g, 1)(1))
                if cross:
                    pe.wait_ge(s["cT_sb"], Count(g, 1)(1))
                    for bank, (weight, columns) in enumerate((("c_wq", xT), ("c_wqr", xT), ("c_wk", cT), ("c_wkr", cT))):
                        last = nc.tensor.matmul(ps[:, bank, :], w(weight), columns[:, :], start=True, stop=True)
                else:
                    nc.tensor.matmul(ps[:, 1, :], w("a_wq"), xT[:, :], start=True, stop=True)
                    last = nc.tensor.matmul(ps[:, 0, :], w("a_wk"), xT[:, :], start=True, stop=True)
                last.then_inc(s["proj_ps"], 1)

            def values(g):
                if cross:
                    pe.wait_ge(s["roped"], Count(g, 1)(1))
                for b in range(GB):
                    for par in range(2):
                        last = nc.tensor.matmul(ps[par * S:(par + 1) * S, 2 + b // 4, (b % 4) * P:(b % 4 + 1) * P],
                                                (cT if cross else xT)[:, b * S:(b + 1) * S], w(pre + "wv"), start=True, stop=True)
                last.then_inc(s["v_ps"], 1)

            def scores(g, t):
                tile = Count(g, T)
                pe.wait_ge(s["kx"], tile(t + 1))
                if t == 0:
                    pe.wait_ge(s["proj_sb"], Count(g, 2)(2))
                elif t == 1:
                    pe.wait_ge(s["v_sb"], Count(g, 1)(1))
                else:
                    pe.wait_ge(s["shifted"], tile(t - 1))
                for half in range(2):
                    for b in range(2):
                        last = nc.tensor.matmul(
                            ps[b * S:(b + 1) * S, 2 * (t % 2) + half, :], QT[:, t * P + b * S:t * P + (b + 1) * S],
                            KX[:, t % 2, b, half * 8:half * 8 + 8, :], start=True, stop=True)
                last.then_inc(s["scores"], 1)

            def turn_probs(g, t):
                pe.wait_ge(s["exped"], Count(g, T)(t + 1))
                if t >= 1:
                    pe.wait_ge(s["pT_sb"], Count(g, T)(t))
                for j in range(PAIRS):
                    last = nc.tensor.transpose(ps[:, 4 + j // 4, (j % 4) * P:(j % 4 + 1) * P],
                                               prob[:, t % 2, 2 * j:2 * j + 2, :], k("ident"))
                last.then_inc(s["pT_ps"], 1)

            def turn_out(g, t):
                pe.wait_ge(s["ao_ready"], Count(g, T)(t + 1))
                nc.tensor.transpose(ps[:, 6, 256:256 + P], ao[:, t % 2, :], k("ident")).then_inc(s["aoT_ps"], 1)

            def project_out(g, t):
                pe.wait_ge(s["aoT_sb"], Count(g, T)(t + 1))
                last = nc.tensor.matmul(ps[:, 7, t * P:(t + 1) * P], aoT[:, t % 2, :], w(pre + "wo"), start=True, stop=True)
                if t == T - 1:
                    last.then_inc(s["out_ps"], 1)

            def weigh(g, t):
                pe.wait_ge(s["pT_sb"], Count(g, T)(t + 1))
                for j in range(PAIRS):
                    for b in range(2):
                        last = nc.tensor.matmul(ps[b * S:(b + 1) * S, 6, j * VW:(j + 1) * VW],
                                                probT[:, t % 2, j, b * S:(b + 1) * S],
                                                V2[:, 2 * t + b, j, :], start=True, stop=True)
                last.then_inc(s["pv_ps"], 1)

            def main(g, ahead):
                for t in range(T):
                    turn_probs(g, t)
                    if t == T - 2 and ahead:
                        columns_of(g + 1)
                    if t + 2 < T:
                        scores(g, t + 2)
                    if t == T - 1 and ahead and cross:
                        project_in(g + 1)
                    if t >= 1:
                        turn_out(g, t - 1)
                    if t == T - 1 and ahead and not cross:
                        values(g + 1)
                    if t >= 1:
                        project_out(g, t - 1)
                    if t == T - 2 and ahead and not cross:
                        project_in(g + 1)
                    weigh(g, t)
                if ahead and cross:
                    values(g + 1)
                turn_out(g, T - 1)
                project_out(g, T - 1)
                if ahead:
                    scores(g + 1, 0)
                    scores(g + 1, 1)

            pe.wait_ge(s["v_ones"], 1)
            columns_of(0)
            project_in(0)
            values(0)
            scores(0, 0)
            scores(0, 1)
            with pe.Fori(0, G - 1) as g:
                main(g, True)
            main(G - 1, False)

        @block.scalar
        def _(act):
            def columns_of(g):
                act.wait_ge(s["xT_ps"], Count(g, 1)(1))
                nc.scalar.copy(xT[:, :], ps[:, 0, :]).then_inc(s["xT_sb"], 1)
                if cross:
                    act.wait_ge(s["cT_ps"], Count(g, 1)(1))
                    nc.scalar.copy(cT[:, :], ps[:, 1, :]).then_inc(s["cT_sb"], 1)

            def project_in(g):
                if not cross:
                    act.wait_ge(s["proj_ps"], Count(g, 1)(1))
                    nc.scalar.activation(KT[:, :], ps[:, 0, :], ACT.Identity, bias=w("a_bk")).then_inc(s["proj_sb"], 1)
                    nc.scalar.activation(QT[:, :], ps[:, 1, :], ACT.Identity, bias=c["bq_scaled"][:, :],
                                         scale=scale).then_inc(s["proj_sb"], 1)

            def exponent(g, t):
                act.wait_ge(s["shifted"], Count(g, T)(t + 1))
                nc.scalar.activation(prob[:, t % 2, :, :], prob[:, t % 2, :, :], ACT.Exp,
                                     scale=scale if cross else 1.0).then_inc(s["exped"], 1)

            def turned_probs(g, t):
                act.wait_ge(s["pT_ps"], Count(g, T)(t + 1))
                nc.scalar.copy(probT[:, t % 2, :, :], ps[:, 4:6, :].rearrange("p a (b q) -> p (a b) q", b=4)
                               ).then_inc(s["pT_sb"], 1)

            def turned_out(g, t):
                act.wait_ge(s["aoT_ps"], Count(g, T)(t + 1))
                nc.scalar.copy(aoT[:, t % 2, :], ps[:, 6, 256:256 + P]).then_inc(s["aoT_sb"], 1)

            def main(g, ahead):
                for t in range(T):
                    turned_probs(g, t)
                    if t == T - 2 and ahead:
                        columns_of(g + 1)
                    if t >= 1:
                        turned_out(g, t - 1)
                    if t + 1 < T:
                        exponent(g, t + 1)
                    if t == T - 2 and ahead:
                        project_in(g + 1)
                turned_out(g, T - 1)
                if ahead:
                    exponent(g + 1, 0)

            columns_of(0)
            project_in(0)
            exponent(0, 0)
            with act.Fori(0, G - 1) as g:
                main(g, True)
            main(G - 1, False)

        @block.vector
        def _(dve):
            def stage(g):
                for t in range(T):
                    tile = g * T + t
                    last = nc.vector.tensor_scalar(xs[:, t, :], stream[:, bass.ds(tile, 1), :],
                                                   moments[:, bass.ds(tile, 1), 0], rstd[:, bass.ds(tile, 1)],
                                                   ALU.subtract, ALU.mult)
                last.then_inc(s["staged"], 1)
                dve.wait_ge(s["staged"], Count(g, 1)(1))
                if cross:
                    nc.vector.tensor_scalar(stream[:, bass.ds(g * T, T), :], xs[:, :, :], 1.0, None, ALU.mult)
                else:
                    nc.vector.tensor_tensor(stream[:, bass.ds(g * T, T), :], xs[:, :, :],
                                            w("a_bo").unsqueeze(1).to_broadcast([P, T, P]), ALU.add)

            def measure(g):
                dve.wait_ge(s["ctx_in"], Count(g, 16)(16))
                dve.sem_inc(s["taken"], 1)
                for t in range(T):
                    last = nc.vector.bn_stats(cstats[:, t, :], cs[:, t, :])
                last.then_inc(s["ctx_read"], 1)
                dve.wait_ge(s["ctx_read"], Count(g, 1)(1))
                dve.sem_inc(s["taken"], 1)
                for t in range(T):
                    last = nc.vector.bn_aggr(cmoments[:, t, :], cstats[:, t, :])
                last.then_inc(s["measured"], 1)
                dve.wait_ge(s["measured"], Count(g, 1)(1))
                nc.vector.tensor_scalar(c["ctx_moments"][:, bass.ds(g * T, T), :], cmoments[:, :, :], 1.0, None, ALU.mult
                                        ).then_inc(s["moments_kept"], 1)

            def rope(g):
                dve.wait_ge(s["proj_ps"], Count(g, 1)(1))
                for n, tab in enumerate(("cos", "sin", "cos", "sin")):
                    last = nc.vector.tensor_tensor(
                        ropes[:, n, :].rearrange("p (b s) -> p b s", s=S), ps[:, n, :].rearrange("p (b s) -> p b s", s=S),
                        k(tab).unsqueeze(1).to_broadcast([P, GB, S]), ALU.mult)
                last.then_inc(s["roped"], 1)

            def values(g):
                dve.wait_ge(s["v_ps"], Count(g, 1)(1))
                for q in range(2):
                    for par in range(2):
                        src = ps[par * S:(par + 1) * S, 2 + q, :].rearrange("p (b j e d) -> p b j e d", b=4, e=2, d=DH)[:, :, :, par, :]
                        dst = V2[par * S:(par + 1) * S, 4 * q:4 * q + 4, :, par * DH:(par + 1) * DH]
                        if cross:
                            last = nc.vector.tensor_copy(dst, src)
                        else:
                            bv = w("a_bv")[par * S:(par + 1) * S, :].rearrange("p (j e d) -> p j e d", e=2, d=DH)[:, :, par, :]
                            last = nc.vector.tensor_tensor(dst, src, bv.unsqueeze(1).to_broadcast([S, 4, PAIRS, DH]), ALU.add)
                last.then_inc(s["v_sb"], 1)

            def soften(g, t):
                step = Chain(dve, s["softening"], g * T + t, SOFTENING)
                dve.wait_ge(s["scores"], Count(g, T)(t + 1))
                if t >= 2:
                    dve.wait_ge(s["pT_ps"], Count(g, T)(t - 1))
                sc = ps[:, 2 * (t % 2):2 * (t % 2) + 2, :].rearrange("p a (h q) -> p (a h) q", q=S)
                if not cross:
                    step(nc.vector.tensor_tensor(prob[:, t % 2, :, :], sc, c["relbias"][:, :, :], ALU.add))
                    sc = prob[:, t % 2, :, :]
                step(nc.vector.tensor_reduce(top[:, t % 2, :], sc, AX.X, ALU.max))
                nc.vector.tensor_tensor(prob[:, t % 2, :, :], sc, top[:, t % 2, :].unsqueeze(2).to_broadcast([P, H, S]),
                                        ALU.subtract).then_inc(s["shifted"], 1)

            def divide(g, t):
                dve.wait_ge(s["pv_ps"], Count(g, T)(t + 1))
                pv = ps[:, 6, 0:PAIRS * VW].rearrange("p (j v) -> p j v", v=VW)
                nc.vector.reciprocal(inv[:, t % 2, :].rearrange("p (j e) -> p j e", e=2), pv[:, :, 2 * DH:VW]
                                     ).then_inc(s["inverse"], 1)
                dve.wait_ge(s["inverse"], Count(g, T)(t + 1))
                nc.vector.tensor_tensor(
                    ao[:, t % 2, :].rearrange("p (j e d) -> p j e d", e=2, d=DH),
                    pv[:, :, 0:2 * DH].rearrange("p j (e d) -> p j e d", e=2),
                    inv[:, t % 2, :].rearrange("p (j e) -> p j e", e=2).unsqueeze(3).to_broadcast([P, PAIRS, 2, DH]),
                    ALU.mult).then_inc(s["ao_ready"], 1)

            def main(g, ahead):
                for t in range(T):
                    if t + 2 < T:
                        soften(g, t + 2)
                    if t == T - 1 and ahead and cross:
                        rope(g + 1)
                    divide(g, t)
                    if t == 0 and ahead:
                        stage(g + 1)
                    if t == 1 and ahead and cross:
                        measure(g + 1)
                if ahead:
                    values(g + 1)
                dve.wait_ge(s["out_ps"], Count(g, 1)(1))
                residual_group(nc, c, norm, Chain(dve, s["steps"], g, 3), g, ps[:, 7, :].rearrange("p (t d) -> p t d", d=P),
                               stream[:, bass.ds(g * T, T), :])
                if ahead:
                    soften(g + 1, 0)
                    soften(g + 1, 1)

            nc.vector.memset(V2[:, :, :, :], 0.0).then_inc(s["v_zero"], 1)
            dve.wait_ge(s["v_zero"], 1)
            nc.vector.memset(V2[0:S, :, :, 2 * DH:2 * DH + 1], 1.0)
            nc.vector.memset(V2[S:P, :, :, 2 * DH + 1:VW], 1.0).then_inc(s["v_ones"], 1)
            dve.wait_ge(s["v_ones"], 1)
            stage(0)
            if cross:
                rope(0)
                measure(0)
            values(0)
            soften(0, 0)
            soften(0, 1)
            with dve.Fori(0, G - 1) as g:
                main(g, True)
            main(G - 1, False)

        @block.gpsimd
        def _(pool):
            def keys(g, t):
                if t == 0:
                    if cross:
                        pool.wait_ge(s["roped"], Count(g, 1)(1))
                        nc.gpsimd.tensor_tensor(KT[:, :], ropes[:, 2, :], ropes[:, 3, :], ALU.add).then_inc(s["proj_sb"], 1)
                        nc.gpsimd.tensor_tensor(QT[:, :], ropes[:, 0, :], ropes[:, 1, :], ALU.add).then_inc(s["proj_sb"], 1)
                    pool.wait_ge(s["proj_sb"], Count(g, 2)(1))
                if t >= 2:
                    pool.wait_ge(s["scores"], Count(g, T)(t - 1))
                nc.gpsimd.tensor_tensor(
                    KX[:, t % 2, :, :, :],
                    KT[:, t * P:(t + 1) * P].rearrange("p (b s) -> p b s", s=S).unsqueeze(2).to_broadcast([P, 2, H, S]),
                    k("headmask").unsqueeze(1).unsqueeze(3).to_broadcast([P, 2, H, S]), ALU.mult).then_inc(s["kx"], 1)

            def main(g, ahead):
                for t in range(2, T):
                    keys(g, t)
                if ahead:
                    pool.wait_ge(s["scores"], Count(g, T)(T))
                    keys(g + 1, 0)
                    keys(g + 1, 1)

            keys(0, 0)
            keys(0, 1)
            with pool.Fori(0, G - 1) as g:
                main(g, True)
            main(G - 1, False)


def stage_tiles(nc, c, xs, i):
    for t in range(T):
        tile = i * T + t
        last = nc.vector.tensor_scalar(xs[:, t, :], c["stream"][:, bass.ds(tile, 1), :], c["moments"][:, bass.ds(tile, 1), 0],
                                       c["rstd"][:, bass.ds(tile, 1)], ALU.subtract, ALU.mult)
    return last


def experts_phase(nc, ctx, c, name):
    sb = lambda n, shape, dt=F32: ctx.enter_context(nc.sbuf_tensor(f"{name}_{n}", shape, dt))
    s = {n: c["sem"](f"{name}_{n}") for n in (
        "staged xT_ps xT_sb logits_ps pad_zero gap expgap prob up pick relu_done gated hidden down_ps down_sb y_ps "
        "steps router_steps").split()}
    w, ps = c["w"], c["psum"]
    E, F = 8, 64
    C = E * F // P
    xs, xT, norm = sb("xs", [P, T, P]), sb("xT", [P, T * P]), Norm(sb)
    logits, best, gap = sb("logits", [P, T, E]), sb("best", [P, T, E]), sb("gap", [P, T])
    chosen, prob = sb("chosen", [P, T, E]), sb("prob", [P, T, E, F], BF16)
    relu, gated, hid = sb("relu", [P, 2, T * P]), sb("gated", [P, 2, T * P]), sb("hid", [P, C + 1, T * P])
    yT = sb("yT", [P, T * P])

    with nc.Block() as block:
        @block.tensor
        def _(pe):
            def columns_of(g):
                pe.wait_ge(s["staged"], Count(g, 1)(1))
                for t in range(T):
                    last = nc.tensor.transpose(ps[:, 0, t * P:(t + 1) * P], xs[:, t, :], c["const"]("ident"))
                last.then_inc(s["xT_ps"], 1)

            def route(g):
                pe.wait_ge(s["xT_sb"], Count(g, 1)(1))
                for t in range(T):
                    last = nc.tensor.matmul(ps[:, 1, t * E:(t + 1) * E], xT[:, t * P:(t + 1) * P], w("e_wr"), start=True, stop=True)
                last.then_inc(s["logits_ps"], 1)

            def raise_(g, n):
                if n >= 2:
                    pe.wait_ge(s["relu_done"], Count(g, C + 1)(n - 1))
                rows = P if n < C else F
                nc.tensor.matmul(ps[0:rows, 2 + n % 2, :], w("e_w1")[:, n * P:n * P + rows], xT[:, :],
                                 start=True, stop=True).then_inc(s["up"], 1)

            def pick(g, n):
                if n == 0:
                    pe.wait_ge(s["prob"], Count(g, 1)(1))
                if n >= 2:
                    pe.wait_ge(s["gated"], Count(g, C)(n - 1))
                for t in range(T):
                    last = nc.tensor.matmul(ps[:, 4 + n % 2, t * P:(t + 1) * P], prob[:, t, 2 * n:2 * n + 2, :],
                                            c["ident16"][:, :], start=True, stop=True)
                last.then_inc(s["pick"], 1)

            def lower(g, n):
                pe.wait_ge(s["hidden"], Count(g, C + 1)(n + 1))
                last = nc.tensor.matmul(ps[:, 6, :], w("e_w2")[:, n * P:(n + 1) * P], hid[:, n, :], start=(n == 0), stop=(n == C))
                if n == C:
                    last.then_inc(s["down_ps"], 1)

            def start(g):
                raise_(g, 0)
                raise_(g, 1)

            def main(g, ahead):
                pick(g, 0)
                pick(g, 1)
                for n in range(C + 1):
                    if n + 2 < C + 1:
                        raise_(g, n + 2)
                    if n + 2 < C:
                        pick(g, n + 2)
                    if ahead and n == 2:
                        columns_of(g + 1)
                    lower(g, n)
                    if ahead and n == 2:
                        route(g + 1)
                if ahead:
                    start(g + 1)
                pe.wait_ge(s["down_sb"], Count(g, 1)(1))
                for t in range(T):
                    last = nc.tensor.transpose(ps[:, 7, t * P:(t + 1) * P], yT[:, t * P:(t + 1) * P], c["const"]("ident"))
                last.then_inc(s["y_ps"], 1)

            pe.wait_ge(s["pad_zero"], 1)
            columns_of(0)
            route(0)
            start(0)
            with pe.Fori(0, G - 1) as g:
                main(g, True)
            main(G - 1, False)

        @block.scalar
        def _(act):
            def columns_of(g):
                act.wait_ge(s["xT_ps"], Count(g, 1)(1))
                nc.scalar.copy(xT[:, :], ps[:, 0, :]).then_inc(s["xT_sb"], 1)

            def exponent(g):
                act.wait_ge(s["gap"], Count(g, 1)(1))
                nc.scalar.activation(gap[:, :], gap[:, :], ACT.Exp).then_inc(s["expgap"], 1)

            def relu_of(g, n):
                rows = P if n < C else F
                act.wait_ge(s["up"], Count(g, C + 1)(n + 1))
                if n >= 2:
                    act.wait_ge(s["gated"], Count(g, C)(n - 1))
                nc.scalar.activation(relu[0:rows, n % 2, :], ps[0:rows, 2 + n % 2, :], ACT.Relu).then_inc(s["relu_done"], 1)

            def square_of(g, n):
                if n < C:
                    act.wait_ge(s["gated"], Count(g, C)(n + 1))
                    nc.scalar.activation(hid[:, n, :], gated[:, n % 2, :], ACT.Square).then_inc(s["hidden"], 1)
                else:
                    act.wait_ge(s["relu_done"], Count(g, C + 1)(C + 1))
                    nc.scalar.activation(hid[0:F, n, :], relu[0:F, n % 2, :], ACT.Square).then_inc(s["hidden"], 1)

            def main(g, ahead):
                relu_of(g, 1)
                for n in range(C + 1):
                    if 1 <= n and n + 1 <= C:
                        relu_of(g, n + 1)
                    square_of(g, n)
                    if ahead and n == 2:
                        columns_of(g + 1)
                    if ahead and n == 3:
                        exponent(g + 1)
                act.wait_ge(s["down_ps"], Count(g, 1)(1))
                nc.scalar.copy(yT[:, :], ps[:, 6, :]).then_inc(s["down_sb"], 1)
                if ahead:
                    relu_of(g + 1, 0)

            columns_of(0)
            relu_of(0, 0)
            exponent(0)
            with act.Fori(0, G - 1) as g:
                main(g, True)
            main(G - 1, False)

        @block.vector
        def _(dve):
            nc.vector.memset(hid[:, C, :], 0.0).then_inc(s["pad_zero"], 1)
            def stage(g):
                stage_tiles(nc, c, xs, g).then_inc(s["staged"], 1)
                dve.wait_ge(s["staged"], Count(g, 1)(1))
                nc.vector.tensor_scalar(c["stream"][:, bass.ds(g * T, T), :], xs[:, :, :], 1.0, None, ALU.mult)

            def route(g):
                step = Chain(dve, s["router_steps"], g, 5)
                dve.wait_ge(s["logits_ps"], Count(g, 1)(1))
                nc.vector.tensor_scalar(logits[:, :, :], ps[:, 1, 0:T * E].rearrange("p (t e) -> p t e", e=E), 1.0, None, ALU.mult)
                for t in range(T):
                    last = nc.vector.max(best[:, t, :], ps[:, 1, t * E:(t + 1) * E])
                step(last)
                nc.vector.tensor_tensor(gap[:, :], best[:, :, 1], best[:, :, 0], ALU.subtract).then_inc(s["gap"], 1)
                step(nc.vector.tensor_tensor(chosen[:, :, :], logits[:, :, :], best[:, :, 0:1].to_broadcast([P, T, E]), ALU.is_equal))
                dve.wait_ge(s["expgap"], Count(g, 1)(1))
                step(nc.vector.tensor_scalar(gap[:, :], gap[:, :], 1.0, None, ALU.add))
                step(nc.vector.reciprocal(gap[:, :], gap[:, :]))
                step(nc.vector.tensor_scalar(gap[:, :], gap[:, :], 1.0, None, ALU.is_ge))
                nc.vector.tensor_tensor(prob[:, :, :, :], chosen[:, :, :].unsqueeze(3).to_broadcast([P, T, E, F]),
                                        gap[:, :].unsqueeze(2).unsqueeze(3).to_broadcast([P, T, E, F]), ALU.mult).then_inc(s["prob"], 1)

            def main(g, ahead):
                for n in range(C):
                    if ahead and n == 1:
                        stage(g + 1)
                    dve.wait_ge(s["relu_done"], Count(g, C + 1)(n + 1))
                    dve.wait_ge(s["pick"], Count(g, C)(n + 1))
                    if n >= 2:
                        dve.wait_ge(s["hidden"], Count(g, C + 1)(n - 1))
                    nc.vector.tensor_tensor(gated[:, n % 2, :], ps[:, 4 + n % 2, :], relu[:, n % 2, :], ALU.mult).then_inc(s["gated"], 1)
                if ahead:
                    route(g + 1)
                dve.wait_ge(s["y_ps"], Count(g, 1)(1))
                residual_group(nc, c, norm, Chain(dve, s["steps"], g, 3), g, ps[:, 7, :].rearrange("p (t d) -> p t d", d=P),
                               c["stream"][:, bass.ds(g * T, T), :])

            stage(0)
            route(0)
            with dve.Fori(0, G - 1) as g:
                main(g, True)
            main(G - 1, False)


def fourier_phase(nc, ctx, c, name):
    sb = lambda n, shape, dt=F32: ctx.enter_context(nc.sbuf_tensor(f"{name}_{n}", shape, dt))
    s = {n: c["sem"](f"{name}_{n}") for n in (
        "consts staged xT_ps xT_sb k_ps k_sb v_ps v_sb q_ps q_sb z_ps reduced rounded wrapped feats kv_ps kv_sb kvT_ps kvT_sb o_ps o_sb "
        "y_ps yT_sb yt_ps steps out_read").split()}
    w, ps = c["w"], c["psum"]
    M = 128
    Q4 = H // 4
    UNIT = 1024
    KU = H * M // UNIT
    UPG = T * KU + Q4 * 2
    MAGIC = 1.5 * 2.0 ** 23
    TWO_PI, HALF_PI = 6.2831850, 1.5707962
    xs, xT, norm = sb("xs", [P, T, P]), sb("xT", [P, T * P]), Norm(sb)
    qT, kT = sb("qT", [P, T * P]), sb("kT", [P, T * P])
    projX = sb("projX", [P, H, M])
    vS = sb("vS", [P, T, H, 32])
    whole, frac, wrap = sb("whole", [P, UNIT]), sb("frac", [P, 2, UNIT]), sb("wrap", [P, 2, UNIT])
    feats = sb("feats", [P, 2, 8, 2, M])
    qf = sb("qf", [P, 2, 4, 2, T * P])
    kvs = sb("kvs", [P, Q4, 2, M])
    kvm = sb("kvm", [P, T, Q4, 2, P])
    oT, yT = sb("oT", [P, Q4, T * P]), sb("yT", [P, T * P])
    half_pi, qb, vb = sb("half_pi", [P, 1]), sb("qb", [P, 1]), sb("vb", [P, P])
    kb = sb("kb", [P, 1])
    turn_scale = float(DH) ** -0.5 / (2 * np.pi)

    with nc.Block() as block:
        @block.tensor
        def _(pe):
            def columns_of(g):
                pe.wait_ge(s["staged"], Count(g, 1)(1))
                for t in range(T):
                    last = nc.tensor.transpose(ps[:, 6, t * P:(t + 1) * P], xs[:, t, :], c["const"]("ident"))
                last.then_inc(s["xT_ps"], 1)

            def keys_and_values(g):
                pe.wait_ge(s["xT_sb"], Count(g, 1)(1))
                nc.tensor.matmul(ps[:, 7, :], w("f_wk"), xT[:, :], start=True, stop=True).then_inc(s["k_ps"], 1)
                for t in range(T):
                    last = nc.tensor.matmul(ps[:, 6, t * P:(t + 1) * P], xT[:, t * P:(t + 1) * P], w("f_wv"), start=True, stop=True)
                last.then_inc(s["v_ps"], 1)

            def queries(g):
                pe.wait_ge(s["k_sb"], Count(g, 1)(1))
                nc.tensor.matmul(ps[:, 7, :], w("f_wq"), xT[:, :], start=True, stop=True).then_inc(s["q_ps"], 1)

            def angles(g, n):
                unit = Count(g, UPG)
                if n == 0:
                    pe.wait_ge(s["k_sb"], Count(g, 1)(1))
                if n == T * KU:
                    pe.wait_ge(s["q_sb"], Count(g, 1)(1))
                if n >= 2:
                    pe.wait_ge(s["reduced"], unit(n - 1))
                for q in range(2):
                    out = ps[:, 2 * (n % 2) + q, :]
                    if n < T * KU:
                        t, u = divmod(n, KU)
                        h = u * 8 + q * 4
                        last = nc.tensor.matmul(out, kT[:, t * P:(t + 1) * P], projX[:, h:h + 4, :], start=True, stop=True)
                    else:
                        last = nc.tensor.matmul(out, projX[:, 2 * (n - T * KU) + q, :], qT[:, :], start=True, stop=True)
                last.then_inc(s["z_ps"], 1)

            def key_values(g, t, u):
                if t >= 1 and u == 0:
                    pe.wait_ge(s["kv_sb"], Count(g, T)(t))
                pe.wait_ge(s["feats"], Count(g, UPG)(t * KU + u + 1))
                if t == 0 and u == 0:
                    pe.wait_ge(s["v_sb"], Count(g, 1)(1))
                for h in range(8 * u, 8 * u + 8):
                    q, r = divmod(h, 4)
                    last = nc.tensor.matmul(ps[32 * r:32 * r + 32, 4 + q // 2, (q % 2) * 256:(q % 2 + 1) * 256],
                                            vS[:, t, h, :], feats[:, (t * KU + u) % 2, h % 8, :, :], start=True, stop=True)
                if u == KU - 1:
                    last.then_inc(s["kv_ps"], 1)

            def turn_key_values(g, t):
                pe.wait_ge(s["kv_sb"], Count(g, T)(t + 1))
                if t >= 1:
                    pe.wait_ge(s["kvT_sb"], Count(g, T)(t))
                for q in range(Q4):
                    for e in range(2):
                        n = 2 * q + e
                        last = nc.tensor.transpose(ps[:, 6 + n // 4, (n % 4) * P:(n % 4 + 1) * P], kvs[:, q, e, :], c["const"]("ident"))
                last.then_inc(s["kvT_ps"], 1)

            def outputs(g, q):
                pe.wait_ge(s["feats"], Count(g, UPG)(T * KU + 2 * q + 2))
                if q == 0:
                    pe.wait_ge(s["kvT_sb"], Count(g, T)(T))
                if q >= 2:
                    pe.wait_ge(s["o_sb"], Count(g, Q4)(q - 1))
                for t in range(T):
                    for e in range(2):
                        for r in range(4):
                            last = nc.tensor.matmul(ps[32 * r:32 * r + 32, 4 + q % 2, t * P:(t + 1) * P],
                                                    kvm[:, t, q, e, 32 * r:32 * r + 32], qf[:, q % 2, r, e, t * P:(t + 1) * P],
                                                    start=(e == 0), stop=(e == 1))
                last.then_inc(s["o_ps"], 1)

            def combine(g):
                for par in range(2):
                    for q in range(Q4):
                        if par == 0:
                            pe.wait_ge(s["o_sb"], Count(g, Q4)(q + 1))
                        at = (par * Q4 + q) * P
                        toks = oT[:, q, :].rearrange("p (t b s) -> p t b s", b=2, s=S)[:, :, par, :]
                        last = nc.tensor.matmul(ps[:, 6, par * 256:(par + 1) * 256], w("f_wo")[:, at:at + P], toks,
                                                start=(q == 0), stop=(q == Q4 - 1))
                last.then_inc(s["y_ps"], 1)

            def turn_back(g):
                pe.wait_ge(s["yT_sb"], Count(g, 1)(1))
                for t in range(T):
                    last = nc.tensor.transpose(ps[:, 7, t * P:(t + 1) * P], yT[:, t * P:(t + 1) * P], c["const"]("ident"))
                last.then_inc(s["yt_ps"], 1)

            def main(g, ahead):
                for t in range(1, T):
                    angles(g, 2 * t + 2)
                    key_values(g, t, 0)
                    angles(g, 2 * t + 3)
                    key_values(g, t, 1)
                    turn_key_values(g, t - 1)
                for q in range(Q4):
                    for n in (T * KU + 2 * q + 2, T * KU + 2 * q + 3):
                        if n < UPG:
                            angles(g, n)
                        elif ahead:
                            pe.wait_ge(s["reduced"], Count(g, UPG)(n - 1))
                            angles(g + 1, n - UPG)
                    if q == 0:
                        turn_key_values(g, T - 1)
                    if ahead and q == 0:
                        pe.wait_ge(s["kvT_sb"], Count(g, T)(T))
                        columns_of(g + 1)
                    if ahead and q == 1:
                        keys_and_values(g + 1)
                    if ahead and q == 2:
                        queries(g + 1)
                    outputs(g, q)
                if ahead:
                    angles(g + 1, 2)
                    pe.wait_ge(s["v_sb"], Count(g + 1, 1)(1))
                    pe.wait_ge(s["q_sb"], Count(g + 1, 1)(1))
                combine(g)
                if ahead:
                    key_values(g + 1, 0, 0)
                turn_back(g)
                if ahead:
                    angles(g + 1, 3)
                    key_values(g + 1, 0, 1)
                    pe.wait_ge(s["out_read"], Count(g, 1)(1))

            pe.wait_ge(s["consts"], 6)
            columns_of(0)
            keys_and_values(0)
            queries(0)
            for n in range(4):
                angles(0, n)
                if n >= 2:
                    key_values(0, 0, n - 2)
            with pe.Fori(0, G - 1) as g:
                main(g, True)
            main(G - 1, False)

        @block.scalar
        def _(act):
            nc.scalar.mul(qb[:, :], w("f_bq"), turn_scale).then_inc(s["consts"], 1)
            nc.scalar.mul(kb[:, :], w("f_bk"), turn_scale).then_inc(s["consts"], 1)
            nc.scalar.mul(vb[:, :], w("f_bv"), 1.0 / M).then_inc(s["consts"], 1)
            act.wait_ge(s["consts"], 6)
            def columns_of(g):
                act.wait_ge(s["xT_ps"], Count(g, 1)(1))
                nc.scalar.copy(xT[:, :], ps[:, 6, :]).then_inc(s["xT_sb"], 1)

            def features(g, n):
                unit = Count(g, UPG)
                act.wait_ge(s["reduced"], unit(n + 1))
                if n < T * KU:
                    if n >= 2 and n % KU == 0:
                        act.wait_ge(s["kv_ps"], Count(g, T)(n // KU))
                    sin, cos = feats[:, n % 2, :, 1, :], feats[:, n % 2, :, 0, :]
                    view = lambda a: a.rearrange("p (h m) -> p h m", m=M)
                else:
                    v = n - T * KU
                    if v >= 4 and v % 2 == 0:
                        act.wait_ge(s["o_ps"], Count(g, Q4)(v // 2 - 1))
                    h = (v % 2) * 2
                    sin, cos = qf[:, (v // 2) % 2, h:h + 2, 1, :], qf[:, (v // 2) % 2, h:h + 2, 0, :]
                    view = lambda a: a.rearrange("p (h m) -> p h m", h=2)
                nc.scalar.activation(sin, view(frac[:, n % 2, :]), ACT.Sin, scale=TWO_PI)
                act.wait_ge(s["wrapped"], unit(n + 1))
                nc.scalar.activation(cos, view(wrap[:, n % 2, :]), ACT.Sin, bias=half_pi[:, :], scale=-TWO_PI).then_inc(s["feats"], 1)

            def keep_kv(g, t):
                act.wait_ge(s["kv_ps"], Count(g, T)(t + 1))
                if t >= 1:
                    act.wait_ge(s["kvT_ps"], Count(g, T)(t))
                nc.scalar.copy(kvs[:, :, :, :], ps[:, 4:6, :].rearrange("p a (b e m) -> p (a b) e m", b=2, e=2)).then_inc(s["kv_sb"], 1)

            def keep_o(g, q):
                act.wait_ge(s["o_ps"], Count(g, Q4)(q + 1))
                nc.scalar.copy(oT[:, q, :], ps[:, 4 + q % 2, :]).then_inc(s["o_sb"], 1)

            def keep_turned(g, t):
                act.wait_ge(s["kvT_ps"], Count(g, T)(t + 1))
                nc.scalar.copy(kvm[:, t, :, :, :], ps[:, 6:8, :].rearrange("p a (b e m) -> p (a b) e m", b=2, e=2)).then_inc(s["kvT_sb"], 1)

            def main(g, ahead):
                for n in range(2, UPG):
                    features(g, n)
                    if n <= T * KU and n % 2 == 0:
                        keep_kv(g, n // 2 - 1)
                        if n >= 4:
                            keep_turned(g, n // 2 - 2)
                    if n == T * KU + 1:
                        keep_turned(g, T - 1)
                    if ahead and n == T * KU + 1:
                        columns_of(g + 1)
                    if n >= T * KU + 3 and n % 2 == 1:
                        keep_o(g, (n - T * KU - 3) // 2)
                if ahead:
                    features(g + 1, 0)
                keep_o(g, Q4 - 1)
                act.wait_ge(s["y_ps"], Count(g, 1)(1))
                nc.scalar.copy(yT[:, :].rearrange("p (t b s) -> p b t s", b=2, s=S),
                               ps[:, 6, :].rearrange("p (b t s) -> p b t s", b=2, s=S)).then_inc(s["yT_sb"], 1)
                if ahead:
                    features(g + 1, 1)

            columns_of(0)
            features(0, 0)
            features(0, 1)
            with act.Fori(0, G - 1) as g:
                main(g, True)
            main(G - 1, False)

        @block.vector
        def _(dve):
            nc.vector.memset(half_pi[:, :], HALF_PI).then_inc(s["consts"], 1)
            nc.vector.memset(vS[:, :, :, :], 0.0).then_inc(s["consts"], 1)
            dve.wait_ge(s["consts"], 6)
            def stage(g):
                stage_tiles(nc, c, xs, g).then_inc(s["staged"], 1)
                dve.wait_ge(s["staged"], Count(g, 1)(1))
                nc.vector.tensor_tensor(c["stream"][:, bass.ds(g * T, T), :], xs[:, :, :],
                                        w("f_bo").unsqueeze(1).to_broadcast([P, T, P]), ALU.add)

            def keys(g):
                dve.wait_ge(s["k_ps"], Count(g, 1)(1))
                nc.vector.tensor_scalar(kT[:, :], ps[:, 7, :], turn_scale, kb[:, :], ALU.mult, ALU.add).then_inc(s["k_sb"], 1)

            def values(g):
                dve.wait_ge(s["v_ps"], Count(g, 1)(1))
                for b in range(2):
                    half = slice(b * S, (b + 1) * S)
                    last = nc.vector.scalar_tensor_tensor(
                        vS[half, :, :, b * DH:(b + 1) * DH], ps[half, 6, :].rearrange("p (t h d) -> p t h d", h=H, d=DH), 1.0 / M,
                        vb[half, :].rearrange("p (h d) -> p h d", d=DH).unsqueeze(1).to_broadcast([S, T, H, DH]), ALU.mult, ALU.add)
                last.then_inc(s["v_sb"], 1)

            def queries(g):
                dve.wait_ge(s["q_ps"], Count(g, 1)(1))
                nc.vector.tensor_scalar(qT[:, :], ps[:, 7, :], turn_scale, qb[:, :], ALU.mult, ALU.add).then_inc(s["q_sb"], 1)

            def reduce_(g, n, unit):
                dve.wait_ge(s["z_ps"], unit)
                z = ps[:, 2 * (n % 2):2 * (n % 2) + 2, :].rearrange("p a b -> p (a b)")
                nc.vector.tensor_scalar(whole[:, :], z, MAGIC, MAGIC, ALU.add, ALU.subtract).then_inc(s["rounded"], 1)
                dve.wait_ge(s["rounded"], unit)
                if n >= 2:
                    dve.wait_ge(s["feats"], Count(g, UPG)(n - 1))
                nc.vector.tensor_tensor(frac[:, n % 2, :], z, whole[:, :], ALU.subtract).then_inc(s["reduced"], 1)
                dve.wait_ge(s["reduced"], unit)
                nc.vector.tensor_scalar(wrap[:, n % 2, :].bitcast(I32), frac[:, n % 2, :].bitcast(I32), 0x7FFFFFFF, None,
                                        ALU.bitwise_and).then_inc(s["wrapped"], 1)

            def main(g, ahead):
                for n in range(4, UPG + (2 if ahead else 0)):
                    if n < UPG:
                        reduce_(g, n, Count(g, UPG)(n + 1))
                    else:
                        dve.wait_ge(s["feats"], Count(g, UPG)(n - 1))
                        reduce_(g + 1, n - UPG, Count(g + 1, UPG)(n - UPG + 1))
                    v = n - T * KU
                    if ahead and v == 0:
                        stage(g + 1)
                    if ahead and v == 5:
                        keys(g + 1)
                        values(g + 1)
                    if ahead and v == 7:
                        queries(g + 1)
                if ahead:
                    reduce_(g + 1, 2, Count(g + 1, UPG)(3))
                dve.wait_ge(s["yt_ps"], Count(g, 1)(1))
                residual_group(nc, c, norm, Chain(dve, s["steps"], g, 3), g, ps[:, 7, :].rearrange("p (t d) -> p t d", d=P),
                               c["stream"][:, bass.ds(g * T, T), :]).then_inc(s["out_read"], 1)
                if ahead:
                    reduce_(g + 1, 3, Count(g + 1, UPG)(4))

            stage(0)
            keys(0)
            values(0)
            queries(0)
            for n in range(4):
                reduce_(0, n, n + 1)
            with dve.Fori(0, G - 1) as g:
                main(g, True)
            main(G - 1, False)

        @block.gpsimd
        def _(pool):
            nc.gpsimd.tensor_tensor(projX[:, :, :], w("f_proj").unsqueeze(1).to_broadcast([P, H, M]),
                                    c["const"]("headmask").unsqueeze(2).to_broadcast([P, H, M]), ALU.mult).then_inc(s["consts"], 1)


def latents_phase(nc, ctx, c, name):
    sb = lambda n, shape, dt=F32: ctx.enter_context(nc.sbuf_tensor(f"{name}_{n}", shape, dt))
    s = {n: c["sem"](f"{name}_{n}") for n in (
        "mats_in mask_in ab_ps ab_sb stats2 root2 ctx_in prep staged scaled latT_ps XT_sb X_ps X_sb "
        "th_ps th_sb th16 rough top diag scores exped sums share px_ps px_sb recip y_ps yT_sb yt_ps steps out_read kept prep0 prep1 prep2 taken XT16").split()}
    w, ps = c["w"], c["psum"]
    norm = Norm(sb)
    lat, cx = sb("lat", [P, T, P]), sb("cx", [P, T, P])
    momc = c["ctx_moments"]
    rstd2, rstdc = sb("rstd2", [P, NT]), sb("rstdc", [P, NT])
    keep, drop, bias = sb("keep", [P, NT]), sb("drop", [P, NT]), sb("bias", [P, B])
    A, N = sb("A", [P, H, P]), sb("N", [P, H, P])
    ident, ident16 = c["const"]("ident"), c["ident16"]
    ones16, ones32 = sb("ones16", [P, P], BF16), sb("ones32", [P, P])
    with ExitStack() as early:
        load = lambda n, shape, dt=F32: early.enter_context(nc.sbuf_tensor(f"{name}_{n}", shape, dt))
        mats = load("mats", [P, 4, PAIRS, P])
        mask = load("mask", [P, NT + B], mybir.dt.uint8)
        with nc.Block() as block:
            @block.sync
            def _(sp):
                sp.dma_start(mats[:, :, :, :], c["l_mats"]).then_inc(s["mats_in"], 16)
                sp.dma_start(mask[:, :], c["mask"]).then_inc(s["mask_in"], 16)

            @block.tensor
            def _(pe):
                pe.wait_ge(s["mats_in"], 16)
                for h in range(H):
                    if h == 8:
                        pe.wait_ge(s["ab_sb"], 4)
                    par = h % 2
                    r = slice(par * S, par * S + S)
                    at = (h % 8 // 2) * P
                    nc.tensor.matmul(ps[:, par, at:at + P], mats[r, 0, h // 2, :], mats[r, 1, h // 2, :], start=True, stop=True)
                    last = nc.tensor.matmul(ps[:, 2 + par, at:at + P], mats[r, 2, h // 2, :], mats[r, 3, h // 2, :], start=True, stop=True)
                    if h % 8 == 7:
                        last.then_inc(s["ab_ps"], 1)

            @block.scalar
            def _(act):
                for q in range(2):
                    act.wait_ge(s["ab_ps"], q + 1)
                    for par in range(2):
                        heads = slice(8 * q + par, 8 * q + 8, 2)
                        nc.scalar.activation(A[:, heads, :], ps[:, par, :].rearrange("p (h d) -> p h d", d=P), ACT.Copy,
                                             scale=0.125).then_inc(s["ab_sb"], 1)
                        nc.scalar.copy(N[:, heads, :], ps[:, 2 + par, :].rearrange("p (h d) -> p h d", d=P)).then_inc(s["ab_sb"], 1)
                act.wait_ge(s["stats2"], 1)
                nc.scalar.activation(rstd2[:, :], rstd2[:, :], ACT.Sqrt)
                nc.scalar.activation(rstdc[:, :], rstdc[:, :], ACT.Sqrt).then_inc(s["root2"], 1)

            @block.vector
            def _(dve):
                nc.vector.memset(ones16[:, :], 1.0)
                nc.vector.memset(ones32[:, :], 1.0)
                dve.wait_ge(s["mask_in"], 16)
                nc.vector.tensor_scalar(keep[:, :], mask[:, 0:NT], 1.0, None, ALU.mult)
                nc.vector.tensor_scalar(drop[:, :], mask[:, 0:NT], -1.0, 1.0, ALU.mult, ALU.add)
                nc.vector.tensor_scalar(bias[:, :], mask[:, NT:NT + B], 1e30, 1e30, ALU.mult, ALU.subtract)
                nc.vector.tensor_tensor(rstd2[:, :], c["moments"][:, :, 1], c["rstd"][:, :], ALU.mult).then_inc(s["prep"], 1)
                dve.wait_ge(s["prep"], 1)
                nc.vector.tensor_tensor(rstd2[:, :], rstd2[:, :], c["rstd"][:, :], ALU.mult).then_inc(s["prep"], 1)
                dve.wait_ge(s["prep"], 2)
                nc.vector.tensor_scalar(rstd2[:, :], rstd2[:, :], LN_EPS, None, ALU.add)
                nc.vector.tensor_scalar(rstdc[:, :], momc[:, :, 1], LN_EPS, None, ALU.add).then_inc(s["stats2"], 1)
                dve.wait_ge(s["root2"], 1)
                nc.vector.reciprocal(rstd2[:, :], rstd2[:, :]).then_inc(s["prep"], 1)
                nc.vector.reciprocal(rstdc[:, :], rstdc[:, :])
                dve.wait_ge(s["prep"], 3)
                nc.vector.tensor_tensor(rstd2[:, :], rstd2[:, :], c["rstd"][:, :], ALU.mult)

    bias_now = sb("bias_now", [P, GB])
    craw, xs = sb("craw", [P, T, P]), sb("xs", [P, T, P])
    gx = sb("gx", [P, 2, T, P])
    XT, XT16 = sb("XT", [P, GB, 2, S]), sb("XT16", [P, GB, 2 * S], BF16)
    X = sb("X", [P, GB, P])
    th, th16 = sb("th", [P, GB, H, S]), sb("th16", [P, GB, H, S], BF16)
    top, diag = sb("top", [P, 4, PAIRS]), sb("diag", [P, 3, PAIRS, P], BF16)
    prob = sb("prob", [P, 4, 2, 512])
    recip = sb("recip", [P, 2, 512])
    share = sb("share", [P, 2, 2, 2, 512])
    px = sb("px", [P, H, GB, S])
    yT = sb("yT", [P, T * P])
    BP = GB // 2
    LAG = 3
    BETWEEN = {3: GB - 3, 8: GB - 2, 13: GB - 1}

    with nc.Block() as block:
        @block.sync
        def _(sp):
            sp.dma_start(craw[:, :, :], c["ctx"][:, 0:T, :]).then_inc(s["ctx_in"], 16)
            with sp.Fori(1, G) as i:
                sp.wait_ge(s["scaled"], i)
                sp.dma_start(craw[:, :, :], c["ctx"][:, bass.ds(i * T, T), :]).then_inc(s["ctx_in"], 16)

        @block.tensor
        def _(pe):
            def heads(g, gathered):
                one, head = Count(g, 1), Count(g, H)
                pe.wait_ge(s["staged"], one(1))
                for t in range(T):
                    nc.tensor.transpose(ps[:, 0, t * P:(t + 1) * P], lat[:, t, :], ident)
                for t in range(T):
                    last = nc.tensor.transpose(ps[:, 1, t * P:(t + 1) * P], cx[:, t, :], ident)
                last.then_inc(s["latT_ps"], 1)
                pe.wait_ge(s["XT_sb"], one(1))
                for h in range(H):
                    if h in BETWEEN and gathered is not None:
                        gather(gathered, BETWEEN[h])
                    if h >= 4:
                        pe.wait_ge(s["th_sb"], head(h - 3))
                    nc.tensor.matmul(ps[:, h % 4, :], A[:, h, :], XT[:, :, 1, :], start=True, stop=True).then_inc(s["th_ps"], 1)

            def keys_back(g):
                for b in range(GB):
                    last = nc.tensor.transpose(ps[:, 4 + b // 4, (b % 4) * P:(b % 4 + 1) * P], XT[:, b, :, :], ident)
                last.then_inc(s["X_ps"], 1)

            def rough(g, b):
                if b == 0:
                    pe.wait_ge(s["th16"], Count(g, H)(H))
                    pe.wait_ge(s["XT16"], Count(g, 1)(1))
                else:
                    pe.wait_ge(s["top"], Count(g, GB)(b))
                for j in range(PAIRS):
                    last = nc.tensor.matmul(ps[:, j // 4, (j % 4) * P:(j % 4 + 1) * P], th16[:, b, 2 * j:2 * j + 2, :],
                                            XT16[:, b, :], start=True, stop=True)
                last.then_inc(s["rough"], 1)

            def scores(g, b):
                if b >= 1:
                    pe.wait_ge(s["exped"], Count(g, GB)(b))
                for q in range(2):
                    nc.tensor.matmul(ps[:, 2 + q, :], XT[:, b, :, :], th[:, b, 8 * q:8 * q + 8, :], start=True, stop=False)

            def shift(g, b):
                pe.wait_ge(s["diag"], Count(g, GB)(b + 1))
                for q in range(2):
                    last = nc.tensor.matmul(ps[:, 2 + q, :], ones16[:, :], diag[:, b % 3, 4 * q:4 * q + 4, :], start=False, stop=True)
                last.then_inc(s["scores"], 1)

            def sums(g, p):
                pe.wait_ge(s["exped"], Count(g, GB)(2 * p + 2))
                if p >= 2:
                    pe.wait_ge(s["recip"], Count(g, BP)(p - 1))
                if p == 1:
                    pe.wait_ge(s["out_read"], Count(g, 1)(1))
                for b in range(2):
                    for q in range(2):
                        at = 32 * (2 * b + q)
                        last = nc.tensor.matmul(ps[at:at + 32, 6 + p % 2, :], ones32[:, 0:32], prob[:, (2 * p + b) % 4, q, :],
                                                start=True, stop=True)
                last.then_inc(s["sums"], 1)

            def gather(g, b):
                if b == 0:
                    pe.wait_ge(s["X_sb"], Count(g, 1)(1))
                else:
                    pe.wait_ge(s["px_sb"], Count(g, GB)(b))
                for q in range(2):
                    last = nc.tensor.matmul(ps[:, 4 + q, :], X[:, b, :], prob[:, b % 4, q, :], start=True, stop=True)
                last.then_inc(s["px_ps"], 1)

            def start(g):
                keys_back(g)
                rough(g, 0)
                scores(g, 0)
                rough(g, 1)

            def main(g):
                for b in range(GB):
                    if b >= 1:
                        scores(g, b)
                    shift(g, b)
                    if b + 2 < GB:
                        rough(g, b + 2)
                    if b >= LAG:
                        gather(g, b - LAG)
                    if b % 2 == 1:
                        sums(g, b // 2)

            def combine(g):
                pe.wait_ge(s["px_sb"], Count(g, GB)(GB))
                for h in range(H):
                    last = nc.tensor.matmul(ps[:, 6, :], N[:, h, :], px[:, h, :, :], start=(h == 0), stop=(h == H - 1))
                last.then_inc(s["y_ps"], 1)

            def finish(g):
                pe.wait_ge(s["yT_sb"], Count(g, 1)(1))
                for t in range(T):
                    last = nc.tensor.transpose(ps[:, 7, t * P:(t + 1) * P], yT[:, t * P:(t + 1) * P], ident)
                last.then_inc(s["yt_ps"], 1)

            heads(0, None)
            start(0)
            with pe.Fori(0, G - 1) as g:
                main(g)
                heads(g + 1, g)
                combine(g)
                start(g + 1)
                finish(g)
            main(G - 1)
            for b in range(GB - LAG, GB):
                gather(G - 1, b)
            combine(G - 1)
            finish(G - 1)

        @block.scalar
        def _(act):
            def heads(g):
                one, head = Count(g, 1), Count(g, H)
                act.wait_ge(s["latT_ps"], one(1))
                nc.scalar.copy(XT[:, :, 1, :], ps[:, 0, :].rearrange("p (b s) -> p b s", s=S))
                nc.scalar.copy(XT[:, :, 0, :], ps[:, 1, :].rearrange("p (b s) -> p b s", s=S)).then_inc(s["XT_sb"], 1)
                for h in range(H):
                    act.wait_ge(s["th_ps"], head(h + 1))
                    nc.scalar.copy(th[:, :, h, :], ps[:, h % 4, :].rearrange("p (b s) -> p b s", s=S)).then_inc(s["th_sb"], 1)
                    if h == 0:
                        act.wait_ge(s["XT_sb"], one(1))
                        nc.scalar.copy(XT16[:, :, :], XT[:, :, :, :].rearrange("p b a s -> p b (a s)")).then_inc(s["XT16"], 1)

            def main(g):
                batch = Count(g, GB)
                for b in range(GB):
                    act.wait_ge(s["scores"], batch(b + 1))
                    if b >= 4:
                        act.wait_ge(s["px_ps"], batch(b - 3))
                    nc.scalar.activation(prob[:, b % 4, :, :], ps[:, 2:4, :], ACT.Exp,
                                         bias=bias_now[:, b:b + 1]).then_inc(s["exped"], 1)

            def finish(g):
                act.wait_ge(s["y_ps"], Count(g, 1)(1))
                nc.scalar.copy(yT[:, :], ps[:, 6, :]).then_inc(s["yT_sb"], 1)

            def keys_back(g):
                act.wait_ge(s["X_ps"], Count(g, 1)(1))
                nc.scalar.copy(X[:, :, :], ps[:, 4:6, :].rearrange("p a (b d) -> p (a b) d", d=P)).then_inc(s["X_sb"], 1)

            heads(0)
            keys_back(0)
            with act.Fori(0, G - 1) as g:
                main(g)
                heads(g + 1)
                finish(g)
                keys_back(g + 1)
            main(G - 1)
            finish(G - 1)

        @block.vector
        def _(dve):
            def prepare(g, after):
                if after is not None:
                    dve.wait_ge(s["latT_ps"], after)
                    dve.wait_ge(s["kept"], Count(g - 1, 1)(1))
                dve.wait_ge(s["ctx_in"], 16 * g + 16)
                for t in range(T):
                    tile = g * T + t
                    nc.vector.tensor_scalar(lat[:, t, :], c["stream"][:, bass.ds(tile, 1), :], c["moments"][:, bass.ds(tile, 1), 0],
                                            rstd2[:, bass.ds(tile, 1)], ALU.subtract, ALU.mult)
                    nc.vector.tensor_scalar(xs[:, t, :], c["stream"][:, bass.ds(tile, 1), :], c["moments"][:, bass.ds(tile, 1), 0],
                                            c["rstd"][:, bass.ds(tile, 1)], ALU.subtract, ALU.mult)
                for t in range(T):
                    tile = g * T + t
                    last = nc.vector.tensor_scalar(cx[:, t, :], craw[:, t, :], momc[:, bass.ds(tile, 1), 0],
                                                   rstdc[:, bass.ds(tile, 1)], ALU.subtract, ALU.mult)
                last.then_inc(s["scaled"], 1)
                dve.wait_ge(s["scaled"], Count(g, 1)(1))
                nc.vector.tensor_scalar(c["stream"][:, bass.ds(g * T, T), :], xs[:, :, :], 1.0, None, ALU.mult).then_inc(s["kept"], 1)

            def heads(g, gathered, prepare_next):
                head = Count(g, H)
                for h in range(H):
                    if h in BETWEEN and gathered is not None:
                        divide(gathered, BETWEEN[h])
                    if h == 4 and prepare_next:
                        prepare(g + 1, Count(g, 1)(1))
                    dve.wait_ge(s["th_sb"], head(h + 1))
                    nc.vector.tensor_copy(th16[:, :, h, :], th[:, :, h, :]).then_inc(s["th16"], 1)

            def divide(g, b):
                batch = Count(g, GB)
                dve.wait_ge(s["px_ps"], batch(b + 1))
                dve.wait_ge(s["share"], Count(g, 2 * GB)(2 * b + 2))
                nc.vector.tensor_tensor(px[:, :, b, :], ps[:, 4:6, :].rearrange("p a (h s) -> p (a h) s", s=S),
                                        share[:, (b // 2) % 2, b % 2, :, :].rearrange("p a (h s) -> p (a h) s", s=S),
                                        ALU.mult).then_inc(s["px_sb"], 1)

            def row_tops(g, b):
                dve.wait_ge(s["rough"], Count(g, GB)(b + 1))
                nc.vector.tensor_reduce(top[:, b % 4, :], ps[:, 0:2, :].rearrange("p a (j n) -> p (a j) n", n=P), AX.X, ALU.max,
                                        negate=True).then_inc(s["top"], 1)

            def invert(g, p):
                dve.wait_ge(s["sums"], Count(g, BP)(p + 1))
                if p >= 2:
                    dve.wait_ge(s["share"], Count(g, 2 * GB)(4 * p - 4))
                nc.vector.reciprocal(recip[:, p % 2, :], ps[:, 6 + p % 2, :]).then_inc(s["recip"], 1)

            def start(g):
                row_tops(g, 0)
                row_tops(g, 1)

            def main(g):
                for b in range(GB):
                    if b + 2 < GB:
                        row_tops(g, b + 2)
                    if b >= LAG:
                        divide(g, b - LAG)
                    if b % 2 == 1:
                        invert(g, b // 2)

            def finish(g):
                step = Chain(dve, s["steps"], g, 3)
                dve.wait_ge(s["yt_ps"], Count(g, 1)(1))
                residual_group(nc, c, norm, step, g, ps[:, 7, :].rearrange("p (t d) -> p t d", d=P),
                               c["stream"][:, bass.ds(g * T, T), :]).then_inc(s["out_read"], 1)

            def turn(g, prepare_next):
                main(g)
                dve.wait_ge(s["exped"], Count(g, GB)(GB))
                nc.vector.tensor_scalar(bias_now[:, :], bias[:, bass.ds((g + 1) * GB, GB)], 1.0, None, ALU.mult)
                heads(g + 1, g, prepare_next)
                start(g + 1)
                finish(g)

            dve.sem_inc(s["out_read"], 1)
            prepare(0, None)
            nc.vector.tensor_scalar(bias_now[:, :], bias[:, 0:GB], 1.0, None, ALU.mult)
            heads(0, None, True)
            start(0)
            with dve.Fori(0, G - 2) as g:
                turn(g, True)
            turn(G - 2, False)
            main(G - 1)
            for b in range(GB - LAG, GB):
                divide(G - 1, b)
            finish(G - 1)

        @block.gpsimd
        def _(pool):
            wide = lambda a: a.unsqueeze(1).to_broadcast([P, T, P])

            group = lambda a, g: a[:, bass.ds(g * T, T)].unsqueeze(2).to_broadcast([P, T, P])

            def prepare(g):
                pool.wait_ge(s["scaled"], Count(g, 1)(1))
                nc.gpsimd.tensor_tensor(gx[:, 0, :, :], lat[:, :, :], wide(w("l_g2")), ALU.mult)
                nc.gpsimd.tensor_tensor(gx[:, 1, :, :], cx[:, :, :], wide(w("l_g1")), ALU.mult).then_inc(s["prep0"], 1)
                pool.wait_ge(s["prep0"], Count(g, 1)(1))
                nc.gpsimd.tensor_tensor(lat[:, :, :], gx[:, 0, :, :], wide(w("l_b2")), ALU.add)
                nc.gpsimd.tensor_tensor(cx[:, :, :], gx[:, 1, :, :], wide(w("l_b1")), ALU.add).then_inc(s["prep1"], 1)
                pool.wait_ge(s["prep1"], Count(g, 1)(1))
                nc.gpsimd.tensor_tensor(gx[:, 0, :, :], cx[:, :, :], group(keep, g), ALU.mult)
                nc.gpsimd.tensor_tensor(gx[:, 1, :, :], lat[:, :, :], group(drop, g), ALU.mult).then_inc(s["prep2"], 1)
                pool.wait_ge(s["prep2"], Count(g, 1)(1))
                nc.gpsimd.tensor_tensor(cx[:, :, :], gx[:, 0, :, :], gx[:, 1, :, :], ALU.add).then_inc(s["staged"], 1)

            def shift(g, b):
                pool.wait_ge(s["top"], Count(g, GB)(b + 1))
                if b >= 3:
                    pool.wait_ge(s["scores"], Count(g, GB)(b - 2))
                nc.gpsimd.tensor_tensor(diag[:, b % 3, :, :], ident16[:, :].unsqueeze(1).to_broadcast([P, PAIRS, P]),
                                        top[:, b % 4, :].unsqueeze(2).to_broadcast([P, PAIRS, P]), ALU.mult).then_inc(s["diag"], 1)

            def spread(g, p):
                pool.wait_ge(s["recip"], Count(g, BP)(p + 1))
                if p >= 2:
                    pool.wait_ge(s["px_sb"], Count(g, GB)(2 * p - 2))
                pool.sem_inc(s["taken"], 1)
                for n in range(4):
                    nc.gpsimd.partition_broadcast(share[:, p % 2, n // 2, n % 2, :], recip[32 * n:32 * n + 1, p % 2, :], P
                                                  ).then_inc(s["share"], 1)
                    pool.wait_ge(s["share"], Count(g, 2 * GB)(4 * p + n + 1))
                    pool.sem_inc(s["taken"], 1)

            def start(g):
                shift(g, 0)
                shift(g, 1)

            def main(g):
                for b in range(GB):
                    if b + 2 < GB:
                        shift(g, b + 2)
                    if b % 2 == 1:
                        spread(g, b // 2)

            prepare(0)
            prepare(1)
            start(0)
            with pool.Fori(0, G - 2) as g:
                main(g)
                prepare(g + 2)
                start(g + 1)
            main(G - 2)
            start(G - 1)
            main(G - 1)


def bitlinear_phase(nc, ctx, c, name, out):
    sb = lambda n, shape, dt=F32: ctx.enter_context(nc.sbuf_tensor(f"{name}_{n}", shape, dt))
    s = {n: c["sem"](f"{name}_{n}") for n in (
        "mags mag_ps quant square root1 rms1 staged x_ready deq_ready deq2_ready x_ps x_sb h_ps r_sb h_sb g_sb ss2 root2 q_ready q_ps "
        "q_sb y_ps out_sb steps x_steps h_steps wsteps var3 root3 rms3 normed stored taken").split()}
    w, ps = c["w"], c["psum"]
    HID = 512
    HC = HID // P
    MAGIC = 1.5 * 2.0 ** 23
    EPS_NORM, EPS_Q = 1e-8, 1e-5
    xs, norm = sb("xs", [P, T, P]), Norm(sb)
    wq, wtmp = sb("wq", [P, 2, HID], BF16), sb("wtmp", [P, 2, HID])
    mags, wmean, wscale, ones = sb("mags", [P, 2]), sb("wmean", [P, 2]), sb("wscale", [P, 2]), sb("ones", [P, P])
    sq, rms1, ss2 = sb("sq", [P, T, HID]), sb("rms1", [P, NT]), sb("ss2", [P, T])
    xn, amax, xscale, deq = sb("xn", [P, T, P]), sb("amax", [P, T]), sb("xscale", [P, T]), sb("deq", [P, T])
    y, std, normed = sb("y", [P, T, P]), sb("std", [P, T]), sb("normed", [P, NT, P])
    out = out.rearrange("(n k) s d -> (k s) n d", k=2)
    xi, xiT = sb("xi", [P, T, P], BF16), sb("xiT", [P, T * P], BF16)
    r, hh, hn = sb("r", [P, T, HID]), sb("hh", [P, T, HID]), sb("hn", [P, T, HID])
    amax2, hscale, deq2 = sb("amax2", [P, T]), sb("hscale", [P, T]), sb("deq2", [P, T])
    hi, hiT = sb("hi", [P, T, HID], BF16), sb("hiT", [P, 2, HID], BF16)
    eps = sb("eps", [P, 1])
    raw = [w("b_w1"), w("b_w2")]
    EARLY = 4

    def quantise(link, values, out, scales, biggest, inverse_rms):
        link(nc.vector.tensor_reduce(biggest[:, :], values[:, :, :], AX.X, ALU.max, apply_absolute_value=True))
        link(nc.vector.tensor_tensor(biggest[:, :], biggest[:, :], inverse_rms, ALU.mult))
        link(nc.vector.tensor_scalar(biggest[:, :], biggest[:, :], EPS_Q, None, ALU.max))
        link(nc.vector.reciprocal(scales[:, :], biggest[:, :]))
        link(nc.vector.tensor_scalar(scales[:, :], scales[:, :], 127.0, None, ALU.mult))
        link(nc.vector.tensor_tensor(scales[:, :], scales[:, :], inverse_rms, ALU.mult))
        for t in range(T):
            last = nc.vector.tensor_scalar(values[:, t, :], values[:, t, :], scales[:, t:t + 1], MAGIC, ALU.mult, ALU.add)
        link(last)
        return nc.vector.tensor_scalar(out[:, :, :], values[:, :, :], MAGIC, 127.0, ALU.subtract, ALU.min)

    with nc.Block() as block:
        @block.tensor
        def _(pe):
            def hidden(g):
                pe.wait_ge(s["x_ready"], Count(g, 1)(1))
                for t in range(T):
                    last = nc.tensor.matmul(ps[:, 0, t * P:(t + 1) * P], xi[:, t, :], c["ident16"][:, :], start=True, stop=True)
                last.then_inc(s["x_ps"], 1)
                pe.wait_ge(s["x_sb"], Count(g, 1)(1))

            def hidden_tiles(g, first):
                for t in range(T):
                    if not first:
                        pe.wait_ge(s["r_sb"], Count(g - 1, T)(t + 1))
                    nc.tensor.matmul(ps[:, 1 + t, :], xiT[:, t * P:(t + 1) * P], wq[:, 0, :], start=True, stop=True
                                     ).then_inc(s["h_ps"], 1)

            def down(g, t):
                pe.wait_ge(s["q_sb"], Count(g, T)(t + 1))
                for n in range(HC):
                    last = nc.tensor.matmul(ps[:, 7, t * P:(t + 1) * P], hiT[:, t % 2, n * P:(n + 1) * P], wq[:, 1, n * P:(n + 1) * P],
                                            start=(n == 0), stop=(n == HC - 1))
                if t == T - 1:
                    last.then_inc(s["y_ps"], 1)

            def output(g):
                pe.wait_ge(s["q_ready"], Count(g, 1)(1))
                for t in range(T):
                    if t >= 2:
                        pe.wait_ge(s["q_sb"], Count(g, T)(t - 1))
                    for n in range(HC):
                        last = nc.tensor.matmul(ps[:, 5 + t % 2, n * P:(n + 1) * P], hi[:, t, n * P:(n + 1) * P], c["ident16"][:, :],
                                                start=True, stop=True)
                    last.then_inc(s["q_ps"], 1)
                    if t >= 1:
                        down(g, t - 1)
                down(g, T - 1)

            pe.wait_ge(s["mags"], 1)
            nc.tensor.matmul(ps[:, 0, 0:2], ones[:, :], mags[:, :], start=True, stop=True).then_inc(s["mag_ps"], 1)
            pe.wait_ge(s["quant"], 1)
            hidden(0)
            hidden_tiles(0, True)
            with pe.Fori(0, G - 1) as g:
                hidden(g + 1)
                hidden_tiles(g + 1, False)
                output(g)
            output(G - 1)

        @block.scalar
        def _(act):
            def tokens_turned(g):
                act.wait_ge(s["x_ps"], Count(g, 1)(1))
                nc.scalar.copy(xiT[:, :], ps[:, 0, :]).then_inc(s["x_sb"], 1)

            def activate(g):
                act.wait_ge(s["deq_ready"], Count(g, 1)(1))
                for t in range(T):
                    act.wait_ge(s["h_ps"], Count(g, T)(t + 1))
                    nc.scalar.activation(r[:, t, :], ps[:, 1 + t, :], ACT.Relu, scale=deq[:, t:t + 1]).then_inc(s["r_sb"], 1)
                for t in range(T):
                    act.wait_ge(s["r_sb"], Count(g, T)(t + 1))
                    nc.scalar.activation(r[:, t, :], r[:, t, :], ACT.Square).then_inc(s["h_sb"], 1)

            def measure(g):
                for t in range(T):
                    act.wait_ge(s["g_sb"], Count(g, T)(t + 1))
                    last = nc.scalar.activation(sq[:, t, :], hh[:, t, :], ACT.Square, accum_out=ss2[:, t:t + 1])
                last.then_inc(s["ss2"], 1)
                act.wait_ge(s["ss2"], Count(g, 1)(1))
                nc.scalar.activation(ss2[:, :], ss2[:, :], ACT.Sqrt, bias=eps[:, :], scale=1.0 / HID).then_inc(s["root2"], 1)

            def hidden_turned(g):
                for t in range(T):
                    act.wait_ge(s["q_ps"], Count(g, T)(t + 1))
                    nc.scalar.copy(hiT[:, t % 2, :], ps[:, 5 + t % 2, :]).then_inc(s["q_sb"], 1)

            def root(g):
                act.wait_ge(s["var3"], Count(g, 1)(1))
                nc.scalar.activation(std[:, :], std[:, :], ACT.Sqrt).then_inc(s["root3"], 1)

            act.wait_ge(s["square"], 3)
            nc.scalar.activation(rms1[:, :], rms1[:, :], ACT.Sqrt).then_inc(s["root1"], 1)
            tokens_turned(0)
            activate(0)
            tokens_turned(1)
            measure(0)
            hidden_turned(0)
            with act.Fori(1, G - 1) as g:
                activate(g)
                tokens_turned(g + 1)
                measure(g)
                root(g - 1)
                hidden_turned(g)
            activate(G - 1)
            measure(G - 1)
            root(G - 2)
            hidden_turned(G - 1)
            root(G - 1)

        @block.sync
        def _(sp):
            with sp.Fori(0, G) as g:
                sp.wait_ge(s["normed"], g + 1)
                sp.dma_start(out[:, bass.ds(g * T, T), :], normed[:, bass.ds(g * T, T), :]).then_inc(s["stored"], 16)
            sp.wait_ge(s["stored"], 16 * G)

        @block.vector
        def _(dve):
            early = Chain(dve, s["wsteps"], 0, EARLY)
            nc.vector.memset(ones[:, :], 1.0)
            nc.vector.memset(eps[:, :], EPS_NORM)
            nc.vector.tensor_tensor(rms1[:, :], c["moments"][:, :, 1], c["rstd"][:, :], ALU.mult).then_inc(s["square"], 1)
            dve.wait_ge(s["square"], 1)
            nc.vector.tensor_tensor(rms1[:, :], rms1[:, :], c["rstd"][:, :], ALU.mult).then_inc(s["square"], 1)
            dve.wait_ge(s["square"], 2)
            nc.vector.tensor_scalar(rms1[:, :], rms1[:, :], EPS_NORM, None, ALU.add).then_inc(s["square"], 1)
            for n in range(2):
                last = nc.vector.tensor_reduce(mags[:, n:n + 1], raw[n], AX.X, ALU.add, apply_absolute_value=True)
            last.then_inc(s["mags"], 1)
            dve.wait_ge(s["mag_ps"], 1)
            early(nc.vector.tensor_scalar(wmean[:, :], ps[:, 0, 0:2], 1.0 / (P * HID), EPS_Q, ALU.mult, ALU.max))
            early(nc.vector.reciprocal(wscale[:, :], wmean[:, :]))
            for n in range(2):
                last = nc.vector.tensor_scalar(wtmp[:, n, :], raw[n], wscale[:, n:n + 1], None, ALU.mult)
            early(last)
            early(nc.vector.tensor_scalar(wtmp[:, :, :], wtmp[:, :, :], MAGIC, MAGIC, ALU.add, ALU.subtract))
            nc.vector.tensor_scalar(wq[:, :, :], wtmp[:, :, :], -1.0, 1.0, ALU.max, ALU.min).then_inc(s["quant"], 1)
            dve.wait_ge(s["root1"], 1)
            nc.vector.reciprocal(rms1[:, :], rms1[:, :]).then_inc(s["rms1"], 1)
            dve.wait_ge(s["rms1"], 1)
            dve.wait_ge(s["quant"], 1)

            def tokens(g, first):
                step = Chain(dve, s["x_steps"], g, 8)
                stage_tiles(nc, c, xs, g).then_inc(s["staged"], 1)
                dve.wait_ge(s["staged"], Count(g, 1)(1))
                nc.vector.tensor_scalar(c["stream"][:, bass.ds(g * T, T), :], xs[:, :, :], 1.0, None, ALU.mult)
                step(nc.vector.tensor_tensor(xn[:, :, :], xs[:, :, :], w("b_n1").unsqueeze(1).to_broadcast([P, T, P]), ALU.mult))
                if not first:
                    dve.wait_ge(s["x_ps"], Count(g - 1, 1)(1))
                quantise(step, xn, xi, xscale, amax, rms1[:, bass.ds(g * T, T)]).then_inc(s["x_ready"], 1)

            def undo(g):
                nc.vector.tensor_scalar(deq[:, :], amax[:, :], 1.0 / 127.0, wmean[:, 0:1], ALU.mult, ALU.mult).then_inc(s["deq_ready"], 1)

            def hidden(g):
                step = Chain(dve, s["h_steps"], g, 9)
                for t in range(T):
                    dve.wait_ge(s["h_sb"], Count(g, T)(t + 1))
                    nc.vector.tensor_scalar(hh[:, t, :], r[:, t, :], w("b_as"), w("b_ab"), ALU.mult, ALU.add).then_inc(s["g_sb"], 1)
                dve.wait_ge(s["g_sb"], Count(g, T)(T))
                step(nc.vector.tensor_tensor(hn[:, :, :], hh[:, :, :], w("b_n2").unsqueeze(1).to_broadcast([P, T, HID]), ALU.mult))
                dve.wait_ge(s["root2"], Count(g, 1)(1))
                step(nc.vector.reciprocal(ss2[:, :], ss2[:, :]))
                quantise(step, hn, hi, hscale, amax2, ss2[:, :]).then_inc(s["q_ready"], 1)
                nc.vector.tensor_scalar(deq2[:, :], amax2[:, :], 1.0 / 127.0, wmean[:, 1:2], ALU.mult, ALU.mult).then_inc(s["deq2_ready"], 1)

            def finish(g):
                dve.wait_ge(s["y_ps"], Count(g, 1)(1))
                dve.wait_ge(s["deq2_ready"], Count(g, 1)(1))
                for t in range(T):
                    last = nc.vector.tensor_scalar(y[:, t, :], ps[:, 7, t * P:(t + 1) * P], deq2[:, t:t + 1], None, ALU.mult)
                last.then_inc(s["out_sb"], 1)
                dve.wait_ge(s["out_sb"], Count(g, 1)(1))
                step = Chain(dve, s["steps"], g, 3)
                step(nc.vector.tensor_tensor(norm.sums[:, :, :], y[:, :, :], c["stream"][:, bass.ds(g * T, T), :], ALU.add))
                for t in range(T):
                    last = nc.vector.bn_stats(norm.stats[:, t, :], norm.sums[:, t, :])
                step(last)
                dve.sem_inc(s["taken"], 1)
                for t in range(T):
                    last = nc.vector.bn_aggr(norm.moments[:, t, :], norm.stats[:, t, :])
                step(last)
                nc.vector.tensor_scalar(std[:, :], norm.moments[:, :, 1], LN_EPS, None, ALU.add).then_inc(s["var3"], 1)

            def normalise(g):
                dve.wait_ge(s["root3"], Count(g, 1)(1))
                nc.vector.reciprocal(std[:, :], std[:, :]).then_inc(s["rms3"], 1)
                dve.wait_ge(s["rms3"], Count(g, 1)(1))
                for t in range(T):
                    last = nc.vector.tensor_scalar(normed[:, bass.ds(g * T + t, 1), :], norm.sums[:, t, :], norm.moments[:, t, 0:1],
                                                   std[:, t:t + 1], ALU.subtract, ALU.mult)
                last.then_inc(s["normed"], 1)

            tokens(0, True)
            undo(0)
            tokens(1, False)
            hidden(0)
            undo(1)
            with dve.Fori(1, G - 1) as g:
                tokens(g + 1, False)
                finish(g - 1)
                hidden(g)
                undo(g + 1)
                normalise(g - 1)
            finish(G - 2)
            hidden(G - 1)
            normalise(G - 2)
            finish(G - 1)
            normalise(G - 1)


def norm_phase(nc, ctx, c, name, loads):
    var_ready = c["sem"](f"{name}_var_ready")
    root_ready = c["sem"](f"{name}_root_ready")
    rstd = c["rstd"]
    with nc.Block() as block:
        if loads is not None:
            @block.sync
            def _(sp):
                sp.wait_ge(loads, 32)

        @block.vector
        def _(dve):
            nc.vector.tensor_scalar(rstd[:, :], c["moments"][:, :, 1], LN_EPS, None, ALU.add).then_inc(var_ready, 1)
            dve.wait_ge(root_ready, 1)
            nc.vector.reciprocal(rstd[:, :], rstd[:, :])

        @block.scalar
        def _(act):
            act.wait_ge(var_ready, 1)
            nc.scalar.activation(rstd[:, :], rstd[:, :], ACT.Sqrt).then_inc(root_ready, 1)


def build(nc, ins, out):
    where_w, n_w = columns(WEIGHTS)
    n_early = where_w["l_g1"][0]
    n_first = where_w["c_wq"][0]
    where_c, n_c = columns(CONST)
    with ExitStack() as ctx:
        sb = lambda n, shape, dt=F32: ctx.enter_context(nc.sbuf_tensor(n, shape, dt))
        late, const = sb("late_weights", [P, n_w - n_early]), sb("const", [P, n_c])

        def weight(n):
            lo, hi = where_w[n]
            return early[:, lo:hi] if hi <= n_early else late[:, lo - n_early:hi - n_early]

        taken = []

        def semaphore(n):
            taken.append(nc.alloc_semaphore(name=n))
            return taken[-1]

        def phase_end():
            nc.clear_and_free_semaphores(taken)
            nc.all_engine_barrier()
            taken.clear()

        c = {
            "sem": semaphore,
            "w": weight, "const": lambda n: const[:, slice(*where_c[n])],
            "stream": sb("stream", [P, NT, P]), "moments": sb("moments", [P, NT, 2]), "rstd": sb("rstd", [P, NT]),
            "ctx_moments": sb("ctx_moments", [P, NT, 2]),
            "bq_scaled": sb("bq_scaled", [P, 1]), "ident16": sb("ident16", [P, P], BF16),
            "psum": ctx.enter_context(nc.psum_tensor("psum", [P, 8, 512], F32)),
            "l_mats": ins["l_mats"], "mask": ins["mask"],
            "ctx": ins["ctx"].rearrange("(n k) s d -> (k s) n d", k=2),
        }
        loaded, loaded_rest = ctx.enter_context(nc.semaphore("loaded")), ctx.enter_context(nc.semaphore("loaded_rest"))
        early_room = ExitStack()
        early = early_room.enter_context(nc.sbuf_tensor("early_weights", [P, n_early], F32))
        c["relbias"] = early_room.enter_context(nc.sbuf_tensor("relbias", [P, H, S], F32))
        with nc.Block() as block:
            @block.sync
            def _(sp):
                sp.dma_start(early[:, 0:n_first], ins["weights"][:, 0:n_first]).then_inc(loaded, 16)
                sp.dma_start(c["stream"][:, :, :], ins["x"].rearrange("(n k) s d -> (k s) n d", k=2)).then_inc(loaded, 16)
                sp.dma_start(early[:, n_first:n_early], ins["weights"][:, n_first:n_early]).then_inc(loaded_rest, 16)
                sp.dma_start(late[:, :], ins["weights"][:, n_early:n_w]).then_inc(loaded_rest, 16)

            @block.scalar
            def _(act):
                act.dma_start(const[:, :], ins["const"]).then_inc(loaded, 16)
                act.dma_start(c["relbias"][:, :, :], ins["relbias"]).then_inc(loaded, 16)
                act.wait_ge(loaded, 64)
                nc.scalar.copy(c["ident16"][:, :], c["const"]("ident"))
                nc.scalar.mul(c["bq_scaled"][:, :], c["w"]("a_bq"), float(DH) ** -0.5)

            @block.vector
            def _(dve):
                nc.vector.memset(c["moments"][:, :, 0], 0.0)
                nc.vector.memset(c["moments"][:, :, 1], 1.0)
                nc.vector.memset(c["rstd"][:, :], 1.0)

        phases = [lambda x: attention_phase(nc, x, c, "a", False), lambda x: attention_phase(nc, x, c, "c", True),
                  lambda x: experts_phase(nc, x, c, "e"), lambda x: fourier_phase(nc, x, c, "f"),
                  lambda x: latents_phase(nc, x, c, "l"), lambda x: bitlinear_phase(nc, x, c, "b", out)]
        for n, phase in enumerate(phases):
            if n == 4:
                early_room.close()
            with ExitStack() as own:
                phase(own)
                if n < len(phases) - 1:
                    norm_phase(nc, own, c, f"n{n}", loaded_rest if n == 0 else None)
                    phase_end()


def laid_out(inp):
    f = {k: np.asarray(v) for k, v in inp.items()}
    col = lambda v: np.reshape(v, (-1, 1))
    rows = lambda v: np.broadcast_to(np.reshape(v, (1, -1)), (P, np.size(v)))
    turned = lambda wt: wt.reshape(H, 2, DH // 2, P)[:, ::-1].reshape(P, P).T
    w = {
        "a_wq": f["L0_attn_Wq"].T, "a_wk": f["L0_attn_Wk"].T, "a_wv": f["L0_attn_Wv"].T, "a_wo": f["L0_attn_Wo"].T,
        "a_bq": col(f["L0_attn_bq"]), "a_bk": col(f["L0_attn_bk"]), "a_bv": rows(f["L0_attn_bv"]), "a_bo": rows(f["L0_attn_bo"]),
        "c_wq": f["L0_xattn_Wq"].T, "c_wqr": turned(f["L0_xattn_Wq"]), "c_wk": f["L0_xattn_Wk"].T,
        "c_wkr": turned(f["L0_xattn_Wk"]), "c_wv": f["L0_xattn_Wv"].T, "c_wo": f["L0_xattn_Wo"].T,
    }
    w["e_wr"] = f["L0_ffn_Wr"]
    w["e_w1"] = np.concatenate([np.moveaxis(f["L0_ffn_W1"], 0, 1).reshape(P, 512), f["L0_ffn_Ws1"]], 1)
    w2 = np.concatenate([f["L0_ffn_W2"].reshape(512, P), f["L0_ffn_Ws2"], np.zeros((64, P), np.float32)])
    w["e_w2"] = np.moveaxis(w2.reshape(5, P, P), 0, 1).reshape(P, 640)
    w["f_wq"], w["f_wk"], w["f_wv"] = f["L1_attn_Wq"].T, f["L1_attn_Wk"].T, f["L1_attn_Wv"].T
    w["f_bq"], w["f_bk"], w["f_bv"] = col(f["L1_attn_bq"]), col(f["L1_attn_bk"]), rows(f["L1_attn_bv"])
    w["f_proj"] = np.tile(f["L1_attn_proj_mat"], (H, 1))
    wo = np.zeros((2, 4, 4, 4, DH, P), np.float32)
    for par in range(2):
        wo[par, :, :, par] = f["L1_attn_Wo"].T.reshape(4, 4, DH, P)
    w["f_wo"] = np.moveaxis(wo.reshape(8, P, P), 0, 1).reshape(P, 1024)
    w["f_bo"] = rows(f["L1_attn_bo"])
    for n in ("g1", "b1", "g2", "b2"):
        w[f"l_{n}"] = rows(f[f"L1_xattn_{n}"])
    w["b_w1"] = f["L1_ffn_w1"].T
    w["b_w2"] = np.moveaxis(f["L1_ffn_w2"].T.reshape(4, P, P), 0, 1).reshape(P, 512)
    w["b_n1"], w["b_n2"] = rows(f["L1_ffn_norm1_w"]), rows(f["L1_ffn_norm2_w"])
    w["b_as"], w["b_ab"] = rows(f["L1_ffn_act_scale"]), rows(f["L1_ffn_act_bias"])
    assert list(w) == list(WEIGHTS)
    by_pair = lambda a: np.moveaxis(a.reshape(PAIRS, P, P), 0, 1)
    kv = f["L1_xattn_Wkv"].T
    mats = np.stack([by_pair(f["L1_xattn_Wq"].T), by_pair(kv[:1024]), by_pair(kv[1024:]), by_pair(f["L1_xattn_Wout"])], 1)
    m = f["mask_BxS2_bk0"]
    mask = np.concatenate([m.reshape(NT, P).T, np.concatenate([m.T, np.ones((S, B), bool)])], 1)
    d = np.arange(P) % DH
    angle = np.outer(1.0 / 10000.0 ** (2 * (d % (DH // 2)) / DH), np.arange(S))
    t = {
        "ident": np.eye(P), "headmask": np.arange(P)[:, None] // DH == np.arange(H), "cos": np.cos(angle),
        "sin": np.where(d[:, None] < DH // 2, -np.sin(angle), np.sin(angle)),
    }
    q, kk = np.arange(P)[:, None] % S, np.arange(S)[None, :]
    return {
        "x": f["x"], "ctx": f["ctx_1024"],
        "weights": np.ascontiguousarray(np.concatenate([w[n] for n in WEIGHTS], 1)),
        "l_mats": np.ascontiguousarray(mats), "mask": np.ascontiguousarray(mask),
        "const": np.concatenate([np.asarray(t[n], np.float32) for n in CONST], 1),
        "relbias": np.ascontiguousarray(np.moveaxis(f["L0_attn_rel_bias"][:, np.clip(q - kk, -128, 128) + 128], 0, 1)),
    }


def kernel(**inputs):
    import concourse.bacc as bacc
    from concourse.bass_utils import run_bass_kernel_spmd

    nc = bacc.Bacc("TRN2", target_bir_lowering=False, num_devices=1)
    arrays = laid_out(inputs)
    ins = {n: nc.dram_tensor(f"in_{n}", a.shape, mybir.dt.from_np(a.dtype), kind="ExternalInput").ap() for n, a in arrays.items()}
    out = nc.dram_tensor("out", (B, S, P), F32, kind="ExternalOutput").ap()
    build(nc, ins, out)
    return run_bass_kernel_spmd(nc, [{f"in_{n}": a for n, a in arrays.items()}], core_ids=[0]).results[0]["out"]
```
